# Optimizing a Trainium2 kernel written in Bass

```python
import numpy as np
import jax
import jax.numpy as jnp

def _softmax(x, axis=-1):
    return jax.nn.softmax(x, axis=axis)

def _gelu(x):
    return jax.nn.gelu(x, approximate=True)

def _silu(x):
    return jax.nn.silu(x)

def _sigmoid(x):
    return jax.nn.sigmoid(x)

def _layernorm(x, axis=-1, eps=1e-05):
    m = jnp.mean(x, axis=axis, keepdims=True)
    v = jnp.var(x, axis=axis, keepdims=True)
    return (x - m) / jnp.sqrt(v + eps)

def _scatter_add(tgt, idx, src, axis=0):
    return tgt.at[idx].add(src)

def _segment_sum(src, seg, n):
    return jax.ops.segment_sum(src, seg, n)
kernel_name = 'mk_flamingo_gated_d2_seqx_r8_82f785'

def setup_inputs(seed: int=0):
    np.random.seed(seed)
    _w = jnp.asarray

    def _rec_inputs():
        import jax
        import jax.numpy as jnp
        _rk = jax.random.key(seed)
        x = -0.000929 + 1 * jax.random.normal(jax.random.fold_in(_rk, 1), (32, 64, 256), jnp.float32)
        _lenS = 64 - jax.random.randint(jax.random.fold_in(_rk, 7), (32,), 0, max(1, 64 // 4) + 1, jnp.int32)
        _lenS2 = 64 - jax.random.randint(jax.random.fold_in(_rk, 8), (32,), 0, max(1, 64 // 4) + 1, jnp.int32)
        _ctx_2048P = jax.random.normal(jax.random.fold_in(_rk, 11), (32, 16, 256), jnp.float32)
        _ctx_2048c = jax.random.dirichlet(jax.random.fold_in(_rk, 511), 0.3 * jnp.ones((16,), jnp.float32), (32, 64))
        _ctx_2048t = jnp.einsum('bsk,bkd->bsd', _ctx_2048c, _ctx_2048P)
        _ctx_2048t = _ctx_2048t * jax.lax.rsqrt(jnp.mean(jnp.square(_ctx_2048t)) + 1e-12) * 0.953939
        ctx_2048 = 2.81802e-05 + 1.00001 * (_ctx_2048t + 0.3 * jax.random.normal(jax.random.fold_in(_rk, 611), (32, 64, 256), jnp.float32))
        itok_BxS_0_1023 = jax.random.randint(jax.random.fold_in(_rk, 12), (32, 64), 0, 128, jnp.int32)
        _g = jax.random.normal(jax.random.fold_in(_rk, 9001), (2, 2), jnp.float32)
        _g = jnp.sign(_g) * jnp.maximum(jnp.abs(_g), 1.0) + (_g == 0) * 1.0
        g_xattn = _g[0]
        g_ffn = _g[1]
        return (x, ctx_2048, itok_BxS_0_1023, g_xattn, g_ffn)
    x, ctx_2048, itok_BxS_0_1023, g_xattn, g_ffn = _rec_inputs()

    def _L0_xattn_setup():
        import jax, jax.numpy as jnp
        import numpy as np
        from jax import lax
        LN_EPS = 1e-05
        key = jax.random.key(seed)
        ks = jax.random.split(key, 8)
        B, S, T, D = (4, 128, 256, 256)
        scale = 0.02
        return {'Z': jax.random.normal(ks[0], (B, S, D), dtype=jnp.float32), 'kv': jax.random.normal(ks[1], (B, T, D), dtype=jnp.float32), 'decay': jnp.float32(0.9), 'W_in': jax.random.normal(ks[2], (D, D), dtype=jnp.float32) * scale, 'b_in': jnp.zeros((D,), dtype=jnp.float32), 'W_out': jax.random.normal(ks[3], (D, D), dtype=jnp.float32) * scale, 'b_out': jnp.zeros((D,), dtype=jnp.float32), 'gamma': jnp.ones((D,), dtype=jnp.float32), 'beta': jnp.zeros((D,), dtype=jnp.float32)}
    _L0_xattn_all = _L0_xattn_setup()
    _L0_xattn_in = {k: v for k, v in _L0_xattn_all.items() if k in ('decay', 'W_in', 'b_in', 'W_out', 'b_out', 'gamma', 'beta')}
    del _L0_xattn_all

    def _L0_ffn_setup():
        import jax, jax.numpy as jnp
        import numpy as np
        DIM = 256
        INTER = 176
        E = 16
        TOPK = 4
        G = 4
        TOPK_G = 2
        N_SHARED = 2
        SHARED_INTER = N_SHARED * INTER
        ROUTE_SCALE = 1.0

        def _moe_forward(x, Wg, W1, W3, W2, Ws1, Ws3, Ws2):
            B, S, D = x.shape
            xt = x.reshape(-1, D)
            T = xt.shape[0]
            scores = jax.nn.softmax(xt @ Wg.T, axis=-1)
            sg = scores.reshape(T, G, E // G)
            group_scores = sg.max(axis=-1)
            gidx = jax.lax.top_k(group_scores, TOPK_G)[1]
            gmask = jax.nn.one_hot(gidx, G, dtype=jnp.float32).sum(axis=1) > 0
            masked = jnp.where(gmask[:, :, None], sg, -jnp.inf).reshape(T, E)
            topi = jax.lax.top_k(masked, TOPK)[1]
            weights = jnp.take_along_axis(scores, topi, axis=1) * ROUTE_SCALE
            combine = jnp.zeros((T, E), xt.dtype).at[jnp.arange(T)[:, None], topi].add(weights)
            h = jax.nn.silu(jnp.einsum('td,eid->eti', xt, W1)) * jnp.einsum('td,eid->eti', xt, W3)
            expert_out = jnp.einsum('eti,edi->etd', h, W2)
            y = jnp.einsum('etd,te->td', expert_out, combine)
            z = jax.nn.silu(xt @ Ws1.T) * (xt @ Ws3.T) @ Ws2.T
            return (y + z).reshape(B, S, D)
        key = jax.random.key(seed)
        ks = jax.random.split(key, 8)
        s = 0.02
        x = jax.random.normal(ks[0], (1, 256, DIM), dtype=jnp.float32)
        Wg = jax.random.normal(ks[1], (E, DIM), dtype=jnp.float32) * s
        W1 = jax.random.normal(ks[2], (E, INTER, DIM), dtype=jnp.float32) * s
        W3 = jax.random.normal(ks[3], (E, INTER, DIM), dtype=jnp.float32) * s
        W2 = jax.random.normal(ks[4], (E, DIM, INTER), dtype=jnp.float32) * s
        Ws1 = jax.random.normal(ks[5], (SHARED_INTER, DIM), dtype=jnp.float32) * s
        Ws3 = jax.random.normal(ks[6], (SHARED_INTER, DIM), dtype=jnp.float32) * s
        Ws2 = jax.random.normal(ks[7], (DIM, SHARED_INTER), dtype=jnp.float32) * s
        return {'x': x, 'Wg': Wg, 'W1': W1, 'W3': W3, 'W2': W2, 'Ws1': Ws1, 'Ws3': Ws3, 'Ws2': Ws2}
    _L0_ffn_all = _L0_ffn_setup()
    _L0_ffn_in = {k: v for k, v in _L0_ffn_all.items() if k in ('Wg', 'W1', 'W3', 'W2', 'Ws1', 'Ws3', 'Ws2')}
    del _L0_ffn_all

    def _L1_xattn_setup():
        import jax, jax.numpy as jnp
        import numpy as np
        B, Lq, Lk = (2, 512, 128)
        Q_DIM, KV_DIM = (256, 256)
        H, HD = (16, 128)
        KVC, QC, R = (64, 96, 64)
        LOOKBACK = 8
        NEG = -1e+30

        def _rope(x, L):
            half = x.shape[-1] // 2
            inv_freq = 1.0 / 10000.0 ** (jnp.arange(half, dtype=jnp.float32) / half)
            ang = jnp.arange(L, dtype=jnp.float32)[:, None] * inv_freq
            cos, sin = (jnp.cos(ang), jnp.sin(ang))
            x1, x2 = (x[..., :half], x[..., half:])
            return jnp.concatenate([x1 * cos - x2 * sin, x1 * sin + x2 * cos], axis=-1)
        key = jax.random.key(seed)
        ks = jax.random.split(key, 11)

        def w(k, shape, fan_in):
            return jax.random.normal(k, shape, jnp.float32) / np.sqrt(fan_in).astype(np.float32)
        return {'q': jax.random.normal(ks[0], (B, Lq, Q_DIM), jnp.float32), 'kv': jax.random.normal(ks[1], (B, Lk, KV_DIM), jnp.float32), 'seg_id': jnp.sort(jax.random.randint(ks[2], (B, Lq), 0, Lk), axis=-1), 'W_kvc': w(ks[3], (KV_DIM, KVC), KV_DIM), 'W_dq': w(ks[4], (Q_DIM, QC), Q_DIM), 'W_uq': w(ks[5], (QC, H * HD), QC), 'W_qr': w(ks[6], (QC, H * R), QC), 'W_uk': w(ks[7], (KVC, H * HD), KVC), 'W_kr': w(ks[8], (KVC, R), KVC), 'W_uv': w(ks[9], (KVC, H * HD), KVC), 'W_o': w(ks[10], (H * HD, Q_DIM), H * HD)}
    _L1_xattn_all = _L1_xattn_setup()
    _L1_xattn_in = {k: v for k, v in _L1_xattn_all.items() if k in ('W_kvc', 'W_dq', 'W_uq', 'W_qr', 'W_uk', 'W_kr', 'W_uv', 'W_o')}
    del _L1_xattn_all

    def _L1_ffn_setup():
        import jax, jax.numpy as jnp
        import numpy as np
        N_EXPERTS = 8
        TOP_K = 2
        C = 256
        H = 128
        HS = 256
        B, T = (1, 64)
        SCALE = 0.02
        key = jax.random.key(seed)
        ks = jax.random.split(key, 10)
        x = jax.random.normal(ks[0], (B, T, C), dtype=jnp.float32)
        gate_w = jax.random.normal(ks[1], (N_EXPERTS, C), dtype=jnp.float32) * SCALE
        w_gate = jax.random.normal(ks[2], (N_EXPERTS, H, C), dtype=jnp.float32) * SCALE
        w_up = jax.random.normal(ks[3], (N_EXPERTS, H, C), dtype=jnp.float32) * SCALE
        w_down = jax.random.normal(ks[4], (N_EXPERTS, C, H), dtype=jnp.float32) * SCALE
        sh_gate = jax.random.normal(ks[5], (HS, C), dtype=jnp.float32) * SCALE
        sh_up = jax.random.normal(ks[6], (HS, C), dtype=jnp.float32) * SCALE
        sh_down = jax.random.normal(ks[7], (C, HS), dtype=jnp.float32) * SCALE
        se_gate_w = jax.random.normal(ks[8], (1, C), dtype=jnp.float32) * SCALE
        return {'x': x, 'gate_w': gate_w, 'w_gate': w_gate, 'w_up': w_up, 'w_down': w_down, 'sh_gate': sh_gate, 'sh_up': sh_up, 'sh_down': sh_down, 'se_gate_w': se_gate_w}
    _L1_ffn_all = _L1_ffn_setup()
    _L1_ffn_in = {k: v for k, v in _L1_ffn_all.items() if k in ('gate_w', 'w_gate', 'w_up', 'w_down', 'sh_gate', 'sh_up', 'sh_down', 'se_gate_w')}
    del _L1_ffn_all
    return {'x': x, 'ctx_2048': ctx_2048, 'itok_BxS_0_1023': itok_BxS_0_1023, 'g_xattn': g_xattn, 'g_ffn': g_ffn, 'L0_xattn_decay': _L0_xattn_in['decay'], 'L0_xattn_W_in': _L0_xattn_in['W_in'], 'L0_xattn_b_in': _L0_xattn_in['b_in'], 'L0_xattn_W_out': _L0_xattn_in['W_out'], 'L0_xattn_b_out': _L0_xattn_in['b_out'], 'L0_xattn_gamma': _L0_xattn_in['gamma'], 'L0_xattn_beta': _L0_xattn_in['beta'], 'L0_ffn_Wg': _L0_ffn_in['Wg'], 'L0_ffn_W1': _L0_ffn_in['W1'], 'L0_ffn_W3': _L0_ffn_in['W3'], 'L0_ffn_W2': _L0_ffn_in['W2'], 'L0_ffn_Ws1': _L0_ffn_in['Ws1'], 'L0_ffn_Ws3': _L0_ffn_in['Ws3'], 'L0_ffn_Ws2': _L0_ffn_in['Ws2'], 'L1_xattn_W_kvc': _L1_xattn_in['W_kvc'], 'L1_xattn_W_dq': _L1_xattn_in['W_dq'], 'L1_xattn_W_uq': _L1_xattn_in['W_uq'], 'L1_xattn_W_qr': _L1_xattn_in['W_qr'], 'L1_xattn_W_uk': _L1_xattn_in['W_uk'], 'L1_xattn_W_kr': _L1_xattn_in['W_kr'], 'L1_xattn_W_uv': _L1_xattn_in['W_uv'], 'L1_xattn_W_o': _L1_xattn_in['W_o'], 'L1_ffn_gate_w': _L1_ffn_in['gate_w'], 'L1_ffn_w_gate': _L1_ffn_in['w_gate'], 'L1_ffn_w_up': _L1_ffn_in['w_up'], 'L1_ffn_w_down': _L1_ffn_in['w_down'], 'L1_ffn_sh_gate': _L1_ffn_in['sh_gate'], 'L1_ffn_sh_up': _L1_ffn_in['sh_up'], 'L1_ffn_sh_down': _L1_ffn_in['sh_down'], 'L1_ffn_se_gate_w': _L1_ffn_in['se_gate_w']}

def reference(x, ctx_2048, itok_BxS_0_1023, g_xattn, g_ffn, L0_xattn_decay, L0_xattn_W_in, L0_xattn_b_in, L0_xattn_W_out, L0_xattn_b_out, L0_xattn_gamma, L0_xattn_beta, L0_ffn_Wg, L0_ffn_W1, L0_ffn_W3, L0_ffn_W2, L0_ffn_Ws1, L0_ffn_Ws3, L0_ffn_Ws2, L1_xattn_W_kvc, L1_xattn_W_dq, L1_xattn_W_uq, L1_xattn_W_qr, L1_xattn_W_uk, L1_xattn_W_kr, L1_xattn_W_uv, L1_xattn_W_o, L1_ffn_gate_w, L1_ffn_w_gate, L1_ffn_w_up, L1_ffn_w_down, L1_ffn_sh_gate, L1_ffn_sh_up, L1_ffn_sh_down, L1_ffn_se_gate_w):
    import jax
    import jax.numpy as jnp

    def _L0_xattn_ref(Z, kv, decay, W_in, b_in, W_out, b_out, gamma, beta):
        import jax, jax.numpy as jnp
        import numpy as np
        from jax import lax
        LN_EPS = 1e-05
        B, T, D = kv.shape
        K = jax.nn.sigmoid(decay)
        x = jnp.einsum('btd,ed->bte', kv, W_in) + b_in

        def scan_fn(s, xt):
            s = K * s + xt
            return (s, s)
        s0 = jnp.zeros((B, D), dtype=kv.dtype)
        _, states = lax.scan(scan_fn, s0, jnp.swapaxes(x, 0, 1))
        states = jnp.swapaxes(states, 0, 1)
        proj = jnp.einsum('btd,ed->bte', states, W_out) + b_out
        summary = jnp.mean(proj, axis=1, keepdims=True)
        y = Z + summary
        mu = jnp.mean(y, axis=-1, keepdims=True)
        var = jnp.mean((y - mu) ** 2, axis=-1, keepdims=True)
        return (y - mu) / jnp.sqrt(var + LN_EPS) * gamma + beta

    def _L0_ffn_ref(x, Wg, W1, W3, W2, Ws1, Ws3, Ws2):
        import jax, jax.numpy as jnp
        import numpy as np
        DIM = 256
        INTER = 176
        E = 16
        TOPK = 4
        G = 4
        TOPK_G = 2
        N_SHARED = 2
        SHARED_INTER = N_SHARED * INTER
        ROUTE_SCALE = 1.0

        def _moe_forward(x, Wg, W1, W3, W2, Ws1, Ws3, Ws2):
            B, S, D = x.shape
            xt = x.reshape(-1, D)
            T = xt.shape[0]
            scores = jax.nn.softmax(xt @ Wg.T, axis=-1)
            sg = scores.reshape(T, G, E // G)
            group_scores = sg.max(axis=-1)
            gidx = jax.lax.top_k(group_scores, TOPK_G)[1]
            gmask = jax.nn.one_hot(gidx, G, dtype=jnp.float32).sum(axis=1) > 0
            masked = jnp.where(gmask[:, :, None], sg, -jnp.inf).reshape(T, E)
            topi = jax.lax.top_k(masked, TOPK)[1]
            weights = jnp.take_along_axis(scores, topi, axis=1) * ROUTE_SCALE
            combine = jnp.zeros((T, E), xt.dtype).at[jnp.arange(T)[:, None], topi].add(weights)
            h = jax.nn.silu(jnp.einsum('td,eid->eti', xt, W1)) * jnp.einsum('td,eid->eti', xt, W3)
            expert_out = jnp.einsum('eti,edi->etd', h, W2)
            y = jnp.einsum('etd,te->td', expert_out, combine)
            z = jax.nn.silu(xt @ Ws1.T) * (xt @ Ws3.T) @ Ws2.T
            return (y + z).reshape(B, S, D)
        return _moe_forward(x, Wg, W1, W3, W2, Ws1, Ws3, Ws2)

    def _L1_xattn_ref(q, kv, seg_id, W_kvc, W_dq, W_uq, W_qr, W_uk, W_kr, W_uv, W_o):
        import jax, jax.numpy as jnp
        import numpy as np
        B, Lq, Lk = (2, 512, 128)
        Q_DIM, KV_DIM = (256, 256)
        H, HD = (16, 128)
        KVC, QC, R = (64, 96, 64)
        LOOKBACK = 8
        NEG = -1e+30

        def _rope(x, L):
            half = x.shape[-1] // 2
            inv_freq = 1.0 / 10000.0 ** (jnp.arange(half, dtype=jnp.float32) / half)
            ang = jnp.arange(L, dtype=jnp.float32)[:, None] * inv_freq
            cos, sin = (jnp.cos(ang), jnp.sin(ang))
            x1, x2 = (x[..., :half], x[..., half:])
            return jnp.concatenate([x1 * cos - x2 * sin, x1 * sin + x2 * cos], axis=-1)
        b, lq, _ = q.shape
        lk = kv.shape[1]
        kv_c = kv @ W_kvc
        q_c = q @ W_dq
        q_nope = (q_c @ W_uq).reshape(b, lq, H, HD).transpose(0, 2, 1, 3)
        q_rope = (q_c @ W_qr).reshape(b, lq, H, R).transpose(0, 2, 1, 3)
        k_nope = (kv_c @ W_uk).reshape(b, lk, H, HD)
        v = (kv_c @ W_uv).reshape(b, lk, H, HD)
        k_rope = kv_c @ W_kr
        q_rope = _rope(q_rope, lq)
        k_rope = _rope(k_rope, lk)
        scale = 1.0 / np.sqrt(HD + R).astype(np.float32)
        scores = (jnp.einsum('bhqd,bkhd->bhqk', q_nope, k_nope) + jnp.einsum('bhqr,bkr->bhqk', q_rope, k_rope)) * scale
        k_ids = jnp.arange(lk)[None, None, :]
        qs = seg_id[:, :, None]
        good = (k_ids <= qs) & (k_ids >= qs - LOOKBACK)
        scores = jnp.where(good[:, None, :, :], scores, NEG)
        attn = jax.nn.softmax(scores, axis=-1)
        out = jnp.einsum('bhqk,bkhd->bqhd', attn, v).reshape(b, lq, H * HD)
        return out @ W_o

    def _L1_ffn_ref(x, gate_w, w_gate, w_up, w_down, sh_gate, sh_up, sh_down, se_gate_w):
        import jax, jax.numpy as jnp
        import numpy as np
        N_EXPERTS = 8
        TOP_K = 2
        C = 256
        H = 128
        HS = 256
        B, T = (1, 64)
        SCALE = 0.02
        Bb, Tt, Cc = x.shape
        xf = x.reshape(-1, Cc)
        scores = xf @ gate_w.T
        ew, ei = jax.lax.top_k(scores, TOP_K)
        ew = jax.nn.softmax(ew, axis=-1)
        x1 = jax.nn.silu(jnp.einsum('td,ehd->teh', xf, w_gate))
        x3 = jnp.einsum('td,ehd->teh', xf, w_up)
        expert_out = jnp.einsum('teh,edh->ted', x1 * x3, w_down)
        onehot = jax.nn.one_hot(ei, N_EXPERTS, dtype=ew.dtype)
        comb = jnp.einsum('ta,tae->te', ew, onehot)
        routed = jnp.einsum('te,ted->td', comb, expert_out)
        shared = jax.nn.silu(xf @ sh_gate.T) * (xf @ sh_up.T) @ sh_down.T
        sgate = jax.nn.sigmoid(xf @ se_gate_w.T)
        return (routed + sgate * shared).reshape(Bb, Tt, Cc)
    x = x + jnp.tanh(g_xattn[0]) * _L0_xattn_ref(_layernorm(x, axis=-1), ctx_2048, L0_xattn_decay, L0_xattn_W_in, L0_xattn_b_in, L0_xattn_W_out, L0_xattn_b_out, L0_xattn_gamma, L0_xattn_beta)
    x = x + jnp.tanh(g_ffn[0]) * _L0_ffn_ref(_layernorm(x, axis=-1), L0_ffn_Wg, L0_ffn_W1, L0_ffn_W3, L0_ffn_W2, L0_ffn_Ws1, L0_ffn_Ws3, L0_ffn_Ws2)
    x = x + jnp.tanh(g_xattn[1]) * _L1_xattn_ref(_layernorm(x, axis=-1), ctx_2048, itok_BxS_0_1023, L1_xattn_W_kvc, L1_xattn_W_dq, L1_xattn_W_uq, L1_xattn_W_qr, L1_xattn_W_uk, L1_xattn_W_kr, L1_xattn_W_uv, L1_xattn_W_o)
    x = x + jnp.tanh(g_ffn[1]) * _L1_ffn_ref(_layernorm(x, axis=-1), L1_ffn_gate_w, L1_ffn_w_gate, L1_ffn_w_up, L1_ffn_w_down, L1_ffn_sh_gate, L1_ffn_sh_up, L1_ffn_sh_down, L1_ffn_se_gate_w)
    return x

_drawn_inputs = setup_inputs


def setup_inputs(seed=0):
    import zlib

    import numpy as np

    out = dict(_drawn_inputs(seed))
    spreads = {'g_ffn': (-1.0, 0.6),
     'L0_xattn_b_in': (0.0, 0.1),
     'L0_xattn_b_out': (0.0, 0.1),
     'L0_xattn_gamma': (1.0, 0.2),
     'L0_xattn_beta': (0.0, 0.1)}
    factors = {'L0_ffn_Wg': 8.0,
     'L0_ffn_W1': 8.0,
     'L0_ffn_W3': 8.0,
     'L0_ffn_W2': 8.0,
     'L0_ffn_Ws1': 7.022,
     'L0_ffn_Ws3': 6.961,
     'L0_ffn_Ws2': 6.966,
     'L1_ffn_gate_w': 8.0,
     'L1_ffn_w_gate': 8.0,
     'L1_ffn_w_up': 8.0,
     'L1_ffn_w_down': 8.0,
     'L1_ffn_sh_gate': 8.0,
     'L1_ffn_sh_up': 8.0,
     'L1_ffn_sh_down': 8.0,
     'L1_ffn_se_gate_w': 8.0}
    for name, (base, spread) in spreads.items():
        noise = np.random.default_rng([zlib.crc32(name.encode()), seed]).standard_normal(out[name].shape)
        drawn = base * np.exp(spread * noise) if base else spread * noise
        out[name] = jnp.asarray(drawn.astype(out[name].dtype))
    for name, factor in factors.items():
        out[name] = (out[name] * factor).astype(out[name].dtype)
    return out
```

```python
from contextlib import ExitStack

import numpy as np

import concourse.bass as bass
from concourse import mybir

F32 = mybir.dt.float32
F32R = mybir.dt.float32r
BF16 = mybir.dt.bfloat16
I32 = mybir.dt.int32
U32 = mybir.dt.uint32
ALU = mybir.AluOpType
ACT = mybir.ActivationFunctionType
AX = mybir.AxisListType

P = 128
BATCH, SEQ, D = 32, 64, 256
TOKENS = BATCH * SEQ
TILES = TOKENS // P
KC = D // P
GROUPS = 4
GT = TILES // GROUPS
GTOK = GT * P
LN_EPS = 1e-5

E0, HID0, TOP0, EGROUPS, EPG, TOPG = 16, 176, 4, 4, 4, 2
HID0_REST = HID0 - P
W13_0 = 2 * HID0
COLS0 = KC * W13_0 + 2 * D
SH0 = 384
SHC0 = SH0 // P
SHCOLS0 = 2 * KC * SH0 + SHC0 * D
SLOTS0_NEED = (TOKENS * TOP0 - E0) // P + E0
UNROLL = 4
SLOTS0 = -(-SLOTS0_NEED // UNROLL) * UNROLL
EARLY0 = 10
E1, HID1, TOP1 = 8, 128, 2
W13_1 = 2 * HID1
COLS1 = KC * W13_1 + D
SH1 = 256
SHC1 = SH1 // P
SHCOLS1 = 2 * KC * SH1 + SHC1 * D
SLOTS1_NEED = (TOKENS * TOP1 - E1) // P + E1
SLOTS1 = -(-SLOTS1_NEED // UNROLL) * UNROLL
HEADS, HD, KVC, QC, ROPE, LOOKBACK = 16, 128, 64, 96, 64, 8
PAIRS = HEADS // 2
NEG = 1e30
SM_SCALE = float(1.0 / np.sqrt(np.float32(HD + ROPE)))

CONST = {}
_at = 0
for _name, _n in (("ident", 128), ("before", 128), ("cos", 64), ("sin", 64), ("key_id", 64),
                  ("keep", 256), ("expert_id", 16), ("earlier_group", 16), ("later_groups", 4),
                  ("slot_id", 80), ("same_head", 128)):
    CONST[_name] = (_at, _at + _n)
    _at += _n
NCONST = _at


def constants():
    c = np.zeros((P, NCONST), np.float32)

    def put(name, value):
        a, b = CONST[name]
        c[:, a:b] = value

    p = np.arange(P)
    put("ident", np.eye(P))
    put("before", p[:, None] < p[None, :])
    half = ROPE // 2
    inv = (1.0 / np.float32(10000.0) ** (np.arange(half, dtype=np.float32) / np.float32(half))).astype(np.float32)
    ang = np.arange(SEQ, dtype=np.float32)[None, :] * inv[p % half][:, None]
    put("cos", np.cos(ang))
    put("sin", np.sin(ang) * np.where(p % ROPE < half, -1.0, 1.0)[:, None])
    put("key_id", np.arange(SEQ)[None, :])
    put("keep", np.arange(256)[None, :] % TILES != 0)
    put("expert_id", np.arange(16)[None, :])
    j = np.arange(16)
    put("earlier_group", (j % 4 < j // 4)[None, :])
    put("later_groups", 3 - np.arange(4)[None, :])
    put("slot_id", np.arange(80)[None, :])
    put("same_head", (p[:, None] // 64) == (p[None, :] // 64))
    select = (np.arange(TOKENS)[None, :] // SEQ == np.arange(BATCH)[:, None]).astype(np.float32)
    return c, select


class Map:

    BASE, END = 16512, 229312

    def __init__(self, nc):
        self.nc, self.at, self.top = nc, self.BASE, self.BASE

    def put(self, name, shape, dtype, at=None):
        size = int(np.prod(shape[1:])) * (2 if dtype == BF16 else 4)
        size = -(-size // 64) * 64
        if at is None:
            at = self.at
            self.at += size
        self.end = at + size
        self.top = max(self.top, self.end)
        assert self.end <= self.END, (name, self.end)
        return self.nc.alloc_sbuf_tensor_at(name, shape, dtype, offset=at)


class Moe:
    pass


def build_program(nc, a):
    ctx = ExitStack()
    with ctx:
        def sem(name):
            return ctx.enter_context(nc.semaphore(name))

        m = Map(nc)
        X = m.put("X", [P, TILES, D], F32)
        C = m.put("C", [P, NCONST], F32)
        PAR = m.put("PAR", [P, 16], F32)
        TRI = m.put("TRI", [P, P], BF16)
        ONES = m.put("ONES", [P, P], BF16)
        SEL = m.put("SEL", [P, TILES, 16], BF16)
        STAT = m.put("STAT", [P, TILES, 6], F32)
        MV = m.put("MV", [P, TILES, 2], F32)
        RSTD = m.put("RSTD", [P, TILES], F32)
        SHIFT = m.put("SHIFT", [P, TILES], F32)
        SD = m.put("SD", [P, TILES], F32)
        TOPW = m.put("TOPW", [P, TILES, 8], F32)
        TOPI = m.put("TOPI", [P, TILES, 8], U32)
        WK = m.put("WK", [P, 4, TILES], F32)
        SGATE = m.put("SGATE", [P, TILES], F32)
        POSI = m.put("POSI", [P, 4, TILES], U32)
        EID = m.put("EID", [1, SLOTS0], I32)
        SMALL = m.put("SMALL", [P, 8, 16], F32)
        SMALLI = m.put("SMALLI", [P, 16], I32)
        ONE64 = m.put("ONE64", [P, SEQ], F32)
        ITOK = m.put("ITOK", [P, TILES], I32)
        SEG = m.put("SEG", [P, TILES], F32)
        phase_base = m.at

        GB_AT = Map.END - 8 * D * 4

        def slot_buffers(M, at):
            q = at
            M.XS = m.put(M.tag + "XS", [P, 4, D], F32, at=q); q = m.end
            M.XHI = m.put(M.tag + "XHI", [P, 2, D], F32R, at=q); q = m.end
            M.XLO = m.put(M.tag + "XLO", [P, 2, D], F32R, at=q); q = m.end
            M.SIL = m.put(M.tag + "SIL", [P, 2, M.hid], F32, at=q); q = m.end
            M.G = m.put(M.tag + "G", [P, 2, M.hchunks * P], F32, at=q); q = m.end
            M.GHI = m.put(M.tag + "GHI", [P, 2, M.hchunks * P], F32R, at=q); q = m.end
            M.GLO = m.put(M.tag + "GLO", [P, 2, M.hchunks * P], F32R, at=q); q = m.end
            M.YS = m.put(M.tag + "YS", [P, 4, D], F32, at=q); q = m.end
            M.GB = m.put(M.tag + "GB", [P, 8, D], F32, at=GB_AT)
            return q

        both = [sem(name) for name in (
            "xn_transposed", "xn_transpose_copied", "logits_done", "logits_copied", "logits_token_major", "gate_loaded",
            "shared_loaded", "shared_split", "shared_x_split", "shared_hidden", "shared_silu", "shared_product",
            "shared_hi", "shared_lo", "shared_out", "shared_added", "expert_hi", "expert_weights_ready", "combined",
            "slot_xT", "slot_x_hi", "slot_x_lo", "slot_hidden", "slot_silu", "slot_g", "slot_gT", "slot_g_hi", "slot_g_lo",
            "slot_y", "slot_y_copied")]
        raw = [sem(f"expert{e}_loaded") for e in range(E0)]
        xl = [sem(f"slot_x_loaded{r}") for r in range(4)]
        st = [sem(f"slot_y_stored{r}") for r in range(4)]
        gath = [sem(f"gathered{r}") for r in range(8)]

        def moe(tag, before, E, hid, top, slots, shared):
            M = Moe()
            M.tag, M.E, M.hid, M.top, M.slots = tag, E, hid, top, slots
            M.hchunks = -(-hid // P)
            M.w13 = 2 * hid
            M.cols = KC * M.w13 + M.hchunks * D
            M.sh, M.shc = shared, shared // P
            M.x_by_expert = nc.dram_tensor(tag + "x_by_expert", [slots * P, D], F32, kind="Internal").ap()
            M.y_by_expert = nc.dram_tensor(tag + "y_by_expert", [slots * P, D], F32, kind="Internal").ap()
            (M.shifted, M.exped, M.sel, M.counts, M.routed, M.pos, M.eid, M.fill, M.scat) = [sem(tag + name) for name in (
                "scores_shifted", "scores_exp", "choice_ready", "counts_done", "routing_left_psum", "rows_known",
                "slot_experts_known", "rows_cleared", "rows_scattered")]
            (M.xt, M.xtc, M.lg, M.lgc, M.lgt, M.wg, M.shw, M.shsplit, M.shx, M.shh, M.shs, M.shu, M.shg, M.shl, M.shy,
             M.shadd, M.split, M.wready, M.comb, M.p_xt, M.a_xhi, M.d_xlo, M.p_h, M.a_sil, M.d_g, M.p_gt, M.a_ghi, M.d_glo,
             M.p_y, M.a_y) = both
            M.raw, M.xl, M.st, M.gath = raw, xl, st, gath
            M.n = 1 if before else 0
            M.slot0 = before.slots if before else 0
            M.chunk0 = GROUPS * before.shc if before else 0
            M.expert0 = before.E if before else 0
            M.copy0 = TILES * before.top if before else 0
            return M

        L0 = moe("l0_", None, E0, HID0, TOP0, SLOTS0, SH0)
        L0.pass_no = 2
        L0.norm_base = 2 * TILES
        L0.logits = E0
        L0.WHI = m.put("W0HI", [P, E0, COLS0], F32R)
        w0lo_at = m.at
        L0.WLO = m.put("W0LO", [P, E0, COLS0], F32R)
        L0.WRAW = [m.put(f"W0RAW{e}", [P, COLS0], F32, at=w0lo_at + e * COLS0 * 4) for e in range(E0)]
        tail_at = m.at
        hi_late = phase_base + EARLY0 * COLS0 * 4
        lo_late = w0lo_at + EARLY0 * COLS0 * 4
        late_size = (E0 - EARLY0) * COLS0 * 4
        XN = L0.XN = m.put("XN", [P, TILES, D], F32, at=tail_at)
        slot_buffers(L0, tail_at)
        q = hi_late
        L0.SHRAW = m.put("SH0RAW", [P, SHCOLS0], F32, at=q)
        L0.SHLO = m.put("SH0LO", [P, SHCOLS0], F32R, at=q); q = m.end
        L0.SHHI = m.put("SH0HI", [P, SHCOLS0], F32R, at=q); q = m.end
        L0.XSHI = m.put("XS0HI", [P, KC, GTOK], F32R, at=q); q = m.end
        L0.XSLO = m.put("XS0LO", [P, KC, GTOK], F32R, at=q); q = m.end
        L0.WG = m.put("WG0", [P, KC, E0], F32, at=q); q = m.end
        assert q <= hi_late + late_size, (q - hi_late, late_size)
        q = lo_late
        L0.XT = m.put("XT0", [P, KC, TOKENS], F32, at=q); q = m.end
        L0.SGHI = m.put("SG0HI", [P, SHC0, GTOK], F32R, at=q); q = m.end
        L0.SGLO = m.put("SG0LO", [P, SHC0, GTOK], F32R, at=q); q = m.end
        assert q <= lo_late + late_size
        q = phase_base + 4 * COLS0 * 4
        CTX = m.put("CTX", [P, KC, TOKENS], F32, at=q); q = m.end
        L0.SSIL = m.put("SSIL0", [P, 2, GTOK], F32, at=q); q = m.end
        L0.SU = m.put("SU0", [P, 2, GTOK], F32, at=q); q = m.end
        L0.LGT = m.put("LGT0", [16, GTOK], F32, at=q); q = m.end
        ZERO = m.put("ZERO", [P, D], F32, at=q); q = m.end
        assert q <= hi_late
        q = w0lo_at + 6 * COLS0 * 4
        CTXW = m.put("CTXW", [P, TOKENS], F32, at=q); q = m.end
        WIN = m.put("WIN", [P, KC, D], F32, at=q); q = m.end
        WOUT = m.put("WOUT", [P, KC, D], F32, at=q); q = m.end
        BOUT = m.put("BOUT", [P, D], F32, at=q); q = m.end
        GAMMA = m.put("GAMMA", [P, D], F32, at=q); q = m.end
        BETA = m.put("BETA", [P, D], F32, at=q); q = m.end
        assert q <= lo_late
        SELB = m.put("SELB", [BATCH, TOKENS], F32, at=phase_base)
        q = m.end
        EMA = m.put("EMA", [P, SEQ], F32, at=q); q = m.end
        EMAC = m.put("EMAC", [P, SEQ], F32, at=q); q = m.end
        CSUM = m.put("CSUM", [P, KC, BATCH], F32, at=q); q = m.end
        M1T = m.put("M1T", [P, KC, BATCH], F32, at=q); q = m.end
        SUMM = m.put("SUMM", [BATCH, D], F32, at=q); q = m.end
        BIN = m.put("BIN", [P, KC], F32, at=q); q = m.end
        L0.R = [m.put(f"R0_{i}", [P, 16, 16], F32, at=q + 1024 * i) for i in range(8)]
        assert m.end <= phase_base + 4 * COLS0 * 4
        L0.XCMP = m.put("XCMP0", [1, SLOTS0 * (E0 + 1)], F32, at=phase_base + 4 * COLS0 * 4)

        q = phase_base
        KB = m.put("KB", [P, TILES, 4, P], F32, at=q); q = m.end
        KR = m.put("KR", [P, 4, 4, P], F32, at=q); q = m.end
        AHI = m.put("AHI", [QC, PAIRS, 3, P], F32R, at=q); q = m.end
        ARAW = m.put("ARAW", [QC, PAIRS, 3, P], F32, at=q)
        ALO = m.put("ALO", [QC, PAIRS, 3, P], F32R, at=q); q = m.end
        BHI = m.put("BHI", [P, PAIRS, D], F32R, at=q); q = m.end
        BLO = m.put("BLO", [P, PAIRS, D], F32R, at=q); q = m.end
        MASK = m.put("MASK", [P, TILES, SEQ], F32, at=q); q = m.end
        WDQ = m.put("WDQ", [P, KC, QC], F32, at=q); q = m.end
        WKR = m.put("WKR", [KVC, 2, P], F32, at=q); q = m.end
        WKVC = m.put("WKVC", [P, KC, P], F32, at=q); q = m.end
        XNG = m.put("XNG", [P, 2, 2, D], F32, at=q); q = m.end
        XTG = m.put("XTG", [P, KC, 2 * P], F32, at=q); q = m.end
        QCHI = m.put("QCHI", [QC, 2 * P], F32R, at=q); q = m.end
        QCLO = m.put("QCLO", [QC, 2 * P], F32R, at=q); q = m.end
        RC = m.put("RC", [P, 2, 2 * P], F32, at=q); q = m.end
        RS = m.put("RS", [P, 2, 2 * P], F32, at=q); q = m.end
        CTHI = m.put("CTHI", [P, PAIRS, P], F32R, at=q); q = m.end
        CTLO = m.put("CTLO", [P, PAIRS, P], F32R, at=q); q = m.end
        OX = m.put("OX", [P, 2, D], F32, at=q); q = m.end
        SMX = m.put("SMX", [P, 2, 2, HEADS], F32, at=q); q = m.end
        prep_at = q
        Q = m.put("Q", [P, 2, HEADS, 2 * P], F32, at=q); q = m.end
        SM = m.put("SM", [P, 2, HEADS, SEQ], F32, at=q); q = m.end
        PT = m.put("PT", [P, PAIRS, P], F32, at=q); q = m.end
        assert q <= GB_AT
        q = prep_at
        CTX1 = m.put("CTX1", [P, KC, TOKENS], F32, at=q); q = m.end
        UQT = m.put("UQT", [P, HEADS, QC], F32, at=q); q = m.end
        UKT = m.put("UKT", [P, HEADS, KVC], F32, at=q); q = m.end
        UVT = m.put("UVT", [P, HEADS, KVC], F32, at=q); q = m.end
        WO = m.put("WO", [P, HEADS, D], F32, at=q); q = m.end
        assert q <= GB_AT, (prep_at, q, GB_AT)

        L1 = moe("l1_", L0, E1, HID1, TOP1, SLOTS1, SH1)
        L1.pass_no = 4
        L1.norm_base = 3 * TILES
        L1.logits = E1 + 1
        q = phase_base
        L1.WHI = m.put("W1HI", [P, E1, COLS1], F32R, at=q); q = m.end
        w1lo_at = q
        L1.WLO = m.put("W1LO", [P, E1, COLS1], F32R, at=q); q = m.end
        L1.WRAW = [m.put(f"W1RAW{e}", [P, COLS1], F32, at=w1lo_at + e * COLS1 * 4) for e in range(E1)]
        L1.SHRAW = m.put("SH1RAW", [P, SHCOLS1], F32, at=q)
        L1.SHLO = m.put("SH1LO", [P, SHCOLS1], F32R, at=q); q = m.end
        L1.SHHI = m.put("SH1HI", [P, SHCOLS1], F32R, at=q); q = m.end
        L1.XSHI = m.put("XS1HI", [P, KC, GTOK], F32R, at=q); q = m.end
        L1.XSLO = m.put("XS1LO", [P, KC, GTOK], F32R, at=q); q = m.end
        L1.WG = m.put("WG1", [P, KC, E1 + 1], F32, at=q); q = m.end
        L1.XT = m.put("XT1", [P, KC, TOKENS], F32, at=q); q = m.end
        L1.SGHI = m.put("SG1HI", [P, SHC1, GTOK], F32R, at=q); q = m.end
        L1.SGLO = m.put("SG1LO", [P, SHC1, GTOK], F32R, at=q); q = m.end
        L1.SSIL = m.put("SSIL1", [P, 2, GTOK], F32, at=q); q = m.end
        L1.SU = m.put("SU1", [P, 2, GTOK], F32, at=q); q = m.end
        L1.LGT = m.put("LGT1", [16, GTOK], F32, at=q); q = m.end
        L1.R = [m.put(f"R1_{i}", [P, 16, 16], F32, at=q + 1024 * i) for i in range(8)]; q = m.end
        L1.XCMP = m.put("XCMP1", [1, SLOTS1 * (E1 + 1)], F32, at=q); q = m.end
        L1.XN = m.put("XN1", [P, TILES, D], F32, at=q); q = m.end
        slot_buffers(L1, q)

        PS = ctx.enter_context(nc.psum_tensor("PS", [P, 8, 512], F32))
        B = [PS[:, i, :] for i in range(8)]

        def const(name, rows=P):
            lo, hi = CONST[name]
            return C[0:rows, lo:hi]

        ident = const("ident")

        DECAY, KEEP, GX, TX, GF, TF, BC, CTOT = 0, 1, 2, 4, 6, 8, 10, 12
        L0.gate, L1.gate = TF, TF + 1

        s_const = sem("const_loaded")
        s_par = sem("params_loaded")
        s_x = [sem(f"x_loaded{g}") for g in range(GROUPS)]
        s_ctx = [sem(f"ctx_loaded{k}") for k in range(KC)]
        s_wio = sem("ema_weights_loaded")
        s_zero = sem("zero_tile")
        s_act = sem("act_chain")
        s_dve = sem("dve_chain")
        s_pool = sem("pool_chain")
        s_var = sem("variance_ready")
        s_sd = sem("sqrt_ready")
        s_rstd = sem("rstd_ready")
        s_norm = sem("tiles_normalised")
        s_beta = sem("beta_scaled")
        s_xb = sem("beta_added")
        s_csum = sem("ctx_sums_ready")
        s_m1 = sem("m1_done")
        s_m1t = sem("m1_copied")
        s_summ = sem("summary_done")
        s_summc = sem("summary_copied")
        s_spread = sem("summary_spread")
        s_spused = sem("spread_used")
        k_ctx, k_wkv, k_up, k_raw = sem("k_ctx_loaded"), sem("k_wkv_loaded"), sem("k_up_loaded"), sem("k_raw_loaded")
        k_zero = sem("kv_blocks_zeroed")
        k_kvc, k_kvcc = sem("kvc_done"), sem("kvc_copied")
        k_tok, k_tokc = sem("kvc_token_done"), sem("kvc_token_copied")
        k_rope, k_ropem, k_roped = sem("key_rope_done"), sem("key_rope_terms"), sem("key_rope_added")
        k_a, k_ahi, k_alo = sem("absorbed_done"), sem("absorbed_hi"), sem("absorbed_lo")
        k_b, k_bhi, k_blo = sem("out_weights_done"), sem("out_weights_hi"), sem("out_weights_lo")
        k_mask = sem("mask_ready")
        t_norm, t_xt, t_xtc = sem("pair_normalised"), sem("pair_transposed"), sem("pair_transpose_copied")
        t_qc, t_qchi, t_qclo = sem("qc_done"), sem("qc_hi"), sem("qc_lo")
        t_abs, t_absc, t_rv, t_rvm, t_q = (sem("q_absorbed"), sem("q_absorbed_copied"), sem("q_rope_done"),
                                           sem("q_rope_terms"), sem("q_rope_added"))
        t_kl = [sem(f"keys_loaded{r}") for r in range(4)]
        t_s, t_masked, t_max, t_sub, t_exp, t_sum, t_rec, t_prob = (sem("scores"), sem("scores_masked"), sem("row_max"),
                                                            sem("max_subtracted"), sem("exp_done"), sem("row_sum"), sem("row_sum_inverse"),
                                                            sem("probs_ready"))
        t_pt, t_ptc, t_ct, t_cthi, t_ctlo = (sem("probsT"), sem("probsT_copied"), sem("ctxT"), sem("ctxT_hi"),
                                             sem("ctxT_lo"))
        t_o, t_oc, t_x = sem("attn_out"), sem("attn_out_scaled"), sem("attn_added")
        s_out = sem("out_stored")

        class Count:

            def __init__(self, eng, semaphore):
                self.eng, self.sem, self.n = eng, semaphore, 0

            def mark(self, ins):
                ins.then_inc(self.sem, 1)
                self.n += 1
                return ins

            def wait(self, back=0):
                self.eng.wait_ge(self.sem, self.n - back)

        def at_least(i, n):
            return not isinstance(i, int) or i >= n

        x_rows = a["x"].rearrange("(t p) d -> p t d", p=P)
        out_rows = a["out"].rearrange("(t p) d -> p t d", p=P)

        def run_stages(i, j, slots, stages):
            for d, stage in stages:
                if not isinstance(i, int) or 0 <= i + d < slots:
                    stage(i + d, (j + d) % UNROLL)

        def slot_loop(eng, slots, step, lead, trail):
            for i in range(-lead, UNROLL):
                step(i, i % UNROLL)
            with eng.Fori(1, slots // UNROLL - 1) as it:
                for j in range(UNROLL):
                    step(it * UNROLL + j, j)
            for i in range(slots - UNROLL, slots + trail):
                step(i, i % UNROLL)

        def tile_loop(eng, step):
            for i in range(-4, UNROLL):
                step(i, i % UNROLL, i // UNROLL * 2)
            with eng.Fori(1, TILES // UNROLL - 1) as it:
                for j in range(UNROLL):
                    step(it * UNROLL + j, j, it * 2)
            for i in range(TILES - UNROLL, TILES + 1):
                step(i, i % UNROLL, i // UNROLL * 2)

        def tile(i, j, h, d, stage):
            if not isinstance(i, int) or 0 <= i + d < TILES:
                stage(i + d, (j + d) % 4, h + (j + d) // 2, (j + d) % 2)

        def pair(i, j, h, d, stage):
            if not isinstance(i, int) or 0 <= i + d < TILES:
                stage(h + (j + d) // 2, (j + d) // 2 % 2)

        block = ctx.enter_context(nc.Block())

        def load_gate_and_shared(sp, M, n):
            sp.dma_start(M.WG[:, :, :], a[f"Wg{n}T"].rearrange("(k p) n -> p k n", p=P)).then_inc(M.wg, 16)
            sp.dma_start(M.SHRAW[:, :], a[f"sh{n}"]).then_inc(M.shw, 16)

        def stream_slots(sp, M):
            def load(i, r):
                if at_least(i, 4):
                    sp.wait_ge(M.p_xt, i + (M.slot0 - 3))
                sp.dma_start(M.XS[:, r, :], M.x_by_expert[bass.ds(i * P, P), :]).then_inc(M.xl[r], 16)

            def store(i, r):
                sp.wait_ge(M.a_y, i + (M.slot0 + 1))
                sp.dma_start(M.y_by_expert[bass.ds(i * P, P), :], M.YS[:, r, :]).then_inc(M.st[r], 16)

            for i in range(4):
                load(i, i)
            for i in range(4):
                load(i + 4, i)
                store(i, i)
            with sp.Fori(1, M.slots // UNROLL - 1) as it:
                for j in range(UNROLL):
                    load(it * UNROLL + (j + 4), j)
                    store(it * UNROLL + j, j)
            for i in range(M.slots - 4, M.slots):
                store(i, i % 4)

        @block.sync
        def _(sp):
            sp.dma_start(C[:, :], a["const"]).then_inc(s_const, 16)
            sp.dma_start(PAR[:, DECAY:DECAY + 1], a["decay"].to_broadcast([P, 1])).then_inc(s_par, 16)
            sp.dma_start(PAR[:, GX:GX + 2], a["g_xattn"].to_broadcast([P, 2])).then_inc(s_par, 16)
            sp.dma_start(PAR[:, GF:GF + 2], a["g_ffn"].to_broadcast([P, 2])).then_inc(s_par, 16)
            sp.dma_start(BIN[:, :], a["b_in"]).then_inc(s_par, 16)
            for g in range(GROUPS):
                sp.dma_start(X[:, g * GT:(g + 1) * GT, :], x_rows[:, g * GT:(g + 1) * GT, :]).then_inc(s_x[g], 16)
            for k in range(KC):
                sp.dma_start(CTX[:, k, :], a["ctxT"][k * P:(k + 1) * P, :]).then_inc(s_ctx[k], 16)
            sp.dma_start(WIN[:, :, :], a["W_inT"].rearrange("(k p) n -> p k n", p=P)).then_inc(s_wio, 16)
            sp.dma_start(WOUT[:, :, :], a["W_outT"].rearrange("(k p) n -> p k n", p=P)).then_inc(s_wio, 16)
            sp.dma_start(BOUT[:, :], a["b_out"].to_broadcast([P, D])).then_inc(s_wio, 16)
            sp.dma_start(GAMMA[:, :], a["gamma"].to_broadcast([P, D])).then_inc(s_wio, 16)
            sp.dma_start(BETA[:, :], a["beta"].to_broadcast([P, D])).then_inc(s_wio, 16)
            sp.dma_start(SELB[:, :], a["select"]).then_inc(s_wio, 16)
            load_gate_and_shared(sp, L0, 0)
            sp.wait_ge(s_zero, 2)
            for M in (L0, L1):
                sp.dma_start(M.x_by_expert.rearrange("(n p) d -> p n d", p=P),
                             ZERO[:, :].unsqueeze(1).to_broadcast([P, M.slots, D])).then_inc(M.fill, 16)
            sp.wait_ge(L0.lgt, TILES)
            sp.wait_ge(L0.fill, 16)
            sp.wait_ge(L1.fill, 16)
            for e in range(EARLY0):
                sp.dma_start(L0.WRAW[e][:, :], a["w0"][e]).then_inc(L0.raw[e], 16)
            sp.wait_ge(L0.shadd, TILES)
            for e in range(EARLY0, E0):
                sp.dma_start(L0.WRAW[e][:, :], a["w0"][e]).then_inc(L0.raw[e], 16)
            sp.wait_ge(L0.scat, 16 * TILES * TOP0)
            stream_slots(sp, L0)
            sp.wait_ge(L0.wready, E0)
            sp.dma_start(ITOK[:, :], a["seg"]).then_inc(k_wkv, 16)
            sp.dma_start(WKVC[:, :, :], a["W_kvc2"].rearrange("p (k n) -> p k n", k=KC)).then_inc(k_wkv, 16)
            sp.dma_start(WKR[:, :, :], a["W_kr2"].rearrange("p (k n) -> p k n", k=2)).then_inc(k_wkv, 16)
            sp.dma_start(WDQ[:, :, :], a["W_dq"].rearrange("p (k n) -> p k n", k=KC)).then_inc(k_wkv, 16)
            for k in range(KC):
                sp.dma_start(CTX1[:, k, :], a["ctxT"][k * P:(k + 1) * P, :]).then_inc(k_ctx, 16)
            sp.dma_start(ARAW[:, :, 1:3, :], a["W_qrv"].rearrange("q (p v n) -> q p v n", p=PAIRS, v=2)).then_inc(k_raw, 16)
            sp.dma_start(UQT[:, :, :], a["W_uqT"].rearrange("p (h n) -> p h n", h=HEADS)).then_inc(k_up, 16)
            sp.dma_start(UKT[:, :, :], a["W_ukT"].rearrange("p (h n) -> p h n", h=HEADS)).then_inc(k_up, 16)
            sp.dma_start(UVT[:, :, :], a["W_uvT"].rearrange("p (h n) -> p h n", h=HEADS)).then_inc(k_up, 16)
            sp.dma_start(WO[:, :, :], a["W_oh"].rearrange("p (h n) -> p h n", h=HEADS)).then_inc(k_up, 16)
            sp.wait_ge(k_roped, 2 * GROUPS)
            sp.wait_ge(k_kvcc, 2 * GROUPS)
            sp.wait_ge(k_tokc, 4 * GROUPS)

            def keys(i, r, u, o):
                if at_least(i, 4):
                    sp.wait_ge(t_ct, i * 2 - 6)
                sp.dma_start(KR[:, r, :, :], KB[:, bass.ds(i, 1), :, :].rearrange("p o k n -> p (o k) n"))\
                    .then_inc(t_kl[r], 16)

            tile_loop(sp, lambda i, j, h: tile(i, j, h, 4, keys))
            sp.wait_ge(t_x, TILES)
            load_gate_and_shared(sp, L1, 1)
            for e in range(E1):
                sp.dma_start(L1.WRAW[e][:, :], a["w1"][e]).then_inc(L1.raw[e], 16)
            sp.wait_ge(L1.scat, 16 * TILES * TOP1)
            stream_slots(sp, L1)
            for g in range(GROUPS):
                sp.wait_ge(L1.comb, L1.copy0 + (g + 1) * GT * TOP1)
                sp.dma_start(out_rows[:, g * GT:(g + 1) * GT, :], X[:, g * GT:(g + 1) * GT, :]).then_inc(s_out, 16)
            sp.wait_ge(s_out, 16 * GROUPS)

        def scatter(pool, M):
            pool.wait_ge(M.fill, 16)
            pool.wait_ge(M.pos, 1)
            for t in range(TILES):
                for k in range(M.top):
                    pool.indirect_dma_start(M.x_by_expert, bass.IndirectOffsetOnAxis(POSI[:, k, t:t + 1], 0),
                                            M.XN[:, t, :], None, bounds_check=M.slots * P - 1,
                                            oob_is_err=False).then_inc(M.scat, 16)

        def gather(pool, M):
            for r in range(4):
                pool.wait_ge(M.st[r], 16 * ((M.slot0 + M.slots) // 4))
            for t in range(TILES):
                for k in range(M.top):
                    n = M.copy0 + t * M.top + k
                    if n >= 8:
                        pool.wait_ge(M.comb, n - 7)
                    pool.indirect_dma_start(M.GB[:, n % 8, :], None, M.y_by_expert,
                                            bass.IndirectOffsetOnAxis(POSI[:, k, t:t + 1], 0),
                                            bounds_check=M.slots * P - 1,
                                            oob_is_err=False).then_inc(M.gath[n % 8], 16)

        @block.gpsimd
        def _(pool):
            ch = Count(pool, s_pool)
            pool.memset(ZERO[:, :], 0.0).then_inc(s_zero, 1)
            pool.memset(ONE64[:, :], 1.0).then_inc(s_zero, 1)
            pool.wait_ge(s_wio, 16 * 6)
            pool.wait_ge(s_beta, 1)
            for t in range(TILES):
                pool.wait_ge(s_norm, t + 1)
                pool.tensor_tensor(X[:, t, :], X[:, t, :], BETA[:, :], ALU.add).then_inc(s_xb, 1)
            scatter(pool, L0)
            pool.wait_ge(L0.wready, EARLY0)
            for e in range(EARLY0, E0):
                pool.wait_ge(L0.raw[e], 16)
                ch.mark(pool.tensor_scalar(L0.WHI[:, e, :], L0.WRAW[e][:, :], 1.0, None, ALU.mult))
                ch.wait()
                pool.tensor_tensor(L0.WLO[:, e, :], L0.WRAW[e][:, :], L0.WHI[:, e, :].bitcast(F32),
                                   ALU.subtract).then_inc(L0.wready, 1)
            gather(pool, L0)
            cos = const("cos").unsqueeze(1)

            def roped(u, n):
                c = u * 2 * PAIRS + n
                return min(c, TILES * PAIRS) if isinstance(c, int) else c

            def sub(i, r, u, o):
                pool.wait_ge(t_max, i + 1)
                pool.wait_ge(t_q, roped(u, 2 * PAIRS + 8 * o))
                pool.tensor_tensor(SM[:, r % 2, :, :], SM[:, r % 2, :, :],
                                   SMX[:, r % 2, 0, :].unsqueeze(2).to_broadcast([P, HEADS, SEQ]), ALU.subtract)\
                    .then_inc(t_sub, 1)

            def prob(i, r, u, o):
                pool.wait_ge(t_rec, i + 1)
                pool.wait_ge(t_q, roped(u, 2 * PAIRS + 8 * o + 4))
                pool.tensor_tensor(SM[:, r % 2, :, :], SM[:, r % 2, :, :],
                                   SMX[:, r % 2, 1, :].unsqueeze(2).to_broadcast([P, HEADS, SEQ]), ALU.mult)\
                    .then_inc(t_prob, 1)

            def rope(p):
                def stage(v, par):
                    pool.wait_ge(t_rvm, v * 2 * PAIRS + (2 * p + 2))
                    if at_least(v, 2):
                        pool.wait_ge(t_s, v * 4 - 4)
                    before = v * 2 + (-1 if p < 4 else 0)
                    if p % 2 == 0 and (not isinstance(v, int) or before > 0):
                        pool.wait_ge(t_prob if p % 4 else t_sub, before)
                    for n, half, head in ((0, 0, 2 * p + 1), (1, 64, 2 * p)):
                        s = slice(half, half + 64)
                        if not (isinstance(v, int) and v == 0 and 2 * p + n == 0):
                            pool.wait_ge(t_q, v * 2 * PAIRS + 2 * p + n)
                        pool.tensor_tensor(Q[s, par, head, :], RC[s, p % 2, :], RS[s, p % 2, :], ALU.add)\
                            .then_inc(t_q, 1)
                return stage

            def add_x(i, r, u, o):
                pool.wait_ge(t_oc, i + 1)
                pool.wait_ge(t_q, roped(u, 4 * PAIRS + 8 + 8 * o))
                at = bass.ds(i, 1)
                pool.tensor_tensor(X[:, at, :].rearrange("p o d -> p (o d)"), X[:, at, :].rearrange("p o d -> p (o d)"),
                                   OX[:, r % 2, :], ALU.add).then_inc(t_x, 1)

            def step(i, j, h):
                tile(i, j, h, 1, sub)
                first = 0 if j % 2 else 4
                d = 3 if j % 2 else 2
                for p in (first, first + 1):
                    pair(i, j, h, d, rope(p))
                tile(i, j, h, 1, prob)
                for p in (first + 2, first + 3):
                    pair(i, j, h, d, rope(p))
                tile(i, j, h, -1, add_x)

            tile_loop(pool, step)
            scatter(pool, L1)
            gather(pool, L1)

        @block.scalar
        def _(act):
            act.wait_ge(s_par, 16 * 4)
            act.activation(PAR[:, KEEP:KEEP + 1], PAR[:, DECAY:DECAY + 1], ACT.Sigmoid).then_inc(s_act, 1)
            act.activation(PAR[:, TX:TX + 2], PAR[:, GX:GX + 2], ACT.Tanh).then_inc(s_act, 1)
            act.activation(PAR[:, TF:TF + 2], PAR[:, GF:GF + 2], ACT.Tanh).then_inc(s_act, 1)

            def sqrt_group(c):
                s = slice(c % GROUPS * GT, (c % GROUPS + 1) * GT)
                act.wait_ge(s_var, c + 1)
                act.activation(SD[:, s], SD[:, s], ACT.Sqrt).then_inc(s_sd, 1)
                act.wait_ge(s_rstd, c + 1)

            def norm_pass(n, src):
                for g in range(GROUPS):
                    sqrt_group(n * GROUPS + g)
                    for t in range(g * GT, (g + 1) * GT):
                        act.activation(XN[:, t, :], src[:, t, :], ACT.Identity, bias=SHIFT[:, t:t + 1],
                                       scale=RSTD[:, t:t + 1]).then_inc(s_norm, 1)

            norm_pass(0, X)
            norm_pass(1, XN)

            def norm_and_gate(M):
                for g in range(GROUPS):
                    sqrt_group(M.pass_no * GROUPS + g)
                    for t in range(g * GT, (g + 1) * GT):
                        act.activation(M.XN[:, t, :], X[:, t, :], ACT.Identity, bias=SHIFT[:, t:t + 1],
                                       scale=RSTD[:, t:t + 1]).then_inc(s_norm, 1)
                    for k in range(KC):
                        act.wait_ge(M.xt, (M.n * GROUPS + g) * KC + k + 1)
                        act.copy(M.XT[:, k, g * GTOK:(g + 1) * GTOK], B[k][:, :]).then_inc(M.xtc, 1)
                    act.wait_ge(M.lg, M.n * GROUPS + g + 1)
                    if g:
                        act.wait_ge(M.lgt, M.n * TILES + g * GT)
                    act.copy(M.LGT[0:M.logits, :], B[2][0:M.logits, :]).then_inc(M.lgc, 1)

            def shared(M):
                act.wait_ge(M.shw, 16 * (M.n + 1))
                act.copy(M.SHHI[:, :], M.SHRAW[:, :]).then_inc(M.shsplit, 1)
                for g in range(GROUPS):
                    if g:
                        act.wait_ge(M.shh, M.chunk0 + g * M.shc)
                    act.wait_ge(M.xtc, KC * GROUPS * (M.n + 1))
                    act.copy(M.XSHI[:, :, :], M.XT[:, :, g * GTOK:(g + 1) * GTOK]).then_inc(M.shx, 1)
                    for c in range(M.shc):
                        n = g * M.shc + c
                        act.wait_ge(M.shh, M.chunk0 + n + 1)
                        if n >= 2:
                            act.wait_ge(M.shu, M.chunk0 + n - 1)
                        act.activation(M.SSIL[:, n % 2, :], B[2 * (n % 2)][:, :], ACT.Silu).then_inc(M.shs, 1)
                        act.wait_ge(M.shu, M.chunk0 + n + 1)
                        if g:
                            act.wait_ge(M.shy, M.n * TILES + g * GT)
                        act.copy(M.SGHI[:, c, :], M.SU[:, n % 2, :]).then_inc(M.shg, 1)

            def split_hi(M, experts):
                for e in experts:
                    act.wait_ge(M.raw[e], 16 * (M.n + 1))
                    act.copy(M.WHI[:, e, :], M.WRAW[e][:, :]).then_inc(M.split, 1)

            def slots(M):
                def hi(i, j):
                    act.wait_ge(M.p_xt, i + (M.slot0 + 1))
                    if at_least(i, 2):
                        act.wait_ge(M.p_h, i + (M.slot0 - 1))
                    act.copy(M.XHI[:, j % 2, :], B[j % 2][:, 0:D]).then_inc(M.a_xhi, 1)

                def sil(i, j):
                    act.wait_ge(M.p_h, i + (M.slot0 + 1))
                    if at_least(i, 2):
                        act.wait_ge(M.d_g, i + (M.slot0 - 1))
                    act.activation(M.SIL[:, j % 2, :], B[2 + j % 2][:, 0:M.hid], ACT.Silu).then_inc(M.a_sil, 1)

                def ghi(i, j):
                    act.wait_ge(M.p_gt, i + (M.slot0 + 1))
                    if at_least(i, 2):
                        act.wait_ge(M.p_y, i + (M.slot0 - 1))
                    act.copy(M.GHI[:, j % 2, :], B[4 + j % 2][:, 0:M.hchunks * P]).then_inc(M.a_ghi, 1)

                def y(i, j):
                    act.wait_ge(M.p_y, i + (M.slot0 + 1))
                    if at_least(i, 4):
                        if isinstance(i, int):
                            act.wait_ge(M.st[j % 4], 16 * ((i + M.slot0) // 4))
                        else:
                            act.wait_ge(M.st[j % 4], (i - j) * 4 + 4 * M.slot0)
                    act.copy(M.YS[:, j % 4, :], B[6 + j % 2][:, 0:D]).then_inc(M.a_y, 1)

                def step(i, j):
                    run_stages(i, j, M.slots, ((2, hi), (1, sil), (0, ghi), (-1, y)))

                slot_loop(act, M.slots, step, 2, 1)

            norm_and_gate(L0)
            act.wait_ge(L0.shifted, 1)
            act.activation(L0.R[0][:, :, :], L0.R[0][:, :, :], ACT.Exp).then_inc(L0.exped, 1)
            shared(L0)
            act.wait_ge(L0.shadd, TILES)
            act.wait_ge(L0.shg, GROUPS * SHC0)
            split_hi(L0, range(EARLY0))
            slots(L0)
            for n in range(GROUPS):
                act.wait_ge(k_kvc, n + 1)
                for half, which in ((0, 0), (64, 1)):
                    s = slice(half, half + 64)
                    act.copy(KB[s, n * GT:(n + 1) * GT, which, :],
                             B[n][s, :].rearrange("p (t n) -> p t n", n=P)).then_inc(k_kvcc, 1)
            act.wait_ge(k_raw, 16)
            act.copy(AHI[:, :, 1:3, :], ARAW[:, :, 1:3, :]).then_inc(k_ahi, 1)
            for n in range(2):
                act.wait_ge(k_a, n + 1)
                act.copy(AHI[:, 4 * n:4 * n + 4, 0, :], B[n][0:QC, :].rearrange("p (h n) -> p h n", n=P))\
                    .then_inc(k_ahi, 1)
            for n in range(4):
                act.wait_ge(k_b, n + 1)
                act.copy(BHI[:, 2 * n:2 * n + 2, :], B[2 + n][:, :].rearrange("p (h n) -> p h n", n=D))\
                    .then_inc(k_bhi, 1)
            for g in range(GROUPS):
                sqrt_group(3 * GROUPS + g)

            def norm_pair(v, par):
                if at_least(v, 2):
                    act.wait_ge(t_xt, v - 1)
                for o in range(2):
                    at = v * 2 + o
                    act.activation(XNG[:, par, o, :], X[:, bass.ds(at, 1), :].rearrange("p o d -> p (o d)"), ACT.Identity,
                                   bias=SHIFT[:, bass.ds(at, 1)], scale=RSTD[:, bass.ds(at, 1)]).then_inc(t_norm, 1)

            def copy_xt(v, par):
                act.wait_ge(t_xt, v + 1)
                if at_least(v, 1):
                    act.wait_ge(t_qc, v)
                act.copy(XTG[:, :, :], B[7][:, :].rearrange("p (k n) -> p k n", k=KC)).then_inc(t_xtc, 1)

            def qc_hi(v, par):
                act.wait_ge(t_qc, v + 1)
                if at_least(v, 1):
                    act.wait_ge(t_rv, v * PAIRS)
                act.copy(QCHI[:, :], B[6][0:QC, 0:2 * P]).then_inc(t_qchi, 1)

            def absorbed(p):
                def stage(v, par):
                    act.wait_ge(t_abs, v * PAIRS + (p + 1))
                    if at_least(v, 2):
                        act.wait_ge(t_s, v * 4 - 4)
                    for half, head in ((0, 2 * p), (64, 2 * p + 1)):
                        s = slice(half, half + 64)
                        act.copy(Q[s, par, head, :], B[6][s, 0:2 * P]).then_inc(t_absc, 1)
                return stage

            def copy_pt(i, r, u, o):
                for n in range(2):
                    act.wait_ge(t_pt, i * 2 + (n + 1))
                    if at_least(i, 1):
                        act.wait_ge(t_ct, i * 2)
                    act.copy(PT[:, 4 * n:4 * n + 4, :], B[2 + n][:, :].rearrange("p (h n) -> p h n", n=P))\
                        .then_inc(t_ptc, 1)

            def scale_out(i, r, u, o):
                act.wait_ge(t_o, i + 1)
                if at_least(i, 2):
                    act.wait_ge(t_x, i - 1)
                act.activation(OX[:, r % 2, :], B[6][:, 2 * P:], ACT.Copy, scale=PAR[:, TX + 1:TX + 2]).then_inc(t_oc, 1)

            def exp(i, r, u, o):
                act.wait_ge(t_sub, i + 1)
                act.activation(SM[:, r % 2, :, :], SM[:, r % 2, :, :], ACT.Exp, scale=SM_SCALE).then_inc(t_exp, 1)

            def ct_hi(i, r, u, o):
                for b in range(2):
                    act.wait_ge(t_ct, i * 2 + (b + 1))
                    if at_least(i, 1):
                        act.wait_ge(t_o, i)
                    act.copy(CTHI[:, :, b * 64:(b + 1) * 64], B[4 + b][:, :].rearrange("p (h n) -> p h n", n=64))\
                        .then_inc(t_cthi, 1)

            def step(i, j, h):
                if j % 2:
                    pair(i, j, h, 3, copy_xt)
                    pair(i, j, h, 3, qc_hi)
                    tile(i, j, h, 0, copy_pt)
                    pair(i, j, h, 3, absorbed(0))
                    tile(i, j, h, -1, scale_out)
                    tile(i, j, h, 1, exp)
                    pair(i, j, h, 3, absorbed(1))
                    tile(i, j, h, 0, ct_hi)
                    pair(i, j, h, 3, absorbed(2))
                    pair(i, j, h, 3, absorbed(3))
                else:
                    pair(i, j, h, 2, absorbed(4))
                    tile(i, j, h, 0, copy_pt)
                    pair(i, j, h, 2, absorbed(5))
                    tile(i, j, h, -1, scale_out)
                    tile(i, j, h, 1, exp)
                    pair(i, j, h, 2, absorbed(6))
                    tile(i, j, h, 0, ct_hi)
                    pair(i, j, h, 2, absorbed(7))
                    pair(i, j, h, 4, norm_pair)

            tile_loop(act, step)
            act.wait_ge(t_x, TILES)
            norm_and_gate(L1)
            act.wait_ge(L1.shifted, 1)
            act.activation(SGATE[:, :], L1.R[0][:, :, E1], ACT.Sigmoid).then_inc(L1.exped, 1)
            act.wait_ge(L1.shifted, 2)
            act.activation(SMALL[:, 6, :], SMALL[:, 5, :], ACT.Exp).then_inc(L1.exped, 1)
            shared(L1)
            split_hi(L1, range(E1))
            slots(L1)

        @block.tensor
        def _(pe):
            def three_passes(out, operands, first=True, last=True):
                passes = [(x, w) for xh, xl, wh, wl in operands for x, w in ((xh, wh), (xh, wl), (xl, wh))]
                for n, (x, w) in enumerate(passes):
                    mm = pe.matmul(out, x, w, start=(n == 0), stop=(n == len(passes) - 1))
                return mm

            def gate(M):
                pe.wait_ge(M.wg, 16 * (M.n + 1))
                for g in range(GROUPS):
                    for k in range(KC):
                        if g:
                            pe.wait_ge(M.xtc, (M.n * GROUPS + g - 1) * KC + k + 1)
                        for t in range(GT):
                            pe.wait_ge(s_norm, M.norm_base + g * GT + t + 1)
                            tr = pe.transpose(B[k][:, t * P:(t + 1) * P], M.XN[:, g * GT + t, k * P:(k + 1) * P], ident)
                        tr.then_inc(M.xt, 1)
                    if g:
                        pe.wait_ge(M.lgc, M.n * GROUPS + g)
                    pe.wait_ge(M.xtc, (M.n * GROUPS + g + 1) * KC)
                    for k in range(KC):
                        mm = pe.matmul(B[2][0:M.logits, :], M.WG[:, k, :], M.XT[:, k, g * GTOK:(g + 1) * GTOK],
                                       start=(k == 0), stop=(k == KC - 1))
                    mm.then_inc(M.lg, 1)
                    pe.wait_ge(M.lgc, M.n * GROUPS + g + 1)
                    for t in range(GT):
                        at = (g * GT + t) * 16
                        pe.transpose(B[3][:, at:at + M.logits], M.LGT[0:M.logits, t * P:(t + 1) * P],
                                     C[0:M.logits, 0:M.logits]).then_inc(M.lgt, 1)

            def counts(M):
                pe.wait_ge(M.sel, 1)
                pe.matmul(B[4][:, 0:256], TRI[:, :], SEL[:, :, :].rearrange("p t e -> p (t e)"), start=True, stop=True)
                pe.matmul(B[5][:, 0:256], ONES[:, :], SEL[:, :, :].rearrange("p t e -> p (t e)"),
                          start=True, stop=True).then_inc(M.counts, 1)

            def shared(M):
                pe.wait_ge(M.shsplit, 2 * (M.n + 1))
                pe.wait_ge(M.routed, 1)
                SH, n13 = M.sh, KC * M.sh
                w1 = [s[:, 0:n13].rearrange("p (k n) -> p k n", k=KC) for s in (M.SHHI, M.SHLO)]
                w3 = [s[:, n13:2 * n13].rearrange("p (k n) -> p k n", k=KC) for s in (M.SHHI, M.SHLO)]
                w2 = [s[:, 2 * n13:].rearrange("p (c n) -> p c n", c=M.shc) for s in (M.SHHI, M.SHLO)]
                for g in range(GROUPS):
                    pe.wait_ge(M.shx, 2 * (M.n * GROUPS + g + 1))
                    for c in range(M.shc):
                        n = g * M.shc + c
                        if n >= 2:
                            pe.wait_ge(M.shu, M.chunk0 + n - 1)
                        for w, bank in ((w1, B[2 * (n % 2)]), (w3, B[2 * (n % 2) + 1])):
                            mm = three_passes(bank[:, :], [(w[0][:, k, c * P:(c + 1) * P], w[1][:, k, c * P:(c + 1) * P],
                                                            M.XSHI[:, k, :], M.XSLO[:, k, :]) for k in range(KC)])
                        mm.then_inc(M.shh, 1)
                    pe.wait_ge(M.shl, M.chunk0 + (g + 1) * M.shc)
                    for t in range(GT):
                        n = g * GT + t
                        if n >= 2:
                            pe.wait_ge(M.shadd, M.n * TILES + n - 1)
                        s = slice(t * P, (t + 1) * P)
                        three_passes(B[4 + n % 2][:, 0:D], [(M.SGHI[:, c, s], M.SGLO[:, c, s], w2[0][:, c, :], w2[1][:, c, :])
                                                            for c in range(M.shc)]).then_inc(M.shy, 1)

            def slots(M):
                whi = M.WHI[:, :, :].rearrange("p e c -> p (e c)")
                wlo = M.WLO[:, :, :].rearrange("p e c -> p (e c)")

                def expert(i):
                    return pe.value_load(EID[0:1, bass.ds(i, 1)], min_val=0, max_val=M.E - 1)

                def xt(i, j):
                    if isinstance(i, int):
                        pe.wait_ge(M.xl[j % 4], 16 * ((i + M.slot0) // 4 + 1))
                    else:
                        pe.wait_ge(M.xl[j % 4], (i - j) * 4 + (4 * M.slot0 + 16))
                    if at_least(i, 2):
                        pe.wait_ge(M.d_xlo, i + (M.slot0 - 1))
                    for k in range(KC):
                        tr = pe.transpose(B[j % 2][:, k * P:(k + 1) * P], M.XS[:, j % 4, k * P:(k + 1) * P], ident)
                    tr.then_inc(M.p_xt, 1)

                def hidden(i, j):
                    e = expert(i)
                    pe.wait_ge(M.wready, e + (M.expert0 + 1))
                    pe.wait_ge(M.d_xlo, i + (M.slot0 + 1))
                    if at_least(i, 2):
                        pe.wait_ge(M.d_g, i + (M.slot0 - 1))
                    ops = []
                    for k in range(KC):
                        at = bass.ds(e * M.cols + k * M.w13, M.w13)
                        s = slice(k * P, (k + 1) * P)
                        ops.append((M.XHI[:, j % 2, s], M.XLO[:, j % 2, s], whi[:, at], wlo[:, at]))
                    three_passes(B[2 + j % 2][:, 0:M.w13], ops).then_inc(M.p_h, 1)

                def gt(i, j):
                    pe.wait_ge(M.d_g, i + (M.slot0 + 1))
                    if at_least(i, 2):
                        pe.wait_ge(M.d_glo, i + (M.slot0 - 1))
                    for c in range(M.hchunks):
                        tr = pe.transpose(B[4 + j % 2][:, c * P:(c + 1) * P], M.G[:, j % 2, c * P:(c + 1) * P], ident)
                    tr.then_inc(M.p_gt, 1)

                def y(i, j):
                    e = expert(i)
                    pe.wait_ge(M.d_glo, i + (M.slot0 + 1))
                    if at_least(i, 2):
                        pe.wait_ge(M.a_y, i + (M.slot0 - 1))
                    ops = []
                    for c in range(M.hchunks):
                        at = bass.ds(e * M.cols + KC * M.w13 + c * D, D)
                        s = slice(c * P, (c + 1) * P)
                        ops.append((M.GHI[:, j % 2, s], M.GLO[:, j % 2, s], whi[:, at], wlo[:, at]))
                    three_passes(B[6 + j % 2][:, 0:D], ops).then_inc(M.p_y, 1)

                def step(i, j):
                    run_stages(i, j, M.slots, ((2, xt), (1, hidden), (0, gt), (-1, y)))

                slot_loop(pe, M.slots, step, 2, 1)

            pe.wait_ge(s_const, 16)
            pe.wait_ge(s_wio, 16 * 6)
            pe.wait_ge(s_csum, KC)
            for j in range(KC):
                for k in range(KC):
                    mm = pe.matmul(B[0][:, j * BATCH:(j + 1) * BATCH], WIN[:, k, j * P:(j + 1) * P], CSUM[:, k, :],
                                   start=(k == 0), stop=(k == KC - 1))
            mm.then_inc(s_m1, 1)
            pe.wait_ge(s_m1t, KC)
            for j in range(KC):
                mm = pe.matmul(B[1][0:BATCH, 0:D], M1T[:, j, :], WOUT[:, j, :], start=(j == 0), stop=(j == KC - 1))
            mm.then_inc(s_summ, 1)
            pe.wait_ge(s_summc, 1)
            for t in range(TILES):
                if t >= 6:
                    pe.wait_ge(s_spused, t - 5)
                pe.matmul(B[2 + t % 6][:, 0:D], SELB[:, t * P:(t + 1) * P],
                          SUMM[:, :], start=True, stop=True).then_inc(s_spread, 1)
            pe.wait_ge(s_spused, TILES)
            gate(L0)
            counts(L0)
            shared(L0)
            pe.wait_ge(L0.shadd, TILES)
            pe.wait_ge(L0.eid, 1)
            slots(L0)
            pe.wait_ge(k_wkv, 16 * 4)
            pe.wait_ge(k_ctx, 16 * KC)
            pe.wait_ge(L0.a_y, SLOTS0)
            for n in range(GROUPS):
                for k in range(KC):
                    mm = pe.matmul(B[n][:, :], WKVC[:, k, :], CTX1[:, k, n * GTOK:(n + 1) * GTOK],
                                   start=(k == 0), stop=(k == KC - 1))
                mm.then_inc(k_kvc, 1)
            for n in range(GROUPS):
                for t in range(GT):
                    for k in range(KC):
                        at = (n * GT + t) * P
                        mm = pe.matmul(B[4 + n][:, t * P:(t + 1) * P], CTX1[:, k, at:at + P], WKVC[:, k, :],
                                       start=(k == 0), stop=(k == KC - 1))
                mm.then_inc(k_tok, 1)
            for n in range(GROUPS):
                pe.wait_ge(k_kvcc, 2 * (n + 1))
                kv = KB[0:KVC, n * GT:(n + 1) * GT, 0, :]
                pe.matmul(B[n][:, :], WKR[:, 0, :], kv, start=True, stop=True)
                pe.wait_ge(k_tokc, 4 * (n + 1))
                pe.matmul(B[4 + n][:, :], WKR[:, 1, :], kv, start=True, stop=True).then_inc(k_rope, 1)
            pe.wait_ge(k_up, 16 * 4)
            for n in range(2):
                pe.wait_ge(k_ropem, 2 * (n + 1))
                for h in range(8):
                    mm = pe.matmul(B[n][0:QC, h * KVC:(h + 1) * KVC], UQT[:, 8 * n + h, :], UKT[:, 8 * n + h, :],
                                   start=True, stop=True)
                mm.then_inc(k_a, 1)
            pe.wait_ge(k_ropem, 2 * GROUPS)
            for n in range(4):
                for h in range(4):
                    half = h % 2 * 64
                    mm = pe.matmul(B[2 + n][half:half + 64, h // 2 * D:(h // 2 + 1) * D], UVT[:, 4 * n + h, :],
                                   WO[:, 4 * n + h, :], start=True, stop=True)
                mm.then_inc(k_b, 1)
            pe.wait_ge(k_alo, 3)
            pe.wait_ge(k_blo, 4)

            def transpose_pair(v, par):
                pe.wait_ge(t_norm, v * 2 + 2)
                if at_least(v, 1):
                    pe.wait_ge(t_rvm, v * 2 * PAIRS)
                for k in range(KC):
                    for o in range(2):
                        tr = pe.transpose(B[7][:, (2 * k + o) * P:(2 * k + o + 1) * P],
                                          XNG[:, par, o, k * P:(k + 1) * P], ident)
                tr.then_inc(t_xt, 1)

            def down(v, par):
                pe.wait_ge(t_xtc, v + 1)
                if at_least(v, 1):
                    pe.wait_ge(t_absc, v * 2 * PAIRS)
                if at_least(v, 3):
                    pe.wait_ge(t_oc, v * 2 - 4)
                for k in range(KC):
                    mm = pe.matmul(B[6][0:QC, 0:2 * P], WDQ[:, k, :], XTG[:, k, :], start=(k == 0), stop=(k == KC - 1))
                mm.then_inc(t_qc, 1)

            def up(p, outs):
                def stage(v, par):
                    pe.wait_ge(t_qclo, v + 1)
                    if not (isinstance(v, int) and v == 0 and p == 0):
                        pe.wait_ge(t_absc, v * 2 * PAIRS + 2 * p)
                        pe.wait_ge(t_rvm, v * 2 * PAIRS + 2 * p)
                    n = v * 2 + outs
                    if not isinstance(v, int) or n > 0:
                        pe.wait_ge(t_oc, n)
                    three_passes(B[6][:, 0:2 * P], [(AHI[:, p, 0, :], ALO[:, p, 0, :], QCHI[:, :], QCLO[:, :])])\
                        .then_inc(t_abs, 1)
                    for w in (1, 2):
                        mm = three_passes(B[7][:, (w - 1) * 2 * P:w * 2 * P],
                                          [(AHI[:, p, w, :], ALO[:, p, w, :], QCHI[:, :], QCLO[:, :])])
                    mm.then_inc(t_rv, 1)
                return stage

            def score(i, r, u, o):
                pe.wait_ge(t_absc, u * 2 * PAIRS + 2 * PAIRS)
                pe.wait_ge(t_q, u * 2 * PAIRS + 2 * PAIRS)
                pe.wait_ge(t_kl[r], 16 * (i // 4 + 1) if isinstance(i, int) else (i - r) * 4 + 16)
                if at_least(i, 1):
                    pe.wait_ge(t_masked, i * 2)
                for head in range(HEADS):
                    for b in range(2):
                        mm = pe.matmul(B[head // 8][b * 64:(b + 1) * 64, head % 8 * SEQ:(head % 8 + 1) * SEQ],
                                       Q[:, r // 2, head, o * P + b * 64:o * P + (b + 1) * 64],
                                       KR[:, r, head % 2, b * SEQ:(b + 1) * SEQ], start=True, stop=True)
                    if head % 8 == 7:
                        mm.then_inc(t_s, 1)

            def probs_t(i, r, u, o):
                pe.wait_ge(t_prob, i + 1)
                if at_least(i, 1):
                    pe.wait_ge(t_ptc, i * 2)
                for n in range(2):
                    for h in range(4):
                        tr = pe.transpose(B[2 + n][:, h * P:(h + 1) * P],
                                          SM[:, r % 2, 8 * n + 2 * h:8 * n + 2 * h + 2, :].rearrange("p h n -> p (h n)"),
                                          ident)
                    tr.then_inc(t_pt, 1)

            def context(i, r, u, o):
                pe.wait_ge(t_ptc, i * 2 + 2)
                if at_least(i, 1):
                    pe.wait_ge(t_ctlo, i * 2)
                for b in range(2):
                    pe.matmul(B[4 + b][:, :], KR[:, r, 2 + b, :], PT[:, :, b * 64:(b + 1) * 64], start=True, stop=True)\
                        .then_inc(t_ct, 1)

            def out(i, r, u, o):
                pe.wait_ge(t_ctlo, i * 2 + 2)
                if at_least(i, 1):
                    pe.wait_ge(t_oc, i)
                copied = u * 2 * PAIRS + (34 if o == 0 else 44)
                pe.wait_ge(t_absc, min(copied, TILES * PAIRS) if isinstance(i, int) else copied)
                three_passes(B[6][:, 2 * P:], [(CTHI[:, p, :], CTLO[:, p, :], BHI[:, p, :], BLO[:, p, :])
                                               for p in range(PAIRS)]).then_inc(t_o, 1)

            def step(i, j, h):
                if j % 2:
                    pair(i, j, h, 3, transpose_pair)
                    tile(i, j, h, 1, score)
                    pair(i, j, h, 3, down)
                    tile(i, j, h, 0, probs_t)
                    pair(i, j, h, 3, up(0, -4))
                    tile(i, j, h, -1, out)
                    pair(i, j, h, 3, up(1, -3))
                    tile(i, j, h, 0, context)
                    pair(i, j, h, 3, up(2, -3))
                    pair(i, j, h, 3, up(3, -3))
                else:
                    tile(i, j, h, 1, score)
                    pair(i, j, h, 2, up(4, -3))
                    tile(i, j, h, 0, probs_t)
                    pair(i, j, h, 2, up(5, -3))
                    tile(i, j, h, -1, out)
                    pair(i, j, h, 2, up(6, -2))
                    tile(i, j, h, 0, context)
                    pair(i, j, h, 2, up(7, -2))

            tile_loop(pe, step)
            gate(L1)
            counts(L1)
            shared(L1)
            pe.wait_ge(L1.shadd, 2 * TILES)
            pe.wait_ge(L1.eid, 1)
            slots(L1)

        @block.vector
        def _(dve):
            ch = Count(dve, s_dve)
            mk = ch.mark

            def stats(src, g):
                for t in range(g * GT, (g + 1) * GT):
                    mk(dve.bn_stats(STAT[:, t, :], src[:, t, :]))
                ch.wait()
                for t in range(g * GT, (g + 1) * GT):
                    mk(dve.bn_aggr(MV[:, t, :], STAT[:, t, :]))
                ch.wait()
                dve.tensor_scalar(SD[:, g * GT:(g + 1) * GT], MV[:, g * GT:(g + 1) * GT, 1], LN_EPS, None,
                                  ALU.add).then_inc(s_var, 1)

            def rstd(n, g):
                s = slice(g * GT, (g + 1) * GT)
                dve.wait_ge(s_sd, n * GROUPS + g + 1)
                mk(dve.reciprocal(RSTD[:, s], SD[:, s]))
                ch.wait()
                dve.scalar_tensor_tensor(out=SHIFT[:, s], in0=MV[:, s, 0], scalar=-1.0, in1=RSTD[:, s],
                                         op0=ALU.mult, op1=ALU.mult).then_inc(s_rstd, 1)

            def route(M, SC, weights):
                E, TOP, R = M.E, M.top, M.R
                for t in range(TILES):
                    mk(dve.max(TOPW[:, t, :], SC[:, t, :]))
                ch.wait()
                for t in range(TILES):
                    mk(dve.max_index(TOPI[:, t, :], TOPW[:, t, :], SC[:, t, :]))
                ch.wait()
                IDX = R[5][:, 0:8, :].rearrange("p a b -> p (a b)").rearrange("p (t k) -> p t k", k=8)
                mk(dve.tensor_copy(IDX, TOPI[:, :, :]))
                weights()
                ch.wait()
                eid = const("expert_id")[:, 0:E].unsqueeze(1).to_broadcast([P, TILES, E])
                OH = [R[i][:, :, 0:E] for i in range(TOP)]
                for k in range(TOP):
                    mk(dve.tensor_tensor(OH[k], IDX[:, :, k:k + 1].to_broadcast([P, TILES, E]), eid, ALU.is_equal))
                ch.wait()
                acc = R[4][:, :, 0:E]
                mk(dve.tensor_tensor(acc, OH[0], OH[1], ALU.add))
                for k in range(2, TOP):
                    ch.wait()
                    mk(dve.tensor_tensor(acc, acc, OH[k], ALU.add))
                ch.wait()
                dve.tensor_copy(SEL[:, :, 0:E], acc).then_inc(M.sel, 1)
                dve.wait_ge(M.counts, 1)
                CNT = R[5][:, :, :].rearrange("p a b -> p (a b)")[:, 0:E * TILES].rearrange("p (e t) -> p e t", t=TILES)
                INC = R[6][:, :, :].rearrange("p a b -> p (a b)")[:, 0:E * TILES].rearrange("p (e t) -> p e t", t=TILES)
                mk(dve.tensor_copy(CNT, B[5][:, 0:256].rearrange("p (t e) -> p e t", e=16)[:, 0:E, :]))
                ch.wait()
                mk(dve.tensor_tensor_scan(INC.rearrange("p e t -> p (e t)"), const("keep")[:, 0:E * TILES],
                                          CNT.rearrange("p e t -> p (e t)"), 0.0, ALU.mult, ALU.add))
                ch.wait()
                n, cum, base = SMALL[:, 0, 0:E], SMALL[:, 1, 0:E], SMALL[:, 2, 0:E]
                mk(dve.tensor_scalar(SMALLI[:, 0:E], INC[:, :, TILES - 1], float(P - 1), None, ALU.add))
                ch.wait()
                mk(dve.tensor_scalar(SMALLI[:, 0:E], SMALLI[:, 0:E], 7, None, ALU.arith_shift_right))
                ch.wait()
                mk(dve.tensor_copy(n, SMALLI[:, 0:E]))
                ch.wait()
                mk(dve.tensor_tensor_scan(cum, ONE64[:, 0:E], n, 0.0, ALU.mult, ALU.add))
                ch.wait()
                mk(dve.tensor_tensor(base, cum, n, ALU.subtract))
                ch.wait()
                mk(dve.tensor_scalar(base, base, float(P), None, ALU.mult))
                mk(dve.tensor_tensor(INC, INC, CNT, ALU.subtract))
                ch.wait()
                POS = R[7][:, :, 0:E]
                mk(dve.tensor_tensor(POS, INC.rearrange("p e t -> p t e"), base.unsqueeze(1).to_broadcast([P, TILES, E]),
                                     ALU.add))
                ch.wait()
                dve.tensor_tensor(POS, POS, B[4][:, 0:256].rearrange("p (t e) -> p t e", e=16)[:, :, 0:E], ALU.add)\
                    .then_inc(M.routed, 1)
                dve.wait_ge(M.routed, 1)
                for k in range(TOP):
                    mk(dve.tensor_tensor(OH[k], OH[k], POS, ALU.mult))
                ch.wait()
                PK = R[4][:, 0:4, :]
                for k in range(TOP):
                    mk(dve.tensor_reduce(PK[:, k, :], OH[k], AX.X, ALU.add))
                ch.wait()
                dve.tensor_copy(POSI[:, 0:TOP, :], PK[:, 0:TOP, :]).then_inc(M.pos, 1)
                slots = M.slots
                CMP = M.XCMP[0:1, 0:slots * E].rearrange("p (s e) -> p s e", e=E)
                mk(dve.tensor_tensor(CMP, cum[0:1, :].unsqueeze(1).to_broadcast([1, slots, E]),
                                     const("slot_id")[0:1, 0:slots].unsqueeze(2).to_broadcast([1, slots, E]), ALU.is_le))
                ch.wait()
                row = M.XCMP[0:1, slots * E:slots * E + slots]
                mk(dve.tensor_reduce(row, CMP, AX.X, ALU.add))
                ch.wait()
                dve.tensor_scalar(EID[0:1, 0:slots], row, float(E - 1), None, ALU.min).then_inc(M.eid, 1)

            def shared(M, scale):
                dve.wait_ge(M.shsplit, 2 * M.n + 1)
                dve.tensor_tensor(M.SHLO[:, :], M.SHRAW[:, :], M.SHHI[:, :].bitcast(F32), ALU.subtract)\
                    .then_inc(M.shsplit, 1)
                for g in range(GROUPS):
                    dve.wait_ge(M.shx, 2 * (M.n * GROUPS + g) + 1)
                    dve.tensor_tensor(M.XSLO[:, :, :], M.XT[:, :, g * GTOK:(g + 1) * GTOK], M.XSHI[:, :, :].bitcast(F32),
                                      ALU.subtract).then_inc(M.shx, 1)
                    for c in range(M.shc):
                        n = g * M.shc + c
                        dve.wait_ge(M.shs, M.chunk0 + n + 1)
                        if n >= 2:
                            dve.wait_ge(M.shl, M.chunk0 + n - 1)
                            dve.wait_ge(M.shg, M.chunk0 + n - 1)
                        dve.tensor_tensor(M.SU[:, n % 2, :], M.SSIL[:, n % 2, :], B[2 * (n % 2) + 1][:, :], ALU.mult)\
                            .then_inc(M.shu, 1)
                        dve.wait_ge(M.shg, M.chunk0 + n + 1)
                        dve.wait_ge(M.shu, M.chunk0 + n + 1)
                        dve.tensor_tensor(M.SGLO[:, c, :], M.SU[:, n % 2, :], M.SGHI[:, c, :].bitcast(F32), ALU.subtract)\
                            .then_inc(M.shl, 1)
                    for t in range(g * GT, (g + 1) * GT):
                        dve.wait_ge(M.shy, M.n * TILES + t + 1)
                        dve.scalar_tensor_tensor(out=X[:, t, :], in0=B[4 + t % 2][:, 0:D], scalar=scale(t),
                                                 in1=X[:, t, :], op0=ALU.mult, op1=ALU.add).then_inc(M.shadd, 1)

            def split_lo(M, experts):
                for e in experts:
                    dve.wait_ge(M.split, (EARLY0 if M.n else 0) + e + 1)
                    dve.tensor_tensor(M.WLO[:, e, :], M.WRAW[e][:, :], M.WHI[:, e, :].bitcast(F32), ALU.subtract)\
                        .then_inc(M.wready, 1)

            def slots(M):
                def lo(i, j):
                    dve.wait_ge(M.a_xhi, i + (M.slot0 + 1))
                    dve.tensor_tensor(M.XLO[:, j % 2, :], B[j % 2][:, 0:D], M.XHI[:, j % 2, :].bitcast(F32), ALU.subtract)\
                        .then_inc(M.d_xlo, 1)

                def g_(i, j):
                    dve.wait_ge(M.a_sil, i + (M.slot0 + 1))
                    if at_least(i, 2):
                        dve.wait_ge(M.p_gt, i + (M.slot0 - 1))
                    dve.tensor_tensor(M.G[:, j % 2, 0:M.hid], M.SIL[:, j % 2, :], B[2 + j % 2][:, M.hid:M.w13], ALU.mult)\
                        .then_inc(M.d_g, 1)

                def glo(i, j):
                    dve.wait_ge(M.a_ghi, i + (M.slot0 + 1))
                    dve.tensor_tensor(M.GLO[:, j % 2, :], B[4 + j % 2][:, 0:M.hchunks * P], M.GHI[:, j % 2, :].bitcast(F32),
                                      ALU.subtract).then_inc(M.d_glo, 1)

                def step(i, j):
                    run_stages(i, j, M.slots, ((2, lo), (1, g_), (0, glo)))

                slot_loop(dve, M.slots, step, 2, 1)

            def combine(M):
                for t in range(TILES):
                    for k in range(M.top):
                        n = M.copy0 + t * M.top + k
                        dve.wait_ge(M.gath[n % 8], 16 * (n // 8 + 1))
                        if n:
                            dve.wait_ge(M.comb, n)
                        dve.scalar_tensor_tensor(out=X[:, t, :], in0=M.GB[:, n % 8, :], scalar=WK[:, k, t:t + 1],
                                                 in1=X[:, t, :], op0=ALU.mult, op1=ALU.add).then_inc(M.comb, 1)

            mk(dve.memset(ONES[:, :], 1.0))
            mk(dve.memset(SEL[:, :, :], 0.0))
            dve.wait_ge(s_const, 16)
            mk(dve.tensor_copy(TRI[:, :], const("before")))
            for g in range(GROUPS):
                dve.wait_ge(s_x[g], 16)
                stats(X, g)
            for g in range(GROUPS):
                rstd(0, g)
            dve.wait_ge(s_act, 3)
            dve.wait_ge(s_zero, 2)
            mk(dve.tensor_tensor_scan(EMA[:, :], PAR[:, KEEP:KEEP + 1].to_broadcast([P, SEQ]), ONE64[:, :], 0.0,
                                      ALU.mult, ALU.add))
            ch.wait()
            mk(dve.tensor_scalar(EMAC[:, :], EMA[:, SEQ - 1::-1], 1.0 / SEQ, None, ALU.mult))
            ch.wait()
            mk(dve.tensor_reduce(PAR[:, CTOT:CTOT + 1], EMAC[:, :], AX.X, ALU.add))
            ch.wait()
            mk(dve.tensor_scalar(PAR[:, BC:BC + KC], BIN[:, :], PAR[:, CTOT:CTOT + 1], None, ALU.mult))
            for k in range(KC):
                dve.wait_ge(s_ctx[k], 16)
                ch.wait()
                if k:
                    dve.wait_ge(s_csum, k)
                mk(dve.tensor_tensor(CTXW[:, :].rearrange("p (b s) -> p b s", s=SEQ),
                                     CTX[:, k, :].rearrange("p (b s) -> p b s", s=SEQ),
                                     EMAC[:, :].unsqueeze(1).to_broadcast([P, BATCH, SEQ]), ALU.mult))
                ch.wait()
                dve.tensor_reduce(CSUM[:, k, :], CTXW[:, :].rearrange("p (b s) -> p b s", s=SEQ), AX.X, ALU.add)\
                    .then_inc(s_csum, 1)
            dve.wait_ge(s_wio, 16 * 6)
            mk(dve.tensor_scalar(GAMMA[:, :], GAMMA[:, :], PAR[:, TX:TX + 1], None, ALU.mult))
            dve.tensor_scalar(BETA[:, :], BETA[:, :], PAR[:, TX:TX + 1], None, ALU.mult).then_inc(s_beta, 1)
            dve.wait_ge(s_m1, 1)
            ch.wait()
            for j in range(KC):
                dve.tensor_scalar(M1T[:, j, :], B[0][:, j * BATCH:(j + 1) * BATCH], PAR[:, BC + j:BC + j + 1], None,
                                  ALU.add).then_inc(s_m1t, 1)
            dve.wait_ge(s_summ, 1)
            dve.tensor_tensor(SUMM[:, :], B[1][0:BATCH, 0:D], BOUT[0:BATCH, :], ALU.add).then_inc(s_summc, 1)
            for g in range(GROUPS):
                for t in range(g * GT, (g + 1) * GT):
                    dve.wait_ge(s_norm, t + 1)
                    dve.wait_ge(s_spread, t + 1)
                    dve.tensor_tensor(XN[:, t, :], XN[:, t, :], B[2 + t % 6][:, 0:D], ALU.add).then_inc(s_spused, 1)
                dve.wait_ge(s_spused, (g + 1) * GT)
                stats(XN, g)
                if g:
                    rstd(1, g - 1)
            rstd(1, GROUPS - 1)
            for g in range(GROUPS):
                for t in range(g * GT, (g + 1) * GT):
                    dve.wait_ge(s_norm, TILES + t + 1)
                    mk(dve.tensor_tensor(XN[:, t, :], XN[:, t, :], GAMMA[:, :], ALU.mult))
                ch.wait()
                for t in range(g * GT, (g + 1) * GT):
                    dve.wait_ge(s_xb, t + 1)
                    mk(dve.tensor_tensor(X[:, t, :], X[:, t, :], XN[:, t, :], ALU.add))
                ch.wait()
                stats(X, g)
                if g:
                    rstd(2, g - 1)
            rstd(2, GROUPS - 1)
            R256 = L0.R
            dve.wait_ge(L0.lgt, TILES)
            LG = B[3][:, 0:256].rearrange("p (t e) -> p t e", e=E0)
            mx, inv = SMALL[:, 0, :], SMALL[:, 1, :]
            mk(dve.tensor_reduce(mx, LG, AX.X, ALU.max))
            ch.wait()
            dve.tensor_tensor(R256[0][:, :, :], LG, mx.unsqueeze(2).to_broadcast([P, TILES, E0]), ALU.subtract)\
                .then_inc(L0.shifted, 1)
            dve.wait_ge(L0.exped, 1)
            mk(dve.tensor_reduce(mx, R256[0][:, :, :], AX.X, ALU.add))
            ch.wait()
            mk(dve.reciprocal(inv, mx))
            ch.wait()
            mk(dve.tensor_tensor(R256[1][:, :, :], R256[0][:, :, :], inv.unsqueeze(2).to_broadcast([P, TILES, E0]), ALU.mult))
            ch.wait()
            gm = SMALL[:, 2:6, :].rearrange("p a b -> p (a b)").rearrange("p (t g) -> p t g", g=EGROUPS)
            mk(dve.tensor_reduce(gm, R256[1][:, :, :].rearrange("p t (g i) -> p (t g) i", i=EPG), AX.X, ALU.max))
            ch.wait()
            R4 = R256[2][:, :, :].rearrange("p t (j i) -> p t j i", i=EGROUPS)
            mk(dve.tensor_tensor(R4, gm.unsqueeze(2).to_broadcast([P, TILES, EGROUPS, EGROUPS]),
                                 gm.unsqueeze(3).to_broadcast([P, TILES, EGROUPS, EGROUPS]), ALU.is_ge))
            ch.wait()
            mk(dve.tensor_tensor(R256[3][:, :, :], R256[2][:, :, :],
                                 const("earlier_group").unsqueeze(1).to_broadcast([P, TILES, 16]), ALU.mult))
            ch.wait()
            ra = R256[4][:, 0:4, :].rearrange("p a b -> p (a b)").rearrange("p (t g) -> p t g", g=EGROUPS)
            rb = R256[4][:, 4:8, :].rearrange("p a b -> p (a b)").rearrange("p (t g) -> p t g", g=EGROUPS)
            R4b = R256[3][:, :, :].rearrange("p t (j i) -> p t j i", i=EGROUPS)
            mk(dve.tensor_reduce(ra, R4b, AX.X, ALU.add))
            mk(dve.tensor_reduce(rb, R4b.rearrange("p t j i -> p t i j"), AX.X, ALU.add))
            ch.wait()
            mk(dve.tensor_tensor(ra, ra, rb, ALU.subtract))
            ch.wait()
            mk(dve.tensor_tensor(ra, ra, const("later_groups").unsqueeze(1).to_broadcast([P, TILES, EGROUPS]), ALU.add))
            ch.wait()
            mk(dve.tensor_scalar(ra, ra, TOPG - 0.5, None, ALU.is_lt))
            ch.wait()
            mk(dve.tensor_scalar(rb, ra, 1.0, None, ALU.subtract))
            by_group = "p t (g i) -> p (t g) i"
            mk(dve.tensor_tensor(R256[2][:, :, :].rearrange(by_group, i=EPG), R256[1][:, :, :].rearrange(by_group, i=EPG),
                                 ra.rearrange("p t g -> p (t g)").unsqueeze(2).to_broadcast([P, TILES * EGROUPS, EPG]),
                                 ALU.mult))
            ch.wait()
            mk(dve.tensor_tensor(R256[0][:, :, :].rearrange(by_group, i=EPG), R256[2][:, :, :].rearrange(by_group, i=EPG),
                                 rb.rearrange("p t g -> p (t g)").unsqueeze(2).to_broadcast([P, TILES * EGROUPS, EPG]),
                                 ALU.add))
            ch.wait()

            def weights0():
                mk(dve.tensor_scalar(WK[:, :, :], TOPW[:, :, 0:4].rearrange("p t k -> p k t"), PAR[:, TF:TF + 1], None,
                                     ALU.mult))

            route(L0, R256[0][:, :, 0:E0], weights0)
            shared(L0, lambda t: PAR[:, TF:TF + 1])
            split_lo(L0, range(EARLY0))
            dve.wait_ge(L0.scat, 16 * TILES * TOP0)
            mk(dve.memset(L0.G[:, :, :], 0.0))
            ch.wait()
            slots(L0)
            dve.wait_ge(L0.p_y, SLOTS0)
            dve.wait_ge(L0.wready, E0)
            mk(dve.memset(KB[:, :, 2:4, :], 0.0))
            dve.wait_ge(k_wkv, 16 * 4)
            mk(dve.tensor_copy(SEG[:, :], ITOK[:, :]))
            ch.wait()
            seen = XNG[:, :, :, :].rearrange("p a b d -> p (a b d)").rearrange("p (t s) -> p t s", s=SEQ)
            mk(dve.tensor_tensor(MASK[:, :, :], const("key_id").unsqueeze(1).to_broadcast([P, TILES, SEQ]),
                                 SEG[:, :].unsqueeze(2).to_broadcast([P, TILES, SEQ]), ALU.subtract))
            ch.wait()
            mk(dve.tensor_scalar(seen, MASK[:, :, :], float(-LOOKBACK), None, ALU.is_ge))
            ch.wait()
            mk(dve.tensor_scalar(MASK[:, :, :], MASK[:, :, :], 0.0, None, ALU.is_le))
            ch.wait()
            mk(dve.tensor_tensor(MASK[:, :, :], MASK[:, :, :], seen, ALU.mult))
            ch.wait()
            mk(dve.tensor_scalar(MASK[:, :, :], MASK[:, :, :], -1.0, NEG, ALU.add, ALU.mult))
            ch.wait()
            for n in range(GROUPS):
                dve.wait_ge(k_tok, n + 1)
                for b in range(2):
                    for h in range(2):
                        src = B[4 + n][b * 64:(b + 1) * 64, :].rearrange("p (t n) -> p t n", n=P)[:, :, 0:KVC]
                        dve.tensor_copy(KB[h * 64:(h + 1) * 64, n * GT:(n + 1) * GT, 2 + b, h * 64:(h + 1) * 64], src)\
                            .then_inc(k_tokc, 1)
            RC5 = RC[:, :, :].rearrange("p a n -> p (a n)")
            RS5 = RS[:, :, :].rearrange("p a n -> p (a n)")
            for n in range(GROUPS):
                dve.wait_ge(k_rope, n + 1)
                if n:
                    dve.wait_ge(k_roped, 2 * n)
                for dst, src, table in ((RC5, B[n], "cos"), (RS5, B[4 + n], "sin")):
                    dve.tensor_tensor(dst.rearrange("p (b s) -> p b s", s=SEQ), src[:, :].rearrange("p (b s) -> p b s", s=SEQ),
                                      const(table).unsqueeze(1).to_broadcast([P, 8, SEQ]), ALU.mult).then_inc(k_ropem, 1)
                dve.wait_ge(k_ropem, 2 * n + 2)
                for half, which in ((64, 0), (0, 1)):
                    s = slice(half, half + 64)
                    dve.tensor_tensor(KB[s, n * GT:(n + 1) * GT, which, :], RC5[s, :].rearrange("p (t n) -> p t n", n=P),
                                      RS5[s, :].rearrange("p (t n) -> p t n", n=P), ALU.add).then_inc(k_roped, 1)
            dve.wait_ge(k_ahi, 1)
            dve.tensor_tensor(ALO[:, :, 1:3, :], ARAW[:, :, 1:3, :], AHI[:, :, 1:3, :].bitcast(F32), ALU.subtract)\
                .then_inc(k_alo, 1)
            for n in range(2):
                dve.wait_ge(k_ahi, n + 2)
                dve.tensor_tensor(ALO[:, 4 * n:4 * n + 4, 0, :], B[n][0:QC, :].rearrange("p (h n) -> p h n", n=P),
                                  AHI[:, 4 * n:4 * n + 4, 0, :].bitcast(F32), ALU.subtract).then_inc(k_alo, 1)
            for n in range(4):
                dve.wait_ge(k_bhi, n + 1)
                dve.tensor_tensor(BLO[:, 2 * n:2 * n + 2, :], B[2 + n][:, :].rearrange("p (h n) -> p h n", n=D),
                                  BHI[:, 2 * n:2 * n + 2, :].bitcast(F32), ALU.subtract).then_inc(k_blo, 1)
            combine(L0)
            dve.wait_ge(L0.comb, TILES * TOP0)
            for g in range(GROUPS):
                stats(X, g)
            for g in range(GROUPS):
                rstd(3, g)

            def mask(i, r, u, o):
                if at_least(i, 2):
                    dve.wait_ge(t_pt, i * 2 - 2)
                for n in range(2):
                    dve.wait_ge(t_s, i * 2 + (n + 1))
                    dve.tensor_tensor(SM[:, r % 2, 8 * n:8 * n + 8, :], B[n][:, :].rearrange("p (h n) -> p h n", n=SEQ),
                                      MASK[:, bass.ds(i, 1), :].to_broadcast([P, 8, SEQ]), ALU.add).then_inc(t_masked, 1)
                dve.wait_ge(t_masked, i * 2 + 2)
                dve.tensor_reduce(SMX[:, r % 2, 0, :], SM[:, r % 2, :, :], AX.X, ALU.max).then_inc(t_max, 1)

            def row_sum(i, r, u, o):
                dve.wait_ge(t_exp, i + 1)
                dve.tensor_reduce(SMX[:, r % 2, 1, :], SM[:, r % 2, :, :], AX.X, ALU.add).then_inc(t_sum, 1)
                dve.wait_ge(t_sum, i + 1)
                dve.reciprocal(SMX[:, r % 2, 1, :], SMX[:, r % 2, 1, :]).then_inc(t_rec, 1)

            def qc_lo(v, par):
                dve.wait_ge(t_qchi, v + 1)
                dve.tensor_tensor(QCLO[:, :], B[6][0:QC, 0:2 * P], QCHI[:, :].bitcast(F32), ALU.subtract).then_inc(t_qclo, 1)

            def terms(p):
                def stage(v, par):
                    dve.wait_ge(t_rv, v * PAIRS + (p + 1))
                    if at_least(v, 1) or p >= 2:
                        dve.wait_ge(t_q, v * 2 * PAIRS + (2 * p - 2))
                    for w, dst, table in ((0, RC, "cos"), (1, RS, "sin")):
                        dve.tensor_tensor(dst[:, p % 2, :].rearrange("p (b s) -> p b s", s=SEQ),
                                          B[7][:, w * 2 * P:(w + 1) * 2 * P].rearrange("p (b s) -> p b s", s=SEQ),
                                          const(table).unsqueeze(1).to_broadcast([P, 4, SEQ]), ALU.mult).then_inc(t_rvm, 1)
                return stage

            def ct_lo(i, r, u, o):
                for b in range(2):
                    dve.wait_ge(t_cthi, i * 2 + (b + 1))
                    dve.tensor_tensor(CTLO[:, :, b * 64:(b + 1) * 64], B[4 + b][:, :].rearrange("p (h n) -> p h n", n=64),
                                      CTHI[:, :, b * 64:(b + 1) * 64].bitcast(F32), ALU.subtract).then_inc(t_ctlo, 1)

            def step(i, j, h):
                tile(i, j, h, 1, mask)
                if j % 2:
                    pair(i, j, h, 3, qc_lo)
                    pair(i, j, h, 3, terms(0))
                    pair(i, j, h, 3, terms(1))
                    tile(i, j, h, 1, row_sum)
                    tile(i, j, h, 0, ct_lo)
                    pair(i, j, h, 3, terms(2))
                    pair(i, j, h, 3, terms(3))
                else:
                    pair(i, j, h, 2, terms(4))
                    pair(i, j, h, 2, terms(5))
                    tile(i, j, h, 1, row_sum)
                    pair(i, j, h, 2, terms(6))
                    tile(i, j, h, 0, ct_lo)
                    pair(i, j, h, 2, terms(7))

            tile_loop(dve, step)
            dve.wait_ge(t_x, TILES)
            for g in range(GROUPS):
                stats(X, g)
                if g:
                    rstd(4, g - 1)
            rstd(4, GROUPS - 1)
            dve.wait_ge(L1.lgt, 2 * TILES)
            dve.tensor_copy(L1.R[0][:, :, 0:E1 + 1], B[3][:, 0:256].rearrange("p (t e) -> p t e", e=16)[:, :, 0:E1 + 1])\
                .then_inc(L1.shifted, 1)
            dve.wait_ge(L1.exped, 1)
            mk(dve.tensor_scalar(SGATE[:, :], SGATE[:, :], PAR[:, TF + 1:TF + 2], None, ALU.mult))
            ch.wait()

            def weights1():
                dve.tensor_tensor(SMALL[:, 5, :], TOPW[:, :, 1], TOPW[:, :, 0], ALU.subtract).then_inc(L1.shifted, 1)
                dve.wait_ge(L1.exped, 2)
                mk(dve.tensor_scalar(SMALL[:, 5, :], SMALL[:, 6, :], 1.0, None, ALU.add))
                ch.wait()
                mk(dve.reciprocal(SMALL[:, 5, :], SMALL[:, 5, :]))
                ch.wait()
                mk(dve.tensor_scalar(WK[:, 0, :], SMALL[:, 5, :], PAR[:, TF + 1:TF + 2], None, ALU.mult))
                ch.wait()
                mk(dve.tensor_tensor(WK[:, 1, :], WK[:, 0, :], SMALL[:, 6, :], ALU.mult))

            route(L1, L1.R[0][:, :, 0:E1], weights1)
            shared(L1, lambda t: SGATE[:, t:t + 1])
            split_lo(L1, range(E1))
            slots(L1)
            combine(L1)


def host_layout(v):
    f = {k: np.asarray(x) for k, x in v.items()}
    c, select = constants()
    o = {"const": c, "select": select}
    o["x"] = f["x"].reshape(TOKENS, D)
    o["ctxT"] = f["ctx_2048"].reshape(TOKENS, D).T
    o["decay"] = f["L0_xattn_decay"].reshape(1, 1)
    o["g_xattn"] = f["g_xattn"].reshape(1, 2)
    o["g_ffn"] = f["g_ffn"].reshape(1, 2)
    o["W_inT"] = f["L0_xattn_W_in"].T
    o["W_outT"] = f["L0_xattn_W_out"].T
    o["b_in"] = f["L0_xattn_b_in"].reshape(KC, P).T
    o["b_out"] = f["L0_xattn_b_out"].reshape(1, D)
    o["gamma"] = f["L0_xattn_gamma"].reshape(1, D)
    o["beta"] = f["L0_xattn_beta"].reshape(1, D)
    o["Wg0T"] = f["L0_ffn_Wg"].T

    def chunks(w):
        r, n = w.shape
        k = -(-r // P)
        z = np.zeros((k * P, n), w.dtype)
        z[:r] = w
        return z.reshape(k, P, n).transpose(1, 0, 2).reshape(P, k * n)

    def wide(w, n):
        z = np.zeros((w.shape[0], n), w.dtype)
        z[:, :w.shape[1]] = w
        return z

    o["w0"] = np.stack([np.concatenate([
        chunks(np.concatenate([f["L0_ffn_W1"][e].T, f["L0_ffn_W3"][e].T], 1)), chunks(f["L0_ffn_W2"][e].T)], 1)
        for e in range(E0)])
    o["sh0"] = np.concatenate([chunks(wide(f["L0_ffn_Ws1"].T, SH0)), chunks(wide(f["L0_ffn_Ws3"].T, SH0)),
                               chunks(f["L0_ffn_Ws2"].T)], 1)
    o["seg"] = f["itok_BxS_0_1023"].reshape(TILES, P).T
    o["W_kvc2"] = chunks(np.concatenate([f["L1_xattn_W_kvc"]] * 2, 1))
    swap = np.arange(ROPE).reshape(2, ROPE // 2)[::-1].reshape(-1)
    kr = f["L1_xattn_W_kr"]
    o["W_kr2"] = np.concatenate([kr, kr, kr[:, swap], kr[:, swap]], 1)
    o["W_dq"] = chunks(f["L1_xattn_W_dq"])
    qr = f["L1_xattn_W_qr"].reshape(QC, PAIRS, 2, ROPE)[:, :, ::-1]
    o["W_qrv"] = np.stack([qr, qr[..., swap]], 2).reshape(QC, PAIRS * 2 * P)
    for n in ("uq", "uk", "uv"):
        w = f["L1_xattn_W_" + n]
        o[f"W_{n}T"] = w.reshape(w.shape[0], HEADS, HD).transpose(2, 1, 0).reshape(HD, -1)
    o["W_oh"] = f["L1_xattn_W_o"].reshape(HEADS, HD, D).transpose(1, 0, 2).reshape(HD, HEADS * D)
    o["Wg1T"] = np.concatenate([f["L1_ffn_gate_w"], f["L1_ffn_se_gate_w"]], 0).T
    o["w1"] = np.stack([np.concatenate([
        chunks(np.concatenate([f["L1_ffn_w_gate"][e].T, f["L1_ffn_w_up"][e].T], 1)), chunks(f["L1_ffn_w_down"][e].T)], 1)
        for e in range(E1)])
    o["sh1"] = np.concatenate([chunks(f["L1_ffn_sh_gate"].T), chunks(f["L1_ffn_sh_up"].T),
                               chunks(f["L1_ffn_sh_down"].T)], 1)
    return {k: np.ascontiguousarray(x) for k, x in o.items()}


def kernel(**inputs):
    import concourse.bacc as bacc
    from concourse.bass_utils import run_bass_kernel_spmd

    arrays = host_layout(inputs)
    nc = bacc.Bacc("TRN2", target_bir_lowering=False, num_devices=1)
    aps = {n: nc.dram_tensor(n, x.shape, mybir.dt.from_np(x.dtype), kind="ExternalInput").ap() for n, x in arrays.items()}
    aps["out"] = nc.dram_tensor("out", (TOKENS, D), F32, kind="ExternalOutput").ap()
    build_program(nc, aps)
    r = run_bass_kernel_spmd(nc, [arrays], core_ids=[0])
    return np.asarray(r.results[0]["out"]).reshape(BATCH, SEQ, D)
```

```python
from contextlib import ExitStack

import numpy as np

import concourse.bass as bass
from concourse import mybir

F32 = mybir.dt.float32
F32R = mybir.dt.float32r
BF16 = mybir.dt.bfloat16
I32 = mybir.dt.int32
U32 = mybir.dt.uint32
ALU = mybir.AluOpType
ACT = mybir.ActivationFunctionType
AX = mybir.AxisListType

P = 128
BATCH, SEQ, D = 32, 64, 256
TOKENS = BATCH * SEQ
TILES = TOKENS // P
KC = D // P
GROUPS = 4
GT = TILES // GROUPS
GTOK = GT * P
LN_EPS = 1e-5

E0, HID0, TOP0, EGROUPS, EPG, TOPG = 16, 176, 4, 4, 4, 2
HID0_REST = HID0 - P
W13_0 = 2 * HID0
COLS0 = KC * W13_0 + 2 * D
SH0 = 384
SHC0 = SH0 // P
SHCOLS0 = 2 * KC * SH0 + SHC0 * D
SLOTS0_NEED = (TOKENS * TOP0 - E0) // P + E0
UNROLL = 4
AHEAD = 8
RINGQ = 4
XRING, XLEAD = 8, 6
SLOTS0 = -(-SLOTS0_NEED // UNROLL) * UNROLL
EARLY0 = 10
E1, HID1, TOP1 = 8, 128, 2
W13_1 = 2 * HID1
COLS1 = KC * W13_1 + D
SH1 = 256
SHC1 = SH1 // P
SHCOLS1 = 2 * KC * SH1 + SHC1 * D
SLOTS1_NEED = (TOKENS * TOP1 - E1) // P + E1
SLOTS1 = -(-SLOTS1_NEED // UNROLL) * UNROLL
HEADS, HD, KVC, QC, ROPE, LOOKBACK = 16, 128, 64, 96, 64, 8
PAIRS = HEADS // 2
NEG = 1e30
SM_SCALE = float(1.0 / np.sqrt(np.float32(HD + ROPE)))

CONST = {}
_at = 0
for _name, _n in (("ident", 128), ("before", 128), ("cos", 64), ("sin", 64), ("key_id", 64),
                  ("keep", 256), ("expert_id", 16), ("earlier_group", 16), ("later_groups", 4),
                  ("slot_id", 80), ("same_head", 128)):
    CONST[_name] = (_at, _at + _n)
    _at += _n
NCONST = _at


def constants():
    c = np.zeros((P, NCONST), np.float32)

    def put(name, value):
        a, b = CONST[name]
        c[:, a:b] = value

    p = np.arange(P)
    put("ident", np.eye(P))
    put("before", p[:, None] < p[None, :])
    half = ROPE // 2
    inv = (1.0 / np.float32(10000.0) ** (np.arange(half, dtype=np.float32) / np.float32(half))).astype(np.float32)
    ang = np.arange(SEQ, dtype=np.float32)[None, :] * inv[p % half][:, None]
    put("cos", np.cos(ang))
    put("sin", np.sin(ang) * np.where(p % ROPE < half, -1.0, 1.0)[:, None])
    put("key_id", np.arange(SEQ)[None, :])
    put("keep", np.arange(256)[None, :] % TILES != 0)
    put("expert_id", np.arange(16)[None, :])
    j = np.arange(16)
    put("earlier_group", (j % 4 < j // 4)[None, :])
    put("later_groups", 3 - np.arange(4)[None, :])
    put("slot_id", np.arange(80)[None, :])
    put("same_head", (p[:, None] // 64) == (p[None, :] // 64))
    select = (np.arange(TOKENS)[None, :] // SEQ == np.arange(BATCH)[:, None]).astype(np.float32)
    return c, select


class Map:

    BASE, END = 16512, 229312

    def __init__(self, nc):
        self.nc, self.at, self.top = nc, self.BASE, self.BASE

    def put(self, name, shape, dtype, at=None):
        size = int(np.prod(shape[1:])) * (2 if dtype == BF16 else 4)
        size = -(-size // 64) * 64
        if at is None:
            at = self.at
            self.at += size
        self.end = at + size
        self.top = max(self.top, self.end)
        assert self.end <= self.END, (name, self.end)
        return self.nc.alloc_sbuf_tensor_at(name, shape, dtype, offset=at)


class Moe:
    pass


def build_program(nc, a):
    ctx = ExitStack()
    with ctx:
        def sem(name):
            return ctx.enter_context(nc.semaphore(name))

        m = Map(nc)
        X = m.put("X", [P, TILES, D], F32)
        C = m.put("C", [P, NCONST], F32)
        PAR = m.put("PAR", [P, 16], F32)
        TRI = m.put("TRI", [P, P], BF16)
        ONES = m.put("ONES", [P, P], BF16)
        SEL = m.put("SEL", [P, TILES, 16], BF16)
        STAT = m.put("STAT", [P, TILES, 6], F32)
        MV = m.put("MV", [P, TILES, 2], F32)
        RSTD = m.put("RSTD", [P, TILES], F32)
        SHIFT = m.put("SHIFT", [P, TILES], F32)
        SD = m.put("SD", [P, TILES], F32)
        TOPW = m.put("TOPW", [P, TILES, 8], F32)
        TOPI = m.put("TOPI", [P, TILES, 8], U32)
        WK = m.put("WK", [P, 4, TILES], F32)
        SGATE = m.put("SGATE", [P, TILES], F32)
        POSI = m.put("POSI", [P, 4, TILES], U32)
        EID = m.put("EID", [1, SLOTS0], I32)
        EIDW = m.put("EIDW", [1, SLOTS0], I32)
        SMALL = m.put("SMALL", [P, 8, 16], F32)
        SMALLI = m.put("SMALLI", [P, 16], I32)
        ONE64 = m.put("ONE64", [P, SEQ], F32)
        ITOK = m.put("ITOK", [P, TILES], I32)
        SEG = m.put("SEG", [P, TILES], F32)
        phase_base = m.at

        GB_AT = Map.END - 8 * D * 4

        def slot_buffers(M, at):
            q = at
            M.XS = m.put(M.tag + "XS", [P, XRING, D], F32, at=q); q = m.end
            M.XHI = m.put(M.tag + "XHI", [P, 2, D], F32R, at=q); q = m.end
            M.XLO = m.put(M.tag + "XLO", [P, 2, D], F32R, at=q); q = m.end
            M.SIL = m.put(M.tag + "SIL", [P, 2, M.hid], F32, at=q); q = m.end
            M.G = m.put(M.tag + "G", [P, 2, M.hchunks * P], F32, at=q); q = m.end
            M.GHI = m.put(M.tag + "GHI", [P, 2, M.hchunks * P], F32R, at=q); q = m.end
            M.GLO = m.put(M.tag + "GLO", [P, 2, M.hchunks * P], F32R, at=q); q = m.end
            M.YS = m.put(M.tag + "YS", [P, 4, D], F32, at=q); q = m.end
            M.GB = m.put(M.tag + "GB", [P, 8, D], F32, at=GB_AT)
            return q

        both = [sem(name) for name in (
            "xn_transposed", "xn_transpose_copied", "logits_done", "logits_copied", "logits_token_major", "gate_loaded",
            "shared_loaded", "shared_split", "shared_x_split", "shared_hidden", "shared_silu", "shared_product",
            "shared_hi", "shared_lo", "shared_out", "shared_added", "expert_hi", "expert_weights_ready", "combined",
            "slot_xT", "slot_x_hi", "slot_x_lo", "slot_hidden", "slot_silu", "slot_g", "slot_gT", "slot_g_hi", "slot_g_lo",
            "slot_y", "slot_y_copied")]
        raw = [sem(f"expert{e}_loaded") for e in range(E0)]
        xl = [sem(f"slot_x_loaded{r}") for r in range(XRING)]
        st = [sem(f"slot_y_stored{r}") for r in range(4)]
        gath = [sem(f"gathered{r}") for r in range(8)]

        def moe(tag, before, E, hid, top, slots, shared):
            M = Moe()
            M.tag, M.E, M.hid, M.top, M.slots = tag, E, hid, top, slots
            M.hchunks = -(-hid // P)
            M.w13 = 2 * hid
            M.cols = KC * M.w13 + M.hchunks * D
            M.sh, M.shc = shared, shared // P
            M.x_by_expert = nc.dram_tensor(tag + "x_by_expert", [slots * P, D], F32, kind="Internal").ap()
            M.y_by_expert = nc.dram_tensor(tag + "y_by_expert", [slots * P, D], F32, kind="Internal").ap()
            (M.shifted, M.exped, M.sel, M.counts, M.routed, M.pos, M.eid, M.fill, M.scat) = [sem(tag + name) for name in (
                "scores_shifted", "scores_exp", "choice_ready", "counts_done", "routing_left_psum", "rows_known",
                "slot_experts_known", "rows_cleared", "rows_scattered")]
            (M.xt, M.xtc, M.lg, M.lgc, M.lgt, M.wg, M.shw, M.shsplit, M.shx, M.shh, M.shs, M.shu, M.shg, M.shl, M.shy,
             M.shadd, M.split, M.wready, M.comb, M.p_xt, M.a_xhi, M.d_xlo, M.p_h, M.a_sil, M.d_g, M.p_gt, M.a_ghi, M.d_glo,
             M.p_y, M.a_y) = both
            M.raw, M.xl, M.st, M.gath = raw, xl, st, gath
            M.early_slots = slots // 4
            M.n = 1 if before else 0
            M.slot0 = before.slots if before else 0
            M.chunk0 = GROUPS * before.shc if before else 0
            M.expert0 = before.E if before else 0
            M.copy0 = TILES * before.top if before else 0
            return M

        L0 = moe("l0_", None, E0, HID0, TOP0, SLOTS0, SH0)
        L0.norm_base = 2 * TILES
        L0.var0 = 2 * GROUPS
        L0.logits = E0
        L0.WHI = m.put("W0HI", [P, E0, COLS0], F32R)
        w0lo_at = m.at
        L0.WLO = m.put("W0LO", [P, E0, COLS0], F32R)
        L0.WRAW = [m.put(f"W0RAW{e}", [P, COLS0], F32, at=w0lo_at + e * COLS0 * 4) for e in range(E0)]
        tail_at = m.at
        hi_late = phase_base + EARLY0 * COLS0 * 4
        lo_late = w0lo_at + EARLY0 * COLS0 * 4
        late_size = (E0 - EARLY0) * COLS0 * 4
        XN = L0.XN = m.put("XN", [P, TILES, D], F32, at=tail_at)
        slot_buffers(L0, tail_at)
        q = hi_late
        L0.SHRAW = m.put("SH0RAW", [P, SHCOLS0], F32, at=q)
        L0.SHLO = m.put("SH0LO", [P, SHCOLS0], F32R, at=q); q = m.end
        L0.SHHI = m.put("SH0HI", [P, SHCOLS0], F32R, at=q); q = m.end
        L0.XSHI = m.put("XS0HI", [P, KC, GTOK], F32R, at=q); q = m.end
        L0.XSLO = m.put("XS0LO", [P, KC, GTOK], F32R, at=q); q = m.end
        L0.WG = m.put("WG0", [P, KC, E0], F32, at=q); q = m.end
        assert q <= hi_late + late_size, (q - hi_late, late_size)
        q = lo_late
        L0.XT = m.put("XT0", [P, KC, TOKENS], F32, at=q); q = m.end
        L0.SGHI = m.put("SG0HI", [P, SHC0, GTOK], F32R, at=q); q = m.end
        L0.SGLO = m.put("SG0LO", [P, SHC0, GTOK], F32R, at=q); q = m.end
        assert q <= lo_late + late_size
        q = phase_base + 4 * COLS0 * 4
        CTX = m.put("CTX", [P, KC, TOKENS], F32, at=q); q = m.end
        L0.SSIL = m.put("SSIL0", [P, 2, GTOK], F32, at=q); q = m.end
        L0.SU = m.put("SU0", [P, 2, GTOK], F32, at=q); q = m.end
        L0.LGT = m.put("LGT0", [16, GTOK], F32, at=q); q = m.end
        ZERO = m.put("ZERO", [P, D], F32, at=q); q = m.end
        assert q <= hi_late
        q = w0lo_at + 6 * COLS0 * 4
        CTXW = m.put("CTXW", [P, TOKENS], F32, at=q); q = m.end
        WIN = m.put("WIN", [P, KC, D], F32, at=q); q = m.end
        WOUT = m.put("WOUT", [P, KC, D], F32, at=q); q = m.end
        BOUT = m.put("BOUT", [P, D], F32, at=q); q = m.end
        GAMMA = m.put("GAMMA", [P, D], F32, at=q); q = m.end
        BETA = m.put("BETA", [P, D], F32, at=q); q = m.end
        assert q <= lo_late
        SELB = m.put("SELB", [BATCH, TOKENS], F32, at=phase_base)
        q = m.end
        EMA = m.put("EMA", [P, SEQ], F32, at=q); q = m.end
        EMAC = m.put("EMAC", [P, SEQ], F32, at=q); q = m.end
        CSUM = m.put("CSUM", [P, KC, BATCH], F32, at=q); q = m.end
        M1T = m.put("M1T", [P, KC, BATCH], F32, at=q); q = m.end
        SUMM = m.put("SUMM", [BATCH, D], F32, at=q); q = m.end
        BIN = m.put("BIN", [P, KC], F32, at=q); q = m.end
        L0.R = [m.put(f"R0_{i}", [P, 16, 16], F32, at=q + 1024 * i) for i in range(8)]
        assert m.end <= phase_base + 4 * COLS0 * 4
        L0.XCMP = m.put("XCMP0", [1, SLOTS0 * (E0 + 1)], F32, at=phase_base + 4 * COLS0 * 4)

        q = phase_base
        KB = m.put("KB", [P, TILES, 4, P], F32, at=q); q = m.end
        KR = m.put("KR", [P, 4, 4, P], F32, at=q); q = m.end
        AHI = m.put("AHI", [QC, PAIRS, 3, P], F32R, at=q); q = m.end
        ARAW = m.put("ARAW", [QC, PAIRS, 3, P], F32, at=q)
        ALO = m.put("ALO", [QC, PAIRS, 3, P], F32R, at=q); q = m.end
        BHI = m.put("BHI", [P, PAIRS, D], F32R, at=q); q = m.end
        BLO = m.put("BLO", [P, PAIRS, D], F32R, at=q); q = m.end
        MASK = m.put("MASK", [P, TILES, SEQ], F32, at=q); q = m.end
        WDQ = m.put("WDQ", [P, KC, QC], F32, at=q); q = m.end
        WKR = m.put("WKR", [KVC, 2, P], F32, at=q); q = m.end
        WKVC = m.put("WKVC", [P, KC, P], F32, at=q); q = m.end
        XNG = m.put("XNG", [P, 2, 2, D], F32, at=q); q = m.end
        XTG = m.put("XTG", [P, KC, 2 * P], F32, at=q); q = m.end
        QCHI = m.put("QCHI", [QC, 2 * P], F32R, at=q); q = m.end
        QCLO = m.put("QCLO", [QC, 2 * P], F32R, at=q); q = m.end
        RC = m.put("RC", [P, RINGQ, 2 * P], F32, at=q); q = m.end
        RS = m.put("RS", [P, RINGQ, 2 * P], F32, at=q); q = m.end
        CTHI = m.put("CTHI", [P, PAIRS, P], F32R, at=q); q = m.end
        CTLO = m.put("CTLO", [P, PAIRS, P], F32R, at=q); q = m.end
        OX = m.put("OX", [P, 2, D], F32, at=q); q = m.end
        SMX = m.put("SMX", [P, 2, 2, HEADS], F32, at=q); q = m.end
        prep_at = q
        Q = m.put("Q", [P, 2, HEADS, 2 * P], F32, at=q); q = m.end
        SM = m.put("SM", [P, 2, HEADS, SEQ], F32, at=q); q = m.end
        PT = m.put("PT", [P, PAIRS, P], F32, at=q); q = m.end
        assert q <= GB_AT
        q = prep_at
        CTX1 = m.put("CTX1", [P, KC, TOKENS], F32, at=q); q = m.end
        UQT = m.put("UQT", [P, HEADS, QC], F32, at=q); q = m.end
        UKT = m.put("UKT", [P, HEADS, KVC], F32, at=q); q = m.end
        UVT = m.put("UVT", [P, HEADS, KVC], F32, at=q); q = m.end
        WO = m.put("WO", [P, HEADS, D], F32, at=q); q = m.end
        assert q <= GB_AT, (prep_at, q, GB_AT)

        L1 = moe("l1_", L0, E1, HID1, TOP1, SLOTS1, SH1)
        L1.norm_base = 3 * TILES
        L1.var0 = 3 * GROUPS + TILES // 2
        L1.logits = E1 + 1
        q = phase_base
        L1.WHI = m.put("W1HI", [P, E1, COLS1], F32R, at=q); q = m.end
        w1lo_at = q
        L1.WLO = m.put("W1LO", [P, E1, COLS1], F32R, at=q); q = m.end
        L1.WRAW = [m.put(f"W1RAW{e}", [P, COLS1], F32, at=w1lo_at + e * COLS1 * 4) for e in range(E1)]
        L1.SHRAW = m.put("SH1RAW", [P, SHCOLS1], F32, at=q)
        L1.SHLO = m.put("SH1LO", [P, SHCOLS1], F32R, at=q); q = m.end
        L1.SHHI = m.put("SH1HI", [P, SHCOLS1], F32R, at=q); q = m.end
        L1.XSHI = m.put("XS1HI", [P, KC, GTOK], F32R, at=q); q = m.end
        L1.XSLO = m.put("XS1LO", [P, KC, GTOK], F32R, at=q); q = m.end
        L1.WG = m.put("WG1", [P, KC, E1 + 1], F32, at=q); q = m.end
        L1.XT = m.put("XT1", [P, KC, TOKENS], F32, at=q); q = m.end
        L1.SGHI = m.put("SG1HI", [P, SHC1, GTOK], F32R, at=q); q = m.end
        L1.SGLO = m.put("SG1LO", [P, SHC1, GTOK], F32R, at=q); q = m.end
        L1.SSIL = m.put("SSIL1", [P, 2, GTOK], F32, at=q); q = m.end
        L1.SU = m.put("SU1", [P, 2, GTOK], F32, at=q); q = m.end
        L1.LGT = m.put("LGT1", [16, GTOK], F32, at=q); q = m.end
        L1.R = [m.put(f"R1_{i}", [P, 16, 16], F32, at=q + 1024 * i) for i in range(8)]; q = m.end
        L1.XCMP = m.put("XCMP1", [1, SLOTS1 * (E1 + 1)], F32, at=q); q = m.end
        L1.XN = m.put("XN1", [P, TILES, D], F32, at=q); q = m.end
        slot_buffers(L1, q)

        PS = ctx.enter_context(nc.psum_tensor("PS", [P, 8, 512], F32))
        B = [PS[:, i, :] for i in range(8)]

        def const(name, rows=P):
            lo, hi = CONST[name]
            return C[0:rows, lo:hi]

        ident = const("ident")

        def absorbed_bank(p):
            return B[5 if p % 2 else 6]

        def rope_bank(p):
            return B[4 if p % 2 else 7]

        DECAY, KEEP, GX, TX, GF, TF, BC, CTOT = 0, 1, 2, 4, 6, 8, 10, 12
        L0.gate, L1.gate = TF, TF + 1

        s_const = sem("const_loaded")
        s_par = sem("params_loaded")
        s_x = [sem(f"x_loaded{g}") for g in range(GROUPS)]
        s_ctx = [sem(f"ctx_loaded{k}") for k in range(KC)]
        s_wio = sem("ema_weights_loaded")
        s_zero = sem("zero_tile")
        s_act = sem("act_chain")
        s_dve = sem("dve_chain")
        s_pool = sem("pool_chain")
        s_var = sem("variance_ready")
        s_sd = sem("sqrt_ready")
        s_rstd = sem("rstd_ready")
        s_norm = sem("tiles_normalised")
        s_beta = sem("beta_scaled")
        s_xb = sem("beta_added")
        s_csum = sem("ctx_sums_ready")
        s_ema = sem("ema_steps")
        s_spread = sem("summary_spread")
        s_spused = sem("spread_used")
        k_ctx, k_wkv, k_up, k_raw = sem("k_ctx_loaded"), sem("k_wkv_loaded"), sem("k_up_loaded"), sem("k_raw_loaded")
        k_zero = sem("kv_blocks_zeroed")
        k_kvc, k_kvcc = sem("kvc_done"), sem("kvc_copied")
        k_tok, k_tokc = sem("kvc_token_done"), sem("kvc_token_copied")
        k_rope, k_ropem, k_roped = sem("key_rope_done"), sem("key_rope_terms"), sem("key_rope_added")
        k_a, k_b, k_hi, k_lo = sem("absorbed_done"), sem("out_weights_done"), sem("weights_hi"), sem("weights_lo")
        k_mask = sem("mask_ready")
        t_norm, t_xt, t_xtc = sem("pair_normalised"), sem("pair_transposed"), sem("pair_transpose_copied")
        t_qc, t_qchi, t_qclo = sem("qc_done"), sem("qc_hi"), sem("qc_lo")
        t_abs, t_absc, t_rv, t_rvm, t_q = (sem("q_absorbed"), sem("q_absorbed_copied"), sem("q_rope_done"),
                                           sem("q_rope_terms"), sem("q_rope_added"))
        t_kl = [sem(f"keys_loaded{r}") for r in range(4)]
        t_s, t_masked, t_max, t_sub, t_exp, t_sum, t_rec, t_prob = (sem("scores"), sem("scores_masked"), sem("row_max"),
                                                            sem("max_subtracted"), sem("exp_done"), sem("row_sum"), sem("row_sum_inverse"),
                                                            sem("probs_ready"))
        t_pt, t_ptc, t_ct, t_cthi, t_ctlo = (sem("probsT"), sem("probsT_copied"), sem("ctxT"), sem("ctxT_hi"),
                                             sem("ctxT_lo"))
        t_o, t_oc, t_x = sem("attn_out"), sem("attn_out_scaled"), sem("attn_added")
        s_out = sem("out_stored")

        class Count:

            def __init__(self, eng, semaphore):
                self.eng, self.sem, self.n = eng, semaphore, 0

            def mark(self, ins):
                ins.then_inc(self.sem, 1)
                self.n += 1
                return ins

            def wait(self, back=0):
                self.eng.wait_ge(self.sem, self.n - back)

        def at_least(i, n):
            return not isinstance(i, int) or i >= n

        x_rows = a["x"].rearrange("(t p) d -> p t d", p=P)
        out_rows = a["out"].rearrange("(t p) d -> p t d", p=P)

        def run_stages(i, j, slots, stages):
            for d, stage in stages:
                if not isinstance(i, int) or 0 <= i + d < slots:
                    stage(i + d, (j + d) % UNROLL)

        def slot_loop(eng, slots, step, lead, trail):
            for i in range(-lead, UNROLL):
                step(i, i % UNROLL)
            for it in range(1, slots // UNROLL - 1):
                for j in range(UNROLL):
                    step(it * UNROLL + j, j)
            for i in range(slots - UNROLL, slots + trail):
                step(i, i % UNROLL)

        def tile_loop(step):
            for t in range(-AHEAD, TILES + 1):
                step(t, t % 4, t // 4 * 2)

        def tile(i, j, h, d, stage):
            if not isinstance(i, int) or 0 <= i + d < TILES:
                stage(i + d, (j + d) % 4, h + (j + d) // 2, (j + d) % 2)

        def pair(i, j, h, d, stage):
            if not isinstance(i, int) or 0 <= i + d < TILES:
                stage(h + (j + d) // 2, (j + d) // 2 % 2)

        block = ctx.enter_context(nc.Block())

        def load_gate_and_shared(sp, M, n):
            sp.dma_start(M.WG[:, :, :], a[f"Wg{n}T"].rearrange("(k p) n -> p k n", p=P)).then_inc(M.wg, 16)
            sp.dma_start(M.SHRAW[:, :], a[f"sh{n}"]).then_inc(M.shw, 16)

        def stream_slots(sp, M):
            def load(i):
                if i >= XRING:
                    sp.wait_ge(M.p_xt, M.slot0 + i - XRING + 1)
                sp.dma_start(M.XS[:, i % XRING, :], M.x_by_expert[i * P:(i + 1) * P, :]).then_inc(M.xl[i % XRING], 16)

            def store(i):
                sp.wait_ge(M.a_y, M.slot0 + i + 1)
                sp.dma_start(M.y_by_expert[i * P:(i + 1) * P, :], M.YS[:, i % 4, :]).then_inc(M.st[i % 4], 16)

            for i in range(M.slots + XLEAD):
                if i < M.slots:
                    load(i)
                if i >= XLEAD:
                    store(i - XLEAD)

        @block.sync
        def _(sp):
            sp.dma_start(C[:, :], a["const"]).then_inc(s_const, 16)
            sp.dma_start(PAR[:, DECAY:DECAY + 1], a["decay"].to_broadcast([P, 1])).then_inc(s_par, 16)
            sp.dma_start(PAR[:, GX:GX + 2], a["g_xattn"].to_broadcast([P, 2])).then_inc(s_par, 16)
            sp.dma_start(PAR[:, GF:GF + 2], a["g_ffn"].to_broadcast([P, 2])).then_inc(s_par, 16)
            sp.dma_start(BIN[:, :], a["b_in"]).then_inc(s_par, 16)
            for g in range(GROUPS):
                sp.dma_start(X[:, g * GT:(g + 1) * GT, :], x_rows[:, g * GT:(g + 1) * GT, :]).then_inc(s_x[g], 16)
            for k in range(KC):
                sp.dma_start(CTX[:, k, :], a["ctxT"][k * P:(k + 1) * P, :]).then_inc(s_ctx[k], 16)
            sp.dma_start(WIN[:, :, :], a["W_inT"].rearrange("(k p) n -> p k n", p=P)).then_inc(s_wio, 16)
            sp.dma_start(WOUT[:, :, :], a["W_outT"].rearrange("(k p) n -> p k n", p=P)).then_inc(s_wio, 16)
            sp.dma_start(BOUT[:, :], a["b_out"].to_broadcast([P, D])).then_inc(s_wio, 16)
            sp.dma_start(GAMMA[:, :], a["gamma"].to_broadcast([P, D])).then_inc(s_wio, 16)
            sp.dma_start(BETA[:, :], a["beta"].to_broadcast([P, D])).then_inc(s_wio, 16)
            sp.dma_start(SELB[:, :], a["select"]).then_inc(s_wio, 16)
            load_gate_and_shared(sp, L0, 0)
            sp.wait_ge(s_zero, 2)
            for M in (L0, L1):
                sp.dma_start(M.x_by_expert.rearrange("(n p) d -> p n d", p=P),
                             ZERO[:, :].unsqueeze(1).to_broadcast([P, M.slots, D])).then_inc(M.fill, 16)
            sp.wait_ge(L0.lgt, TILES)
            sp.wait_ge(L0.fill, 16)
            sp.wait_ge(L1.fill, 16)
            for e in range(EARLY0):
                sp.dma_start(L0.WRAW[e][:, :], a["w0"][e]).then_inc(L0.raw[e], 16)
            sp.wait_ge(L0.shadd, TILES)
            for e in range(EARLY0, E0):
                sp.dma_start(L0.WRAW[e][:, :], a["w0"][e]).then_inc(L0.raw[e], 16)
            sp.wait_ge(L0.scat, 16 * TILES * TOP0)
            stream_slots(sp, L0)
            sp.wait_ge(L0.wready, E0)
            sp.dma_start(ITOK[:, :], a["seg"]).then_inc(k_wkv, 16)
            sp.dma_start(WKVC[:, :, :], a["W_kvc2"].rearrange("p (k n) -> p k n", k=KC)).then_inc(k_wkv, 16)
            sp.dma_start(WKR[:, :, :], a["W_kr2"].rearrange("p (k n) -> p k n", k=2)).then_inc(k_wkv, 16)
            sp.dma_start(WDQ[:, :, :], a["W_dq"].rearrange("p (k n) -> p k n", k=KC)).then_inc(k_wkv, 16)
            for k in range(KC):
                sp.dma_start(CTX1[:, k, :], a["ctxT"][k * P:(k + 1) * P, :]).then_inc(k_ctx, 16)
            sp.dma_start(ARAW[:, :, 1:3, :], a["W_qrv"].rearrange("q (p v n) -> q p v n", p=PAIRS, v=2)).then_inc(k_raw, 16)
            sp.dma_start(UQT[:, :, :], a["W_uqT"].rearrange("p (h n) -> p h n", h=HEADS)).then_inc(k_up, 16)
            sp.dma_start(UKT[:, :, :], a["W_ukT"].rearrange("p (h n) -> p h n", h=HEADS)).then_inc(k_up, 16)
            sp.dma_start(UVT[:, :, :], a["W_uvT"].rearrange("p (h n) -> p h n", h=HEADS)).then_inc(k_up, 16)
            sp.dma_start(WO[:, :, :], a["W_oh"].rearrange("p (h n) -> p h n", h=HEADS)).then_inc(k_up, 16)
            sp.wait_ge(k_roped, 2 * GROUPS)
            sp.wait_ge(k_kvcc, 2 * GROUPS)
            sp.wait_ge(k_tokc, 4 * GROUPS)

            def keys(i, r, u, o):
                if at_least(i, 4):
                    sp.wait_ge(t_ct, i * 2 - 6)
                sp.dma_start(KR[:, r, :, :], KB[:, bass.ds(i, 1), :, :].rearrange("p o k n -> p (o k) n"))\
                    .then_inc(t_kl[r], 16)

            tile_loop(lambda i, j, h: tile(i, j, h, 4, keys))
            sp.wait_ge(t_x, TILES)
            load_gate_and_shared(sp, L1, 1)
            for e in range(E1):
                sp.dma_start(L1.WRAW[e][:, :], a["w1"][e]).then_inc(L1.raw[e], 16)
            sp.wait_ge(L1.scat, 16 * TILES * TOP1)
            stream_slots(sp, L1)
            for g in range(GROUPS):
                sp.wait_ge(L1.comb, L1.copy0 + (g + 1) * GT * TOP1)
                sp.dma_start(out_rows[:, g * GT:(g + 1) * GT, :], X[:, g * GT:(g + 1) * GT, :]).then_inc(s_out, 16)
            sp.wait_ge(s_out, 16 * GROUPS)

        def scatter(pool, M):
            pool.wait_ge(M.fill, 16)
            pool.wait_ge(M.pos, 1)
            for t in range(TILES):
                for k in range(M.top):
                    pool.indirect_dma_start(M.x_by_expert, bass.IndirectOffsetOnAxis(POSI[:, k, t:t + 1], 0),
                                            M.XN[:, t, :], None, bounds_check=M.slots * P - 1,
                                            oob_is_err=False).then_inc(M.scat, 16)

        def gather(pool, M, t):
            for k in range(M.top):
                n = M.copy0 + t * M.top + k
                if n >= 8:
                    pool.wait_ge(M.comb, n - 7)
                pool.indirect_dma_start(M.GB[:, n % 8, :], None, M.y_by_expert,
                                        bass.IndirectOffsetOnAxis(POSI[:, k, t:t + 1], 0),
                                        bounds_check=M.slots * P - 1, oob_is_err=False).then_inc(M.gath[n % 8], 16)

        def wait_for_slots(pool, M):
            for r in range(4):
                pool.wait_ge(M.st[r], 16 * ((M.slot0 + M.slots) // 4))

        @block.gpsimd
        def _(pool):
            ch = Count(pool, s_pool)
            pool.memset(ZERO[:, :], 0.0).then_inc(s_zero, 1)
            pool.memset(ONE64[:, :], 1.0).then_inc(s_zero, 1)
            pool.wait_ge(s_wio, 16 * 6)
            pool.wait_ge(s_beta, 1)
            for t in range(TILES):
                pool.wait_ge(s_norm, t + 1)
                pool.tensor_tensor(X[:, t, :], X[:, t, :], BETA[:, :], ALU.add).then_inc(s_xb, 1)
            scatter(pool, L0)
            pool.wait_ge(L0.wready, EARLY0)
            for e in range(EARLY0, E0):
                pool.wait_ge(L0.raw[e], 16)
                ch.mark(pool.tensor_scalar(L0.WHI[:, e, :], L0.WRAW[e][:, :], 1.0, None, ALU.mult))
                ch.wait()
                pool.tensor_tensor(L0.WLO[:, e, :], L0.WRAW[e][:, :], L0.WHI[:, e, :].bitcast(F32),
                                   ALU.subtract).then_inc(L0.wready, 1)
            wait_for_slots(pool, L0)
            cos = const("cos").unsqueeze(1)

            last, gathers = [], []

            def after_last():
                if last:
                    pool.wait_ge(*last[-1])

            def gather_tile(t, r, u, o):
                after_last()
                gather(pool, L0, t)
                gathers.append(t)

            def sub(i, r, u, o):
                pool.wait_ge(t_max, i + 1)
                after_last()
                pool.tensor_tensor(SM[:, r % 2, :, :], SM[:, r % 2, :, :],
                                   SMX[:, r % 2, 0, :].unsqueeze(2).to_broadcast([P, HEADS, SEQ]), ALU.subtract)\
                    .then_inc(t_sub, 1)
                last.append((t_sub, i + 1))

            def rope(p):
                def stage(v, par):
                    n = v * PAIRS + p
                    pool.wait_ge(t_rvm, 2 * n + 2)
                    if v >= 2:
                        pool.wait_ge(t_s, v * 4 - 4)
                    if gathers:
                        for k in range(TOP0):
                            n_g = gathers[-1] * TOP0 + k
                            pool.wait_ge(L0.gath[n_g % 8], 16 * (n_g // 8 + 1))
                        gathers.clear()
                    for half, head in ((0, 2 * p + 1), (64, 2 * p)):
                        after_last()
                        s = slice(half, half + 64)
                        pool.tensor_tensor(Q[s, par, head, :], RC[s, n % RINGQ, :], RS[s, n % RINGQ, :], ALU.add)\
                            .then_inc(t_q, 1)
                        last.append((t_q, 2 * n + (2 if half else 1)))
                return stage

            def add_x(i, r, u, o):
                pool.wait_ge(t_oc, i + 1)
                after_last()
                pool.tensor_tensor(X[:, i, :], X[:, i, :], OX[:, r % 2, :], ALU.add).then_inc(t_x, 1)
                last.append((t_x, i + 1))

            def step(i, j, h):
                tile(i, j, h, 1, sub)
                first = 0 if j % 2 else 4
                d = 3 if j % 2 else 2
                for p in range(first, first + 4):
                    pair(i, j, h, d, rope(p))
                tile(i, j, h, -1, add_x)
                tile(i, j, h, 8, gather_tile)

            tile_loop(step)
            scatter(pool, L1)
            wait_for_slots(pool, L1)
            for t in range(TILES):
                gather(pool, L1, t)

        @block.scalar
        def _(act):
            act.wait_ge(s_par, 16 * 4)
            act.activation(PAR[:, KEEP:KEEP + 1], PAR[:, DECAY:DECAY + 1], ACT.Sigmoid).then_inc(s_act, 1)
            act.activation(PAR[:, TX:TX + 2], PAR[:, GX:GX + 2], ACT.Tanh).then_inc(s_act, 1)
            act.activation(PAR[:, TF:TF + 2], PAR[:, GF:GF + 2], ACT.Tanh).then_inc(s_act, 1)

            def deviations(n, t0, t1):
                act.wait_ge(s_var, n + 1)
                act.activation(SD[:, t0:t1], SD[:, t0:t1], ACT.Sqrt).then_inc(s_sd, 1)

            def norm_pass(n, src):
                for g in range(GROUPS):
                    deviations(n * GROUPS + g, g * GT, (g + 1) * GT)
                    act.wait_ge(s_rstd, n * GROUPS + g + 1)
                    for t in range(g * GT, (g + 1) * GT):
                        act.activation(XN[:, t, :], src[:, t, :], ACT.Identity, bias=SHIFT[:, t:t + 1],
                                       scale=RSTD[:, t:t + 1]).then_inc(s_norm, 1)

            norm_pass(0, X)
            norm_pass(1, XN)

            def norm_and_gate(M):
                for g in range(GROUPS):
                    deviations(M.var0 + g, g * GT, (g + 1) * GT)
                    act.wait_ge(s_rstd, M.var0 + g + 1)
                    for t in range(g * GT, (g + 1) * GT):
                        act.activation(M.XN[:, t, :], X[:, t, :], ACT.Identity, bias=SHIFT[:, t:t + 1],
                                       scale=RSTD[:, t:t + 1]).then_inc(s_norm, 1)
                    for k in range(KC):
                        act.wait_ge(M.xt, (M.n * GROUPS + g) * KC + k + 1)
                        act.copy(M.XT[:, k, g * GTOK:(g + 1) * GTOK], B[k][:, :]).then_inc(M.xtc, 1)
                    act.wait_ge(M.lg, M.n * GROUPS + g + 1)
                    if g:
                        act.wait_ge(M.lgt, M.n * TILES + g * GT)
                    act.copy(M.LGT[0:M.logits, :], B[2][0:M.logits, :]).then_inc(M.lgc, 1)

            def shared(M):
                act.wait_ge(M.shw, 16 * (M.n + 1))
                act.copy(M.SHHI[:, :], M.SHRAW[:, :]).then_inc(M.shsplit, 1)
                for g in range(GROUPS):
                    if g:
                        act.wait_ge(M.shh, M.chunk0 + g * M.shc)
                    act.wait_ge(M.xtc, KC * GROUPS * (M.n + 1))
                    act.copy(M.XSHI[:, :, :], M.XT[:, :, g * GTOK:(g + 1) * GTOK]).then_inc(M.shx, 1)
                    for c in range(M.shc):
                        n = g * M.shc + c
                        act.wait_ge(M.shh, M.chunk0 + n + 1)
                        if n >= 2:
                            act.wait_ge(M.shu, M.chunk0 + n - 1)
                        act.activation(M.SSIL[:, n % 2, :], B[2 * (n % 2)][:, :], ACT.Silu).then_inc(M.shs, 1)
                        act.wait_ge(M.shu, M.chunk0 + n + 1)
                        if g:
                            act.wait_ge(M.shy, M.n * TILES + g * GT)
                        act.copy(M.SGHI[:, c, :], M.SU[:, n % 2, :]).then_inc(M.shg, 1)

            def split_hi(M, experts):
                for e in experts:
                    act.wait_ge(M.raw[e], 16 * (M.n + 1))
                    act.copy(M.WHI[:, e, :], M.WRAW[e][:, :]).then_inc(M.split, 1)

            def slots(M):
                def hi(i, j):
                    act.wait_ge(M.p_xt, i + (M.slot0 + 1))
                    if at_least(i, 2):
                        act.wait_ge(M.p_h, i + (M.slot0 - 1))
                    act.copy(M.XHI[:, j % 2, :], B[j % 2][:, 0:D]).then_inc(M.a_xhi, 1)

                def sil(i, j):
                    act.wait_ge(M.p_h, i + (M.slot0 + 1))
                    if at_least(i, 2):
                        act.wait_ge(M.d_g, i + (M.slot0 - 1))
                    act.activation(M.SIL[:, j % 2, :], B[2 + j % 2][:, 0:M.hid], ACT.Silu).then_inc(M.a_sil, 1)

                def ghi(i, j):
                    act.wait_ge(M.p_gt, i + (M.slot0 + 1))
                    if at_least(i, 2):
                        act.wait_ge(M.p_y, i + (M.slot0 - 1))
                    act.copy(M.GHI[:, j % 2, :], B[4 + j % 2][:, 0:M.hchunks * P]).then_inc(M.a_ghi, 1)

                def y(i, j):
                    act.wait_ge(M.p_y, i + (M.slot0 + 1))
                    if at_least(i, 4):
                        if isinstance(i, int):
                            act.wait_ge(M.st[j % 4], 16 * ((i + M.slot0) // 4))
                        else:
                            act.wait_ge(M.st[j % 4], (i - j) * 4 + 4 * M.slot0)
                    act.copy(M.YS[:, j % 4, :], B[6 + j % 2][:, 0:D]).then_inc(M.a_y, 1)

                def step(i, j):
                    run_stages(i, j, M.slots, ((2, hi), (1, sil), (0, ghi), (-1, y)))

                slot_loop(act, M.slots, step, 2, 1)

            norm_and_gate(L0)
            act.wait_ge(L0.shifted, 1)
            act.activation(L0.R[0][:, :, :], L0.R[0][:, :, :], ACT.Exp).then_inc(L0.exped, 1)
            shared(L0)
            act.wait_ge(L0.shadd, TILES)
            act.wait_ge(L0.shg, GROUPS * SHC0)
            split_hi(L0, range(EARLY0))
            slots(L0)
            for n in range(GROUPS):
                act.wait_ge(k_kvc, n + 1)
                for half, which in ((0, 0), (64, 1)):
                    s = slice(half, half + 64)
                    act.copy(KB[s, n * GT:(n + 1) * GT, which, :],
                             B[n][s, :].rearrange("p (t n) -> p t n", n=P)).then_inc(k_kvcc, 1)
            act.wait_ge(k_raw, 16)
            act.copy(AHI[:, :, 1:3, :], ARAW[:, :, 1:3, :]).then_inc(k_hi, 1)
            for n in range(2):
                act.wait_ge(k_a, n + 1)
                act.copy(AHI[:, 4 * n:4 * n + 4, 0, :], B[n][0:QC, :].rearrange("p (h n) -> p h n", n=P))\
                    .then_inc(k_hi, 1)
            for n in range(4):
                act.wait_ge(k_b, n + 1)
                act.copy(BHI[:, 2 * n:2 * n + 2, :], B[2 + n][:, :].rearrange("p (h n) -> p h n", n=D))\
                    .then_inc(k_hi, 1)

            def sqrt_pair(v, par):
                deviations(3 * GROUPS + v, 2 * v, 2 * v + 2)

            def norm_pair(v, par):
                act.wait_ge(s_rstd, 3 * GROUPS + v + 1)
                if at_least(v, 2):
                    act.wait_ge(t_xt, v - 1)
                for o in range(2):
                    at = v * 2 + o
                    act.activation(XNG[:, par, o, :], X[:, bass.ds(at, 1), :].rearrange("p o d -> p (o d)"), ACT.Identity,
                                   bias=SHIFT[:, bass.ds(at, 1)], scale=RSTD[:, bass.ds(at, 1)]).then_inc(t_norm, 1)

            def copy_xt(v, par):
                act.wait_ge(t_xt, v + 1)
                if at_least(v, 1):
                    act.wait_ge(t_qc, v)
                act.copy(XTG[:, :, :], B[7][:, :].rearrange("p (k n) -> p k n", k=KC)).then_inc(t_xtc, 1)

            def qc_hi(v, par):
                act.wait_ge(t_qc, v + 1)
                if at_least(v, 1):
                    act.wait_ge(t_rv, v * PAIRS)
                act.copy(QCHI[:, :], B[5][0:QC, 0:2 * P]).then_inc(t_qchi, 1)

            def absorbed(p):
                def stage(v, par):
                    act.wait_ge(t_abs, v * PAIRS + (p + 1))
                    if at_least(v, 2):
                        act.wait_ge(t_s, v * 4 - 4)
                    for half, head in ((0, 2 * p), (64, 2 * p + 1)):
                        s = slice(half, half + 64)
                        act.copy(Q[s, par, head, :], absorbed_bank(p)[s, 0:2 * P]).then_inc(t_absc, 1)
                return stage

            def copy_pt(i, r, u, o):
                for n in range(2):
                    act.wait_ge(t_pt, i * 2 + (n + 1))
                    if at_least(i, 1):
                        act.wait_ge(t_ct, i * 2)
                    act.copy(PT[:, 4 * n:4 * n + 4, :], B[2 + n][:, :].rearrange("p (h n) -> p h n", n=P))\
                        .then_inc(t_ptc, 1)

            def scale_out(i, r, u, o):
                act.wait_ge(t_o, i + 1)
                if at_least(i, 2):
                    act.wait_ge(t_x, i - 1)
                act.activation(OX[:, r % 2, :], B[6][:, 2 * P:], ACT.Copy, scale=PAR[:, TX + 1:TX + 2]).then_inc(t_oc, 1)

            def exp(i, r, u, o):
                act.wait_ge(t_sub, i + 1)
                act.activation(SM[:, r % 2, :, :], SM[:, r % 2, :, :], ACT.Exp, scale=SM_SCALE).then_inc(t_exp, 1)

            def ct_hi(i, r, u, o):
                for b in range(2):
                    act.wait_ge(t_ct, i * 2 + (b + 1))
                    if at_least(i, 1):
                        act.wait_ge(t_o, i)
                    act.copy(CTHI[:, :, b * 64:(b + 1) * 64], B[2 + b][:, :].rearrange("p (h n) -> p h n", n=64))\
                        .then_inc(t_cthi, 1)

            def step(i, j, h):
                if j % 2:
                    pair(i, j, h, 3, qc_hi)
                    pair(i, j, h, 5, sqrt_pair)
                    tile(i, j, h, 0, copy_pt)
                    pair(i, j, h, 3, absorbed(0))
                    tile(i, j, h, -1, scale_out)
                    pair(i, j, h, 3, absorbed(1))
                    tile(i, j, h, 1, exp)
                    tile(i, j, h, 0, ct_hi)
                    pair(i, j, h, 3, absorbed(2))
                    pair(i, j, h, 3, absorbed(3))
                    pair(i, j, h, 5, norm_pair)
                else:
                    pair(i, j, h, 2, absorbed(4))
                    pair(i, j, h, 2, absorbed(5))
                    tile(i, j, h, 0, copy_pt)
                    pair(i, j, h, 2, absorbed(6))
                    tile(i, j, h, 1, exp)
                    tile(i, j, h, -1, scale_out)
                    pair(i, j, h, 2, absorbed(7))
                    pair(i, j, h, 4, copy_xt)
                    tile(i, j, h, 0, ct_hi)

            tile_loop(step)
            act.wait_ge(t_x, TILES)
            norm_and_gate(L1)
            act.wait_ge(L1.shifted, 1)
            act.activation(SGATE[:, :], L1.R[0][:, :, E1], ACT.Sigmoid).then_inc(L1.exped, 1)
            act.wait_ge(L1.shifted, 2)
            act.activation(SMALL[:, 6, :], SMALL[:, 5, :], ACT.Exp).then_inc(L1.exped, 1)
            shared(L1)
            split_hi(L1, range(E1))
            slots(L1)

        @block.tensor
        def _(pe):
            def three_passes(out, operands, first=True, last=True):
                passes = [(x, w) for xh, xl, wh, wl in operands for x, w in ((xh, wh), (xh, wl), (xl, wh))]
                for n, (x, w) in enumerate(passes):
                    mm = pe.matmul(out, x, w, start=(n == 0), stop=(n == len(passes) - 1))
                return mm

            def gate(M):
                pe.wait_ge(M.wg, 16 * (M.n + 1))
                for g in range(GROUPS):
                    for k in range(KC):
                        if g:
                            pe.wait_ge(M.xtc, (M.n * GROUPS + g - 1) * KC + k + 1)
                        for t in range(GT):
                            pe.wait_ge(s_norm, M.norm_base + g * GT + t + 1)
                            tr = pe.transpose(B[k][:, t * P:(t + 1) * P], M.XN[:, g * GT + t, k * P:(k + 1) * P], ident)
                        tr.then_inc(M.xt, 1)
                    if g:
                        pe.wait_ge(M.lgc, M.n * GROUPS + g)
                    pe.wait_ge(M.xtc, (M.n * GROUPS + g + 1) * KC)
                    for k in range(KC):
                        mm = pe.matmul(B[2][0:M.logits, :], M.WG[:, k, :], M.XT[:, k, g * GTOK:(g + 1) * GTOK],
                                       start=(k == 0), stop=(k == KC - 1))
                    mm.then_inc(M.lg, 1)
                    pe.wait_ge(M.lgc, M.n * GROUPS + g + 1)
                    for t in range(GT):
                        at = (g * GT + t) * 16
                        pe.transpose(B[3][:, at:at + M.logits], M.LGT[0:M.logits, t * P:(t + 1) * P],
                                     C[0:M.logits, 0:M.logits]).then_inc(M.lgt, 1)

            def counts(M):
                pe.wait_ge(M.sel, 1)
                pe.matmul(B[4][:, 0:256], TRI[:, :], SEL[:, :, :].rearrange("p t e -> p (t e)"), start=True, stop=True)
                pe.matmul(B[5][:, 0:256], ONES[:, :], SEL[:, :, :].rearrange("p t e -> p (t e)"),
                          start=True, stop=True).then_inc(M.counts, 1)

            def shared(M):
                pe.wait_ge(M.shsplit, 2 * (M.n + 1))
                pe.wait_ge(M.routed, 1)
                SH, n13 = M.sh, KC * M.sh
                w1 = [s[:, 0:n13].rearrange("p (k n) -> p k n", k=KC) for s in (M.SHHI, M.SHLO)]
                w3 = [s[:, n13:2 * n13].rearrange("p (k n) -> p k n", k=KC) for s in (M.SHHI, M.SHLO)]
                w2 = [s[:, 2 * n13:].rearrange("p (c n) -> p c n", c=M.shc) for s in (M.SHHI, M.SHLO)]
                for g in range(GROUPS):
                    pe.wait_ge(M.shx, 2 * (M.n * GROUPS + g + 1))
                    for c in range(M.shc):
                        n = g * M.shc + c
                        if n >= 2:
                            pe.wait_ge(M.shu, M.chunk0 + n - 1)
                        for w, bank in ((w1, B[2 * (n % 2)]), (w3, B[2 * (n % 2) + 1])):
                            mm = three_passes(bank[:, :], [(w[0][:, k, c * P:(c + 1) * P], w[1][:, k, c * P:(c + 1) * P],
                                                            M.XSHI[:, k, :], M.XSLO[:, k, :]) for k in range(KC)])
                        mm.then_inc(M.shh, 1)
                    pe.wait_ge(M.shl, M.chunk0 + (g + 1) * M.shc)
                    for t in range(GT):
                        n = g * GT + t
                        if n >= 2:
                            pe.wait_ge(M.shadd, M.n * TILES + n - 1)
                        s = slice(t * P, (t + 1) * P)
                        three_passes(B[4 + n % 2][:, 0:D], [(M.SGHI[:, c, s], M.SGLO[:, c, s], w2[0][:, c, :], w2[1][:, c, :])
                                                            for c in range(M.shc)]).then_inc(M.shy, 1)

            def slots(M):
                whi = M.WHI[:, :, :].rearrange("p e c -> p (e c)")
                wlo = M.WLO[:, :, :].rearrange("p e c -> p (e c)")

                at_expert = {}

                def load_expert(i):
                    if i < M.slots:
                        at_expert[i] = pe.value_load(EID[0:1, i:i + 1], min_val=0, max_val=(M.E - 1) * M.cols)

                def xt(i, j):
                    pe.wait_ge(M.xl[i % XRING], 16 * ((i + M.slot0) // XRING + 1))
                    if at_least(i, 2):
                        pe.wait_ge(M.d_xlo, i + (M.slot0 - 1))
                    for k in range(KC):
                        tr = pe.transpose(B[j % 2][:, k * P:(k + 1) * P], M.XS[:, i % XRING, k * P:(k + 1) * P], ident)
                    tr.then_inc(M.p_xt, 1)

                def hidden(i, j):
                    if i < M.early_slots:
                        pe.wait_ge(M.wready, pe.value_load(EIDW[0:1, i:i + 1], min_val=1, max_val=E0 + E1))
                    else:
                        pe.wait_ge(M.wready, M.expert0 + M.E)
                    pe.wait_ge(M.d_xlo, i + (M.slot0 + 1))
                    if at_least(i, 2):
                        pe.wait_ge(M.d_g, i + (M.slot0 - 1))
                    out = B[2 + j % 2][:, 0:M.w13]
                    for k in range(KC):
                        at = bass.ds(at_expert[i] + k * M.w13, M.w13)
                        s = slice(k * P, (k + 1) * P)
                        pe.matmul(out, M.XHI[:, j % 2, s], whi[:, at], start=(k == 0), stop=False)
                        pe.matmul(out, M.XLO[:, j % 2, s], whi[:, at], start=False, stop=False)
                        mm = pe.matmul(out, M.XHI[:, j % 2, s], wlo[:, at], start=False, stop=(k == KC - 1))
                    mm.then_inc(M.p_h, 1)

                def gt(i, j):
                    pe.wait_ge(M.d_g, i + (M.slot0 + 1))
                    if at_least(i, 2):
                        pe.wait_ge(M.d_glo, i + (M.slot0 - 1))
                    for c in range(M.hchunks):
                        tr = pe.transpose(B[4 + j % 2][:, c * P:(c + 1) * P], M.G[:, j % 2, c * P:(c + 1) * P], ident)
                    tr.then_inc(M.p_gt, 1)

                def y(i, j):
                    pe.wait_ge(M.d_glo, i + (M.slot0 + 1))
                    if at_least(i, 2):
                        pe.wait_ge(M.a_y, i + (M.slot0 - 1))
                    out = B[6 + j % 2][:, 0:D]
                    for c in range(M.hchunks):
                        at = bass.ds(at_expert[i] + KC * M.w13 + c * D, D)
                        s = slice(c * P, (c + 1) * P)
                        pe.matmul(out, M.GHI[:, j % 2, s], whi[:, at], start=(c == 0), stop=False)
                        pe.matmul(out, M.GLO[:, j % 2, s], whi[:, at], start=False, stop=False)
                        if c == 0:
                            load_expert(i + 3)
                        mm = pe.matmul(out, M.GHI[:, j % 2, s], wlo[:, at], start=False, stop=(c == M.hchunks - 1))
                    mm.then_inc(M.p_y, 1)

                def step(i, j):
                    run_stages(i, j, M.slots, ((2, xt), (1, hidden), (0, gt), (-1, y)))

                for i in range(3):
                    load_expert(i)
                slot_loop(pe, M.slots, step, 2, 1)

            pe.wait_ge(s_const, 16)
            pe.wait_ge(s_wio, 16 * 6)
            pe.wait_ge(s_csum, KC)
            for j in range(KC):
                for k in range(KC):
                    mm = pe.matmul(B[0][:, j * BATCH:(j + 1) * BATCH], WIN[:, k, j * P:(j + 1) * P], CSUM[:, k, :],
                                   start=(k == 0), stop=(k == KC - 1))
            mm.then_inc(s_ema, 1)
            pe.wait_ge(s_ema, 1 + KC)
            for j in range(KC):
                mm = pe.matmul(B[1][0:BATCH, 0:D], M1T[:, j, :], WOUT[:, j, :], start=(j == 0), stop=(j == KC - 1))
            mm.then_inc(s_ema, 1)
            pe.wait_ge(s_ema, 3 + KC)
            for t in range(TILES):
                if t >= 6:
                    pe.wait_ge(s_spused, t - 5)
                pe.matmul(B[2 + t % 6][:, 0:D], SELB[:, t * P:(t + 1) * P],
                          SUMM[:, :], start=True, stop=True).then_inc(s_spread, 1)
            pe.wait_ge(s_spused, TILES)
            gate(L0)
            counts(L0)
            shared(L0)
            pe.wait_ge(L0.shadd, TILES)
            pe.wait_ge(L0.eid, 2)
            slots(L0)
            pe.wait_ge(k_wkv, 16 * 4)
            pe.wait_ge(k_ctx, 16 * KC)
            pe.wait_ge(L0.a_y, SLOTS0)
            for n in range(GROUPS):
                for k in range(KC):
                    mm = pe.matmul(B[n][:, :], WKVC[:, k, :], CTX1[:, k, n * GTOK:(n + 1) * GTOK],
                                   start=(k == 0), stop=(k == KC - 1))
                mm.then_inc(k_kvc, 1)
            for n in range(GROUPS):
                for t in range(GT):
                    for k in range(KC):
                        at = (n * GT + t) * P
                        mm = pe.matmul(B[4 + n][:, t * P:(t + 1) * P], CTX1[:, k, at:at + P], WKVC[:, k, :],
                                       start=(k == 0), stop=(k == KC - 1))
                mm.then_inc(k_tok, 1)
            for n in range(GROUPS):
                pe.wait_ge(k_kvcc, 2 * (n + 1))
                kv = KB[0:KVC, n * GT:(n + 1) * GT, 0, :]
                pe.matmul(B[n][:, :], WKR[:, 0, :], kv, start=True, stop=True)
                pe.wait_ge(k_tokc, 4 * (n + 1))
                pe.matmul(B[4 + n][:, :], WKR[:, 1, :], kv, start=True, stop=True).then_inc(k_rope, 1)
            pe.wait_ge(k_up, 16 * 4)
            for n in range(2):
                pe.wait_ge(k_ropem, 2 * (n + 1))
                for h in range(8):
                    mm = pe.matmul(B[n][0:QC, h * KVC:(h + 1) * KVC], UQT[:, 8 * n + h, :], UKT[:, 8 * n + h, :],
                                   start=True, stop=True)
                mm.then_inc(k_a, 1)
            pe.wait_ge(k_ropem, 2 * GROUPS)
            for n in range(4):
                for h in range(4):
                    half = h % 2 * 64
                    mm = pe.matmul(B[2 + n][half:half + 64, h // 2 * D:(h // 2 + 1) * D], UVT[:, 4 * n + h, :],
                                   WO[:, 4 * n + h, :], start=True, stop=True)
                mm.then_inc(k_b, 1)
            pe.wait_ge(k_lo, 7)

            def transpose_pair(v, par):
                pe.wait_ge(t_norm, v * 2 + 2)
                if at_least(v, 1):
                    pe.wait_ge(t_rvm, v * 2 * PAIRS - 2)
                for k in range(KC):
                    for o in range(2):
                        tr = pe.transpose(B[7][:, (2 * k + o) * P:(2 * k + o + 1) * P],
                                          XNG[:, par, o, k * P:(k + 1) * P], ident)
                tr.then_inc(t_xt, 1)

            def down(v, par):
                pe.wait_ge(t_xtc, v + 1)
                if at_least(v, 1):
                    pe.wait_ge(t_absc, v * 2 * PAIRS)
                for k in range(KC):
                    mm = pe.matmul(B[5][0:QC, 0:2 * P], WDQ[:, k, :], XTG[:, k, :], start=(k == 0), stop=(k == KC - 1))
                mm.then_inc(t_qc, 1)

            def up(p):
                def stage(v, par):
                    pe.wait_ge(t_qclo, v + 1)
                    n = v * PAIRS + p
                    if n >= 2:
                        pe.wait_ge(t_absc, 2 * (n - 1))
                        pe.wait_ge(t_rvm, 2 * (n - 1))
                    outs = v * 2 - (4 if p == 0 else 3)
                    if p % 2 == 0 and outs > 0:
                        pe.wait_ge(t_oc, outs)
                    three_passes(absorbed_bank(p)[:, 0:2 * P], [(AHI[:, p, 0, :], ALO[:, p, 0, :], QCHI[:, :], QCLO[:, :])])\
                        .then_inc(t_abs, 1)
                    for w in (1, 2):
                        mm = three_passes(rope_bank(p)[:, (w - 1) * 2 * P:w * 2 * P],
                                          [(AHI[:, p, w, :], ALO[:, p, w, :], QCHI[:, :], QCLO[:, :])])
                    mm.then_inc(t_rv, 1)
                return stage

            def score(i, r, u, o):
                pe.wait_ge(t_absc, u * 2 * PAIRS + 2 * PAIRS)
                pe.wait_ge(t_q, u * 2 * PAIRS + 2 * PAIRS)
                pe.wait_ge(t_kl[r], 16 * (i // 4 + 1) if isinstance(i, int) else (i - r) * 4 + 16)
                if at_least(i, 1):
                    pe.wait_ge(t_masked, i * 2)
                for head in range(HEADS):
                    for b in range(2):
                        mm = pe.matmul(B[head // 8][b * 64:(b + 1) * 64, head % 8 * SEQ:(head % 8 + 1) * SEQ],
                                       Q[:, r // 2, head, o * P + b * 64:o * P + (b + 1) * 64],
                                       KR[:, r, head % 2, b * SEQ:(b + 1) * SEQ], start=True, stop=True)
                    if head % 8 == 7:
                        mm.then_inc(t_s, 1)

            def probs_t(i, r, u, o):
                pe.wait_ge(t_prob, i + 1)
                if at_least(i, 1):
                    pe.wait_ge(t_ctlo, i * 2)
                for n in range(2):
                    for h in range(4):
                        tr = pe.transpose(B[2 + n][:, h * P:(h + 1) * P],
                                          SM[:, r % 2, 8 * n + 2 * h:8 * n + 2 * h + 2, :].rearrange("p h n -> p (h n)"),
                                          ident)
                    tr.then_inc(t_pt, 1)

            def context(i, r, u, o):
                pe.wait_ge(t_ptc, i * 2 + 2)
                for b in range(2):
                    pe.matmul(B[2 + b][:, :], KR[:, r, 2 + b, :], PT[:, :, b * 64:(b + 1) * 64], start=True, stop=True)\
                        .then_inc(t_ct, 1)

            def out(i, r, u, o):
                pe.wait_ge(t_ctlo, i * 2 + 2)
                if at_least(i, 1):
                    pe.wait_ge(t_oc, i)
                copied = u * 2 * PAIRS + (34 if o == 0 else 46)
                pe.wait_ge(t_absc, min(copied, TILES * PAIRS) if isinstance(i, int) else copied)
                three_passes(B[6][:, 2 * P:], [(CTHI[:, p, :], CTLO[:, p, :], BHI[:, p, :], BLO[:, p, :])
                                               for p in range(PAIRS)]).then_inc(t_o, 1)

            def step(i, j, h):
                if j % 2:
                    pair(i, j, h, 3, down)
                    tile(i, j, h, 1, score)
                    tile(i, j, h, 0, probs_t)
                    pair(i, j, h, 3, up(0))
                    tile(i, j, h, -1, out)
                    pair(i, j, h, 3, up(1))
                    tile(i, j, h, 0, context)
                    pair(i, j, h, 3, up(2))
                    pair(i, j, h, 3, up(3))
                else:
                    tile(i, j, h, 1, score)
                    pair(i, j, h, 2, up(4))
                    pair(i, j, h, 2, up(5))
                    tile(i, j, h, 0, probs_t)
                    pair(i, j, h, 2, up(6))
                    tile(i, j, h, -1, out)
                    pair(i, j, h, 2, up(7))
                    pair(i, j, h, 4, transpose_pair)
                    tile(i, j, h, 0, context)

            tile_loop(step)
            gate(L1)
            counts(L1)
            shared(L1)
            pe.wait_ge(L1.shadd, 2 * TILES)
            pe.wait_ge(L1.eid, 2)
            slots(L1)

        @block.vector
        def _(dve):
            ch = Count(dve, s_dve)
            mk = ch.mark

            def moments(src, t0, t1):
                for t in range(t0, t1):
                    mk(dve.bn_stats(STAT[:, t, :], src[:, t, :]))
                ch.wait()
                for t in range(t0, t1):
                    mk(dve.bn_aggr(MV[:, t, :], STAT[:, t, :]))

            def variances(t0, t1):
                ch.wait()
                dve.tensor_scalar(SD[:, t0:t1], MV[:, t0:t1, 1], LN_EPS, None, ALU.add).then_inc(s_var, 1)

            def stats(src, g):
                moments(src, g * GT, (g + 1) * GT)
                variances(g * GT, (g + 1) * GT)

            def inverse(n, t0, t1):
                s = slice(t0, t1)
                dve.wait_ge(s_sd, n + 1)
                mk(dve.reciprocal(RSTD[:, s], SD[:, s]))
                ch.wait()
                dve.scalar_tensor_tensor(out=SHIFT[:, s], in0=MV[:, s, 0], scalar=-1.0, in1=RSTD[:, s],
                                         op0=ALU.mult, op1=ALU.mult).then_inc(s_rstd, 1)

            def rstd(n, g):
                inverse(n * GROUPS + g, g * GT, (g + 1) * GT)

            def route(M, SC, weights):
                E, TOP, R = M.E, M.top, M.R
                for t in range(TILES):
                    mk(dve.max(TOPW[:, t, :], SC[:, t, :]))
                ch.wait()
                for t in range(TILES):
                    mk(dve.max_index(TOPI[:, t, :], TOPW[:, t, :], SC[:, t, :]))
                ch.wait()
                IDX = R[5][:, 0:8, :].rearrange("p a b -> p (a b)").rearrange("p (t k) -> p t k", k=8)
                mk(dve.tensor_copy(IDX, TOPI[:, :, :]))
                weights()
                ch.wait()
                eid = const("expert_id")[:, 0:E].unsqueeze(1).to_broadcast([P, TILES, E])
                OH = [R[i][:, :, 0:E] for i in range(TOP)]
                for k in range(TOP):
                    mk(dve.tensor_tensor(OH[k], IDX[:, :, k:k + 1].to_broadcast([P, TILES, E]), eid, ALU.is_equal))
                ch.wait()
                acc = R[4][:, :, 0:E]
                mk(dve.tensor_tensor(acc, OH[0], OH[1], ALU.add))
                for k in range(2, TOP):
                    ch.wait()
                    mk(dve.tensor_tensor(acc, acc, OH[k], ALU.add))
                ch.wait()
                dve.tensor_copy(SEL[:, :, 0:E], acc).then_inc(M.sel, 1)
                dve.wait_ge(M.counts, 1)
                CNT = R[5][:, :, :].rearrange("p a b -> p (a b)")[:, 0:E * TILES].rearrange("p (e t) -> p e t", t=TILES)
                INC = R[6][:, :, :].rearrange("p a b -> p (a b)")[:, 0:E * TILES].rearrange("p (e t) -> p e t", t=TILES)
                mk(dve.tensor_copy(CNT, B[5][:, 0:256].rearrange("p (t e) -> p e t", e=16)[:, 0:E, :]))
                ch.wait()
                mk(dve.tensor_tensor_scan(INC.rearrange("p e t -> p (e t)"), const("keep")[:, 0:E * TILES],
                                          CNT.rearrange("p e t -> p (e t)"), 0.0, ALU.mult, ALU.add))
                ch.wait()
                n, cum, base = SMALL[:, 0, 0:E], SMALL[:, 1, 0:E], SMALL[:, 2, 0:E]
                mk(dve.tensor_scalar(SMALLI[:, 0:E], INC[:, :, TILES - 1], float(P - 1), None, ALU.add))
                ch.wait()
                mk(dve.tensor_scalar(SMALLI[:, 0:E], SMALLI[:, 0:E], 7, None, ALU.arith_shift_right))
                ch.wait()
                mk(dve.tensor_copy(n, SMALLI[:, 0:E]))
                ch.wait()
                mk(dve.tensor_tensor_scan(cum, ONE64[:, 0:E], n, 0.0, ALU.mult, ALU.add))
                ch.wait()
                mk(dve.tensor_tensor(base, cum, n, ALU.subtract))
                ch.wait()
                mk(dve.tensor_scalar(base, base, float(P), None, ALU.mult))
                mk(dve.tensor_tensor(INC, INC, CNT, ALU.subtract))
                ch.wait()
                POS = R[7][:, :, 0:E]
                mk(dve.tensor_tensor(POS, INC.rearrange("p e t -> p t e"), base.unsqueeze(1).to_broadcast([P, TILES, E]),
                                     ALU.add))
                ch.wait()
                dve.tensor_tensor(POS, POS, B[4][:, 0:256].rearrange("p (t e) -> p t e", e=16)[:, :, 0:E], ALU.add)\
                    .then_inc(M.routed, 1)
                dve.wait_ge(M.routed, 1)
                for k in range(TOP):
                    mk(dve.tensor_tensor(OH[k], OH[k], POS, ALU.mult))
                ch.wait()
                PK = R[4][:, 0:4, :]
                for k in range(TOP):
                    mk(dve.tensor_reduce(PK[:, k, :], OH[k], AX.X, ALU.add))
                ch.wait()
                dve.tensor_copy(POSI[:, 0:TOP, :], PK[:, 0:TOP, :]).then_inc(M.pos, 1)
                slots = M.slots
                CMP = M.XCMP[0:1, 0:slots * E].rearrange("p (s e) -> p s e", e=E)
                mk(dve.tensor_tensor(CMP, cum[0:1, :].unsqueeze(1).to_broadcast([1, slots, E]),
                                     const("slot_id")[0:1, 0:slots].unsqueeze(2).to_broadcast([1, slots, E]), ALU.is_le))
                ch.wait()
                row = M.XCMP[0:1, slots * E:slots * E + slots]
                mk(dve.tensor_reduce(row, CMP, AX.X, ALU.add))
                ch.wait()
                mk(dve.tensor_scalar(EIDW[0:1, 0:slots], row, float(E - 1), float(M.expert0 + 1), ALU.min, ALU.add))
                dve.tensor_scalar(row, row, float(E - 1), float(M.cols), ALU.min, ALU.mult).then_inc(M.eid, 1)
                dve.wait_ge(M.eid, 1)
                ch.wait()
                dve.tensor_copy(EID[0:1, 0:slots], row).then_inc(M.eid, 1)

            def shared(M, scale):
                dve.wait_ge(M.shsplit, 2 * M.n + 1)
                dve.tensor_tensor(M.SHLO[:, :], M.SHRAW[:, :], M.SHHI[:, :].bitcast(F32), ALU.subtract)\
                    .then_inc(M.shsplit, 1)
                for g in range(GROUPS):
                    dve.wait_ge(M.shx, 2 * (M.n * GROUPS + g) + 1)
                    dve.tensor_tensor(M.XSLO[:, :, :], M.XT[:, :, g * GTOK:(g + 1) * GTOK], M.XSHI[:, :, :].bitcast(F32),
                                      ALU.subtract).then_inc(M.shx, 1)
                    for c in range(M.shc):
                        n = g * M.shc + c
                        dve.wait_ge(M.shs, M.chunk0 + n + 1)
                        if n >= 2:
                            dve.wait_ge(M.shl, M.chunk0 + n - 1)
                            dve.wait_ge(M.shg, M.chunk0 + n - 1)
                        dve.tensor_tensor(M.SU[:, n % 2, :], M.SSIL[:, n % 2, :], B[2 * (n % 2) + 1][:, :], ALU.mult)\
                            .then_inc(M.shu, 1)
                        dve.wait_ge(M.shg, M.chunk0 + n + 1)
                        dve.wait_ge(M.shu, M.chunk0 + n + 1)
                        dve.tensor_tensor(M.SGLO[:, c, :], M.SU[:, n % 2, :], M.SGHI[:, c, :].bitcast(F32), ALU.subtract)\
                            .then_inc(M.shl, 1)
                    for t in range(g * GT, (g + 1) * GT):
                        dve.wait_ge(M.shy, M.n * TILES + t + 1)
                        dve.scalar_tensor_tensor(out=X[:, t, :], in0=B[4 + t % 2][:, 0:D], scalar=scale(t),
                                                 in1=X[:, t, :], op0=ALU.mult, op1=ALU.add).then_inc(M.shadd, 1)

            def split_lo(M, experts):
                for e in experts:
                    dve.wait_ge(M.split, (EARLY0 if M.n else 0) + e + 1)
                    dve.tensor_tensor(M.WLO[:, e, :], M.WRAW[e][:, :], M.WHI[:, e, :].bitcast(F32), ALU.subtract)\
                        .then_inc(M.wready, 1)

            def slots(M):
                def lo(i, j):
                    dve.wait_ge(M.a_xhi, i + (M.slot0 + 1))
                    dve.tensor_tensor(M.XLO[:, j % 2, :], B[j % 2][:, 0:D], M.XHI[:, j % 2, :].bitcast(F32), ALU.subtract)\
                        .then_inc(M.d_xlo, 1)

                def g_(i, j):
                    dve.wait_ge(M.a_sil, i + (M.slot0 + 1))
                    if at_least(i, 2):
                        dve.wait_ge(M.p_gt, i + (M.slot0 - 1))
                    dve.tensor_tensor(M.G[:, j % 2, 0:M.hid], M.SIL[:, j % 2, :], B[2 + j % 2][:, M.hid:M.w13], ALU.mult)\
                        .then_inc(M.d_g, 1)

                def glo(i, j):
                    dve.wait_ge(M.a_ghi, i + (M.slot0 + 1))
                    dve.tensor_tensor(M.GLO[:, j % 2, :], B[4 + j % 2][:, 0:M.hchunks * P], M.GHI[:, j % 2, :].bitcast(F32),
                                      ALU.subtract).then_inc(M.d_glo, 1)

                def step(i, j):
                    run_stages(i, j, M.slots, ((2, lo), (1, g_), (0, glo)))

                slot_loop(dve, M.slots, step, 2, 1)

            def combine(M, t):
                for k in range(M.top):
                    n = M.copy0 + t * M.top + k
                    dve.wait_ge(M.gath[n % 8], 16 * (n // 8 + 1))
                    if n:
                        dve.wait_ge(M.comb, n)
                    dve.scalar_tensor_tensor(out=X[:, t, :], in0=M.GB[:, n % 8, :], scalar=WK[:, k, t:t + 1],
                                             in1=X[:, t, :], op0=ALU.mult, op1=ALU.add).then_inc(M.comb, 1)

            mk(dve.memset(ONES[:, :], 1.0))
            mk(dve.memset(SEL[:, :, :], 0.0))
            dve.wait_ge(s_const, 16)
            mk(dve.tensor_copy(TRI[:, :], const("before")))
            for g in range(GROUPS):
                dve.wait_ge(s_x[g], 16)
                stats(X, g)
            for g in range(GROUPS):
                rstd(0, g)
            dve.wait_ge(s_act, 3)
            dve.wait_ge(s_zero, 2)
            mk(dve.tensor_tensor_scan(EMA[:, :], PAR[:, KEEP:KEEP + 1].to_broadcast([P, SEQ]), ONE64[:, :], 0.0,
                                      ALU.mult, ALU.add))
            ch.wait()
            mk(dve.tensor_scalar(EMAC[:, :], EMA[:, SEQ - 1::-1], 1.0 / SEQ, None, ALU.mult))
            ch.wait()
            mk(dve.tensor_reduce(PAR[:, CTOT:CTOT + 1], EMAC[:, :], AX.X, ALU.add))
            ch.wait()
            mk(dve.tensor_scalar(PAR[:, BC:BC + KC], BIN[:, :], PAR[:, CTOT:CTOT + 1], None, ALU.mult))
            for k in range(KC):
                dve.wait_ge(s_ctx[k], 16)
                ch.wait()
                if k:
                    dve.wait_ge(s_csum, k)
                mk(dve.tensor_tensor(CTXW[:, :].rearrange("p (b s) -> p b s", s=SEQ),
                                     CTX[:, k, :].rearrange("p (b s) -> p b s", s=SEQ),
                                     EMAC[:, :].unsqueeze(1).to_broadcast([P, BATCH, SEQ]), ALU.mult))
                ch.wait()
                dve.tensor_reduce(CSUM[:, k, :], CTXW[:, :].rearrange("p (b s) -> p b s", s=SEQ), AX.X, ALU.add)\
                    .then_inc(s_csum, 1)
            dve.wait_ge(s_wio, 16 * 6)
            mk(dve.tensor_scalar(GAMMA[:, :], GAMMA[:, :], PAR[:, TX:TX + 1], None, ALU.mult))
            dve.tensor_scalar(BETA[:, :], BETA[:, :], PAR[:, TX:TX + 1], None, ALU.mult).then_inc(s_beta, 1)
            dve.wait_ge(s_ema, 1)
            ch.wait()
            for j in range(KC):
                dve.tensor_scalar(M1T[:, j, :], B[0][:, j * BATCH:(j + 1) * BATCH], PAR[:, BC + j:BC + j + 1], None,
                                  ALU.add).then_inc(s_ema, 1)
            dve.wait_ge(s_ema, 2 + KC)
            dve.tensor_tensor(SUMM[:, :], B[1][0:BATCH, 0:D], BOUT[0:BATCH, :], ALU.add).then_inc(s_ema, 1)
            for g in range(GROUPS):
                for t in range(g * GT, (g + 1) * GT):
                    dve.wait_ge(s_norm, t + 1)
                    dve.wait_ge(s_spread, t + 1)
                    dve.tensor_tensor(XN[:, t, :], XN[:, t, :], B[2 + t % 6][:, 0:D], ALU.add).then_inc(s_spused, 1)
                dve.wait_ge(s_spused, (g + 1) * GT)
                stats(XN, g)
                if g:
                    rstd(1, g - 1)
            rstd(1, GROUPS - 1)
            for g in range(GROUPS):
                for t in range(g * GT, (g + 1) * GT):
                    dve.wait_ge(s_norm, TILES + t + 1)
                    mk(dve.tensor_tensor(XN[:, t, :], XN[:, t, :], GAMMA[:, :], ALU.mult))
                ch.wait()
                for t in range(g * GT, (g + 1) * GT):
                    dve.wait_ge(s_xb, t + 1)
                    mk(dve.tensor_tensor(X[:, t, :], X[:, t, :], XN[:, t, :], ALU.add))
                ch.wait()
                stats(X, g)
                if g:
                    rstd(2, g - 1)
            rstd(2, GROUPS - 1)
            R256 = L0.R
            dve.wait_ge(L0.lgt, TILES)
            LG = B[3][:, 0:256].rearrange("p (t e) -> p t e", e=E0)
            mx, inv = SMALL[:, 0, :], SMALL[:, 1, :]
            mk(dve.tensor_reduce(mx, LG, AX.X, ALU.max))
            ch.wait()
            dve.tensor_tensor(R256[0][:, :, :], LG, mx.unsqueeze(2).to_broadcast([P, TILES, E0]), ALU.subtract)\
                .then_inc(L0.shifted, 1)
            dve.wait_ge(L0.exped, 1)
            mk(dve.tensor_reduce(mx, R256[0][:, :, :], AX.X, ALU.add))
            ch.wait()
            mk(dve.reciprocal(inv, mx))
            ch.wait()
            mk(dve.tensor_tensor(R256[1][:, :, :], R256[0][:, :, :], inv.unsqueeze(2).to_broadcast([P, TILES, E0]), ALU.mult))
            ch.wait()
            gm = SMALL[:, 2:6, :].rearrange("p a b -> p (a b)").rearrange("p (t g) -> p t g", g=EGROUPS)
            mk(dve.tensor_reduce(gm, R256[1][:, :, :].rearrange("p t (g i) -> p (t g) i", i=EPG), AX.X, ALU.max))
            ch.wait()
            R4 = R256[2][:, :, :].rearrange("p t (j i) -> p t j i", i=EGROUPS)
            mk(dve.tensor_tensor(R4, gm.unsqueeze(2).to_broadcast([P, TILES, EGROUPS, EGROUPS]),
                                 gm.unsqueeze(3).to_broadcast([P, TILES, EGROUPS, EGROUPS]), ALU.is_ge))
            ch.wait()
            mk(dve.tensor_tensor(R256[3][:, :, :], R256[2][:, :, :],
                                 const("earlier_group").unsqueeze(1).to_broadcast([P, TILES, 16]), ALU.mult))
            ch.wait()
            ra = R256[4][:, 0:4, :].rearrange("p a b -> p (a b)").rearrange("p (t g) -> p t g", g=EGROUPS)
            rb = R256[4][:, 4:8, :].rearrange("p a b -> p (a b)").rearrange("p (t g) -> p t g", g=EGROUPS)
            R4b = R256[3][:, :, :].rearrange("p t (j i) -> p t j i", i=EGROUPS)
            mk(dve.tensor_reduce(ra, R4b, AX.X, ALU.add))
            mk(dve.tensor_reduce(rb, R4b.rearrange("p t j i -> p t i j"), AX.X, ALU.add))
            ch.wait()
            mk(dve.tensor_tensor(ra, ra, rb, ALU.subtract))
            ch.wait()
            mk(dve.tensor_tensor(ra, ra, const("later_groups").unsqueeze(1).to_broadcast([P, TILES, EGROUPS]), ALU.add))
            ch.wait()
            mk(dve.tensor_scalar(ra, ra, TOPG - 0.5, None, ALU.is_lt))
            ch.wait()
            mk(dve.tensor_scalar(rb, ra, 1.0, None, ALU.subtract))
            by_group = "p t (g i) -> p (t g) i"
            mk(dve.tensor_tensor(R256[2][:, :, :].rearrange(by_group, i=EPG), R256[1][:, :, :].rearrange(by_group, i=EPG),
                                 ra.rearrange("p t g -> p (t g)").unsqueeze(2).to_broadcast([P, TILES * EGROUPS, EPG]),
                                 ALU.mult))
            ch.wait()
            mk(dve.tensor_tensor(R256[0][:, :, :].rearrange(by_group, i=EPG), R256[2][:, :, :].rearrange(by_group, i=EPG),
                                 rb.rearrange("p t g -> p (t g)").unsqueeze(2).to_broadcast([P, TILES * EGROUPS, EPG]),
                                 ALU.add))
            ch.wait()

            def weights0():
                mk(dve.tensor_scalar(WK[:, :, :], TOPW[:, :, 0:4].rearrange("p t k -> p k t"), PAR[:, TF:TF + 1], None,
                                     ALU.mult))

            route(L0, R256[0][:, :, 0:E0], weights0)
            shared(L0, lambda t: PAR[:, TF:TF + 1])
            split_lo(L0, range(EARLY0))
            dve.wait_ge(L0.scat, 16 * TILES * TOP0)
            mk(dve.memset(L0.G[:, :, :], 0.0))
            ch.wait()
            slots(L0)
            dve.wait_ge(L0.p_y, SLOTS0)
            dve.wait_ge(L0.wready, E0)
            mk(dve.memset(KB[:, :, 2:4, :], 0.0))
            dve.wait_ge(k_wkv, 16 * 4)
            mk(dve.tensor_copy(SEG[:, :], ITOK[:, :]))
            ch.wait()
            seen = XNG[:, :, :, :].rearrange("p a b d -> p (a b d)").rearrange("p (t s) -> p t s", s=SEQ)
            mk(dve.tensor_tensor(MASK[:, :, :], const("key_id").unsqueeze(1).to_broadcast([P, TILES, SEQ]),
                                 SEG[:, :].unsqueeze(2).to_broadcast([P, TILES, SEQ]), ALU.subtract))
            ch.wait()
            mk(dve.tensor_scalar(seen, MASK[:, :, :], float(-LOOKBACK), None, ALU.is_ge))
            ch.wait()
            mk(dve.tensor_scalar(MASK[:, :, :], MASK[:, :, :], 0.0, None, ALU.is_le))
            ch.wait()
            mk(dve.tensor_tensor(MASK[:, :, :], MASK[:, :, :], seen, ALU.mult))
            ch.wait()
            mk(dve.tensor_scalar(MASK[:, :, :], MASK[:, :, :], -1.0, NEG, ALU.add, ALU.mult))
            ch.wait()
            for n in range(GROUPS):
                dve.wait_ge(k_tok, n + 1)
                for b in range(2):
                    for h in range(2):
                        src = B[4 + n][b * 64:(b + 1) * 64, :].rearrange("p (t n) -> p t n", n=P)[:, :, 0:KVC]
                        dve.tensor_copy(KB[h * 64:(h + 1) * 64, n * GT:(n + 1) * GT, 2 + b, h * 64:(h + 1) * 64], src)\
                            .then_inc(k_tokc, 1)
            RC5 = RC[:, 0:2, :].rearrange("p a n -> p (a n)")
            RS5 = RS[:, 0:2, :].rearrange("p a n -> p (a n)")
            for n in range(GROUPS):
                dve.wait_ge(k_rope, n + 1)
                if n:
                    dve.wait_ge(k_roped, 2 * n)
                for dst, src, table in ((RC5, B[n], "cos"), (RS5, B[4 + n], "sin")):
                    dve.tensor_tensor(dst.rearrange("p (b s) -> p b s", s=SEQ), src[:, :].rearrange("p (b s) -> p b s", s=SEQ),
                                      const(table).unsqueeze(1).to_broadcast([P, 8, SEQ]), ALU.mult).then_inc(k_ropem, 1)
                dve.wait_ge(k_ropem, 2 * n + 2)
                for half, which in ((64, 0), (0, 1)):
                    s = slice(half, half + 64)
                    dve.tensor_tensor(KB[s, n * GT:(n + 1) * GT, which, :], RC5[s, :].rearrange("p (t n) -> p t n", n=P),
                                      RS5[s, :].rearrange("p (t n) -> p t n", n=P), ALU.add).then_inc(k_roped, 1)
            dve.wait_ge(k_hi, 1)
            dve.tensor_tensor(ALO[:, :, 1:3, :], ARAW[:, :, 1:3, :], AHI[:, :, 1:3, :].bitcast(F32), ALU.subtract)\
                .then_inc(k_lo, 1)
            for n in range(2):
                dve.wait_ge(k_hi, n + 2)
                dve.tensor_tensor(ALO[:, 4 * n:4 * n + 4, 0, :], B[n][0:QC, :].rearrange("p (h n) -> p h n", n=P),
                                  AHI[:, 4 * n:4 * n + 4, 0, :].bitcast(F32), ALU.subtract).then_inc(k_lo, 1)
            for n in range(4):
                dve.wait_ge(k_hi, n + 4)
                dve.tensor_tensor(BLO[:, 2 * n:2 * n + 2, :], B[2 + n][:, :].rearrange("p (h n) -> p h n", n=D),
                                  BHI[:, 2 * n:2 * n + 2, :].bitcast(F32), ALU.subtract).then_inc(k_lo, 1)

            def combine_tile(t, r, u, o):
                combine(L0, t)
                dve.wait_ge(L0.comb, (t + 1) * TOP0)
                moments(X, t, t + 1)
                if o:
                    variances(t - 1, t + 1)

            def inverse_pair(v, par):
                inverse(3 * GROUPS + v, 2 * v, 2 * v + 2)

            def mask(i, r, u, o):
                if at_least(i, 2):
                    dve.wait_ge(t_pt, i * 2 - 2)
                for n in range(2):
                    dve.wait_ge(t_s, i * 2 + (n + 1))
                    dve.tensor_tensor(SM[:, r % 2, 8 * n:8 * n + 8, :], B[n][:, :].rearrange("p (h n) -> p h n", n=SEQ),
                                      MASK[:, bass.ds(i, 1), :].to_broadcast([P, 8, SEQ]), ALU.add).then_inc(t_masked, 1)
                dve.wait_ge(t_masked, i * 2 + 2)
                dve.tensor_reduce(SMX[:, r % 2, 0, :], SM[:, r % 2, :, :], AX.X, ALU.max).then_inc(t_max, 1)

            def row_sum(i, r, u, o):
                dve.wait_ge(t_exp, i + 1)
                dve.tensor_reduce(SMX[:, r % 2, 1, :], SM[:, r % 2, :, :], AX.X, ALU.add).then_inc(t_sum, 1)
                dve.wait_ge(t_sum, i + 1)
                dve.reciprocal(SMX[:, r % 2, 1, :], SMX[:, r % 2, 1, :]).then_inc(t_rec, 1)
                dve.wait_ge(t_rec, i + 1)
                dve.tensor_tensor(SM[:, r % 2, :, :], SM[:, r % 2, :, :],
                                  SMX[:, r % 2, 1, :].unsqueeze(2).to_broadcast([P, HEADS, SEQ]), ALU.mult)\
                    .then_inc(t_prob, 1)

            def qc_lo(v, par):
                dve.wait_ge(t_qchi, v + 1)
                dve.tensor_tensor(QCLO[:, :], B[5][0:QC, 0:2 * P], QCHI[:, :].bitcast(F32), ALU.subtract).then_inc(t_qclo, 1)

            def terms(p):
                def stage(v, par):
                    dve.wait_ge(t_rv, v * PAIRS + (p + 1))
                    n = v * PAIRS + p
                    if n >= RINGQ:
                        dve.wait_ge(t_q, 2 * (n - RINGQ + 1))
                    for w, dst, table in ((0, RC, "cos"), (1, RS, "sin")):
                        dve.tensor_tensor(dst[:, n % RINGQ, :].rearrange("p (b s) -> p b s", s=SEQ),
                                          rope_bank(p)[:, w * 2 * P:(w + 1) * 2 * P].rearrange("p (b s) -> p b s", s=SEQ),
                                          const(table).unsqueeze(1).to_broadcast([P, 4, SEQ]), ALU.mult).then_inc(t_rvm, 1)
                return stage

            def ct_lo(i, r, u, o):
                for b in range(2):
                    dve.wait_ge(t_cthi, i * 2 + (b + 1))
                    dve.tensor_tensor(CTLO[:, :, b * 64:(b + 1) * 64], B[2 + b][:, :].rearrange("p (h n) -> p h n", n=64),
                                      CTHI[:, :, b * 64:(b + 1) * 64].bitcast(F32), ALU.subtract).then_inc(t_ctlo, 1)

            def step(i, j, h):
                if j % 2:
                    pair(i, j, h, 3, qc_lo)
                    tile(i, j, h, 1, mask)
                    pair(i, j, h, 3, terms(0))
                    pair(i, j, h, 5, inverse_pair)
                    pair(i, j, h, 3, terms(1))
                    tile(i, j, h, 1, row_sum)
                    tile(i, j, h, 0, ct_lo)
                    pair(i, j, h, 3, terms(2))
                    pair(i, j, h, 3, terms(3))
                else:
                    tile(i, j, h, 1, mask)
                    pair(i, j, h, 2, terms(4))
                    pair(i, j, h, 2, terms(5))
                    pair(i, j, h, 2, terms(6))
                    tile(i, j, h, 1, row_sum)
                    pair(i, j, h, 2, terms(7))
                    tile(i, j, h, 0, ct_lo)
                tile(i, j, h, 7, combine_tile)

            tile_loop(step)
            dve.wait_ge(t_x, TILES)
            for g in range(GROUPS):
                stats(X, g)
                if g:
                    inverse(L1.var0 + g - 1, (g - 1) * GT, g * GT)
            inverse(L1.var0 + GROUPS - 1, TILES - GT, TILES)
            dve.wait_ge(L1.lgt, 2 * TILES)
            dve.tensor_copy(L1.R[0][:, :, 0:E1 + 1], B[3][:, 0:256].rearrange("p (t e) -> p t e", e=16)[:, :, 0:E1 + 1])\
                .then_inc(L1.shifted, 1)
            dve.wait_ge(L1.exped, 1)
            mk(dve.tensor_scalar(SGATE[:, :], SGATE[:, :], PAR[:, TF + 1:TF + 2], None, ALU.mult))
            ch.wait()

            def weights1():
                dve.tensor_tensor(SMALL[:, 5, :], TOPW[:, :, 1], TOPW[:, :, 0], ALU.subtract).then_inc(L1.shifted, 1)
                dve.wait_ge(L1.exped, 2)
                mk(dve.tensor_scalar(SMALL[:, 5, :], SMALL[:, 6, :], 1.0, None, ALU.add))
                ch.wait()
                mk(dve.reciprocal(SMALL[:, 5, :], SMALL[:, 5, :]))
                ch.wait()
                mk(dve.tensor_scalar(WK[:, 0, :], SMALL[:, 5, :], PAR[:, TF + 1:TF + 2], None, ALU.mult))
                ch.wait()
                mk(dve.tensor_tensor(WK[:, 1, :], WK[:, 0, :], SMALL[:, 6, :], ALU.mult))

            route(L1, L1.R[0][:, :, 0:E1], weights1)
            shared(L1, lambda t: SGATE[:, t:t + 1])
            split_lo(L1, range(E1))
            slots(L1)
            for t in range(TILES):
                combine(L1, t)


def host_layout(v):
    f = {k: np.asarray(x) for k, x in v.items()}
    c, select = constants()
    o = {"const": c, "select": select}
    o["x"] = f["x"].reshape(TOKENS, D)
    o["ctxT"] = f["ctx_2048"].reshape(TOKENS, D).T
    o["decay"] = f["L0_xattn_decay"].reshape(1, 1)
    o["g_xattn"] = f["g_xattn"].reshape(1, 2)
    o["g_ffn"] = f["g_ffn"].reshape(1, 2)
    o["W_inT"] = f["L0_xattn_W_in"].T
    o["W_outT"] = f["L0_xattn_W_out"].T
    o["b_in"] = f["L0_xattn_b_in"].reshape(KC, P).T
    o["b_out"] = f["L0_xattn_b_out"].reshape(1, D)
    o["gamma"] = f["L0_xattn_gamma"].reshape(1, D)
    o["beta"] = f["L0_xattn_beta"].reshape(1, D)
    o["Wg0T"] = f["L0_ffn_Wg"].T

    def chunks(w):
        r, n = w.shape
        k = -(-r // P)
        z = np.zeros((k * P, n), w.dtype)
        z[:r] = w
        return z.reshape(k, P, n).transpose(1, 0, 2).reshape(P, k * n)

    def wide(w, n):
        z = np.zeros((w.shape[0], n), w.dtype)
        z[:, :w.shape[1]] = w
        return z

    o["w0"] = np.stack([np.concatenate([
        chunks(np.concatenate([f["L0_ffn_W1"][e].T, f["L0_ffn_W3"][e].T], 1)), chunks(f["L0_ffn_W2"][e].T)], 1)
        for e in range(E0)])
    o["sh0"] = np.concatenate([chunks(wide(f["L0_ffn_Ws1"].T, SH0)), chunks(wide(f["L0_ffn_Ws3"].T, SH0)),
                               chunks(f["L0_ffn_Ws2"].T)], 1)
    o["seg"] = f["itok_BxS_0_1023"].reshape(TILES, P).T
    o["W_kvc2"] = chunks(np.concatenate([f["L1_xattn_W_kvc"]] * 2, 1))
    swap = np.arange(ROPE).reshape(2, ROPE // 2)[::-1].reshape(-1)
    kr = f["L1_xattn_W_kr"]
    o["W_kr2"] = np.concatenate([kr, kr, kr[:, swap], kr[:, swap]], 1)
    o["W_dq"] = chunks(f["L1_xattn_W_dq"])
    qr = f["L1_xattn_W_qr"].reshape(QC, PAIRS, 2, ROPE)[:, :, ::-1]
    o["W_qrv"] = np.stack([qr, qr[..., swap]], 2).reshape(QC, PAIRS * 2 * P)
    for n in ("uq", "uk", "uv"):
        w = f["L1_xattn_W_" + n]
        o[f"W_{n}T"] = w.reshape(w.shape[0], HEADS, HD).transpose(2, 1, 0).reshape(HD, -1)
    o["W_oh"] = f["L1_xattn_W_o"].reshape(HEADS, HD, D).transpose(1, 0, 2).reshape(HD, HEADS * D)
    o["Wg1T"] = np.concatenate([f["L1_ffn_gate_w"], f["L1_ffn_se_gate_w"]], 0).T
    o["w1"] = np.stack([np.concatenate([
        chunks(np.concatenate([f["L1_ffn_w_gate"][e].T, f["L1_ffn_w_up"][e].T], 1)), chunks(f["L1_ffn_w_down"][e].T)], 1)
        for e in range(E1)])
    o["sh1"] = np.concatenate([chunks(f["L1_ffn_sh_gate"].T), chunks(f["L1_ffn_sh_up"].T),
                               chunks(f["L1_ffn_sh_down"].T)], 1)
    return {k: np.ascontiguousarray(x) for k, x in o.items()}


def kernel(**inputs):
    import concourse.bacc as bacc
    from concourse.bass_utils import run_bass_kernel_spmd

    arrays = host_layout(inputs)
    nc = bacc.Bacc("TRN2", target_bir_lowering=False, num_devices=1)
    aps = {n: nc.dram_tensor(n, x.shape, mybir.dt.from_np(x.dtype), kind="ExternalInput").ap() for n, x in arrays.items()}
    aps["out"] = nc.dram_tensor("out", (TOKENS, D), F32, kind="ExternalOutput").ap()
    build_program(nc, aps)
    r = run_bass_kernel_spmd(nc, [arrays], core_ids=[0])
    return np.asarray(r.results[0]["out"]).reshape(BATCH, SEQ, D)
```

```python
from contextlib import ExitStack

import numpy as np

import concourse.bass as bass
from concourse import mybir

F32 = mybir.dt.float32
F32R = mybir.dt.float32r
BF16 = mybir.dt.bfloat16
I32 = mybir.dt.int32
U32 = mybir.dt.uint32
ALU = mybir.AluOpType
ACT = mybir.ActivationFunctionType
AX = mybir.AxisListType

P = 128
BATCH, SEQ, D = 32, 64, 256
TOKENS = BATCH * SEQ
TILES = TOKENS // P
KC = D // P
GROUPS = 4
GT = TILES // GROUPS
GTOK = GT * P
LN_EPS = 1e-5

E0, HID0, TOP0, EGROUPS, EPG, TOPG = 16, 176, 4, 4, 4, 2
HID0_REST = HID0 - P
W13_0 = 2 * HID0
COLS0 = KC * W13_0 + 2 * D
SH0 = 384
SHC0 = SH0 // P
SHCOLS0 = 2 * KC * SH0 + SHC0 * D
SLOTS0_NEED = (TOKENS * TOP0 - E0) // P + E0
UNROLL = 4
FIRST = -5
SECOND = -3
BEHIND = 4
AHEAD = 8
RINGQ = 8
XRING, XLEAD = 8, 6
SLOTS0 = -(-SLOTS0_NEED // UNROLL) * UNROLL
EARLY0 = 4
DEAD0 = 4
CTX_PIECES = 8
DEAD0_SLOTS = DEAD0 * (TOKENS // P)
LATE0 = 10
POOLS0 = (4, 8, 12)
DVE_SPLITS1 = 4
LATER0 = LATE0 + 3
E1, HID1, TOP1 = 8, 128, 2
W13_1 = 2 * HID1
COLS1 = KC * W13_1 + D
SH1 = 256
SHC1 = SH1 // P
SHCOLS1 = 2 * KC * SH1 + SHC1 * D
SLOTS1_NEED = (TOKENS * TOP1 - E1) // P + E1
SLOTS1 = -(-SLOTS1_NEED // UNROLL) * UNROLL
HEADS, HD, KVC, QC, ROPE, LOOKBACK = 16, 128, 64, 96, 64, 8
PAIRS = HEADS // 2
NEG = 1e30
SM_SCALE = float(1.0 / np.sqrt(np.float32(HD + ROPE)))

CONST = {}
_at = 0
for _name, _n in (("ident", 128), ("before", 128), ("cos", 64), ("sin", 64), ("key_id", 64),
                  ("keep", 256), ("expert_id", 16), ("earlier_group", 16), ("later_groups", 4),
                  ("slot_id", 80), ("same_head", 128)):
    CONST[_name] = (_at, _at + _n)
    _at += _n
NCONST = _at


def constants():
    c = np.zeros((P, NCONST), np.float32)

    def put(name, value):
        a, b = CONST[name]
        c[:, a:b] = value

    p = np.arange(P)
    put("ident", np.eye(P))
    put("before", p[:, None] < p[None, :])
    half = ROPE // 2
    inv = (1.0 / np.float32(10000.0) ** (np.arange(half, dtype=np.float32) / np.float32(half))).astype(np.float32)
    ang = np.arange(SEQ, dtype=np.float32)[None, :] * inv[p % half][:, None]
    put("cos", np.cos(ang))
    put("sin", np.sin(ang) * np.where(p % ROPE < half, -1.0, 1.0)[:, None])
    put("key_id", np.arange(SEQ)[None, :])
    put("keep", np.arange(256)[None, :] % TILES != 0)
    put("expert_id", np.arange(16)[None, :])
    j = np.arange(16)
    put("earlier_group", (j % 4 < j // 4)[None, :])
    put("later_groups", 3 - np.arange(4)[None, :])
    put("slot_id", np.arange(80)[None, :])
    put("same_head", (p[:, None] // 64) == (p[None, :] // 64))
    select = (np.arange(TOKENS)[None, :] // SEQ == np.arange(BATCH)[:, None]).astype(np.float32)
    return c, select


class Map:

    BASE, END = 16512, 229312

    def __init__(self, nc):
        self.nc, self.at, self.top = nc, self.BASE, self.BASE

    def put(self, name, shape, dtype, at=None):
        size = int(np.prod(shape[1:])) * (2 if dtype == BF16 else 4)
        size = -(-size // 64) * 64
        if at is None:
            at = self.at
            self.at += size
        self.end = at + size
        self.top = max(self.top, self.end)
        assert self.end <= self.END, (name, self.end)
        return self.nc.alloc_sbuf_tensor_at(name, shape, dtype, offset=at)


class Moe:
    pass


def build_program(nc, a):
    ctx = ExitStack()
    with ctx:
        def sem(name):
            return ctx.enter_context(nc.semaphore(name))

        m = Map(nc)
        X = m.put("X", [P, TILES, D], F32)
        C = m.put("C", [P, NCONST], F32)
        PAR = m.put("PAR", [P, 16], F32)
        TRI = m.put("TRI", [P, P], BF16)
        ONES = m.put("ONES", [P, P], BF16)
        SEL = m.put("SEL", [P, TILES, 16], BF16)
        STAT = m.put("STAT", [P, TILES, 6], F32)
        MV = m.put("MV", [P, TILES, 2], F32)
        RSTD = m.put("RSTD", [P, TILES], F32)
        SHIFT = m.put("SHIFT", [P, TILES], F32)
        SD = m.put("SD", [P, TILES], F32)
        TOPW = m.put("TOPW", [P, TILES, 8], F32)
        TOPI = m.put("TOPI", [P, TILES, 8], U32)
        WK = m.put("WK", [P, 4, TILES], F32)
        SGATE = m.put("SGATE", [P, TILES], F32)
        POSI = m.put("POSI", [P, 4, TILES], U32)
        EID = m.put("EID", [1, SLOTS0], I32)
        SMALL = m.put("SMALL", [P, 8, 16], F32)
        SMALLI = m.put("SMALLI", [P, 16], I32)
        ONE64 = m.put("ONE64", [P, SEQ], F32)
        ITOK = m.put("ITOK", [P, TILES], I32)
        SEG = m.put("SEG", [P, TILES], F32)
        phase_base = m.at

        GB_AT = Map.END - 8 * D * 4

        def slot_buffers(M, at):
            q = at
            M.XS = m.put(M.tag + "XS", [P, XRING, D], F32, at=q); q = m.end
            M.XHI = m.put(M.tag + "XHI", [P, 2, D], F32R, at=q); q = m.end
            M.XLO = m.put(M.tag + "XLO", [P, 2, D], F32R, at=q); q = m.end
            M.SIL = m.put(M.tag + "SIL", [P, 2, M.hid], F32, at=q); q = m.end
            M.G = m.put(M.tag + "G", [P, 2, M.hchunks * P], F32, at=q); q = m.end
            M.GHI = m.put(M.tag + "GHI", [P, 2, M.hchunks * P], F32R, at=q); q = m.end
            M.GLO = m.put(M.tag + "GLO", [P, 2, M.hchunks * P], F32R, at=q); q = m.end
            M.YS = m.put(M.tag + "YS", [P, 4, D], F32, at=q); q = m.end
            M.GB = m.put(M.tag + "GB", [P, 8, D], F32, at=GB_AT)
            return q

        both = [sem(name) for name in (
            "xn_transposed", "xn_transpose_copied", "logits_done", "gate_loaded",
            "shared_loaded", "shared_split", "shared_x_hi", "shared_x_lo", "shared_hidden", "shared_silu", "shared_product",
            "shared_hi", "shared_lo", "shared_out", "shared_added", "expert_hi", "expert_weights_ready", "combined",
            "slot_xT", "slot_x_hi", "slot_x_lo", "slot_hidden", "slot_silu", "slot_g", "slot_gT", "slot_g_hi", "slot_g_lo",
            "slot_y", "slot_y_copied")]
        raw = [sem(f"expert{e}_loaded") for e in range(E0)]
        xl = [sem(f"slot_x_loaded{r}") for r in range(XRING)]
        st = [sem(f"slot_y_stored{r}") for r in range(4)]
        gath = [sem(f"gathered{r}") for r in range(8)]

        def moe(tag, before, E, hid, top, slots, shared):
            M = Moe()
            M.tag, M.E, M.hid, M.top, M.slots = tag, E, hid, top, slots
            M.hchunks = -(-hid // P)
            M.w13 = 2 * hid
            M.cols = KC * M.w13 + M.hchunks * D
            M.sh, M.shc = shared, shared // P
            M.x_by_expert = nc.dram_tensor(tag + "x_by_expert", [slots * P, D], F32, kind="Internal").ap()
            M.y_by_expert = nc.dram_tensor(tag + "y_by_expert", [slots * P, D], F32, kind="Internal").ap()
            (M.shifted, M.exped, M.sel, M.counts, M.routed, M.pos, M.eid, M.fill, M.scat) = [sem(tag + name) for name in (
                "scores_shifted", "scores_exp", "choice_ready", "counts_done", "routing_left_psum", "rows_known",
                "slot_experts_known", "rows_cleared", "rows_scattered")]
            (M.xt, M.xtc, M.lgt, M.wg, M.shw, M.shsplit, M.shxh, M.shx, M.shh, M.shs, M.shu, M.shg, M.shl, M.shy,
             M.shadd, M.split, M.wready, M.comb, M.p_xt, M.a_xhi, M.d_xlo, M.p_h, M.a_sil, M.d_g, M.p_gt, M.a_ghi, M.d_glo,
             M.p_y, M.a_y) = both
            M.raw, M.xl, M.st, M.gath = raw, xl, st, gath
            M.n = 1 if before else 0
            M.slot0 = before.slots if before else 0
            M.chunk0 = GROUPS * before.shc if before else 0
            M.expert0 = before.E if before else 0
            M.copy0 = TILES * before.top if before else 0
            return M

        L0 = moe("l0_", None, E0, HID0, TOP0, SLOTS0, SH0)
        L0.norm_base = 2 * TILES
        L0.var0 = 2 * GROUPS
        L0.logits = E0
        L0.WHI = m.put("W0HI", [P, E0, COLS0], F32R)
        w0lo_at = m.at
        L0.WLO = m.put("W0LO", [P, E0, COLS0], F32R)
        L0.WRAW = [m.put(f"W0RAW{e}", [P, COLS0], F32, at=w0lo_at + e * COLS0 * 4) for e in range(E0)]
        tail_at = m.at
        hi_late = phase_base + LATE0 * COLS0 * 4
        lo_late = w0lo_at + LATE0 * COLS0 * 4
        late_size = (E0 - LATE0) * COLS0 * 4
        XN = L0.XN = m.put("XN", [P, TILES, D], F32, at=tail_at)
        slot_buffers(L0, tail_at)
        q = hi_late
        L0.SHRAW = m.put("SH0RAW", [P, SHCOLS0], F32, at=q)
        L0.SHLO = m.put("SH0LO", [P, SHCOLS0], F32R, at=q); q = m.end
        L0.SHHI = m.put("SH0HI", [P, SHCOLS0], F32R, at=q); q = m.end
        L0.XCMP = m.put("XCMP0", [1, SLOTS0 * (E0 + 1)], F32, at=q); q = m.end
        L0.WG = m.put("WG0", [P, KC, E0], F32, at=q); q = m.end
        assert q <= hi_late + late_size, (q - hi_late, late_size)
        q = lo_late
        L0.XT = m.put("XT0", [P, KC, TOKENS], F32, at=q); q = m.end
        L0.SGHI = m.put("SG0HI", [P, SHC0, GTOK], F32R, at=q); q = m.end
        L0.SGLO = m.put("SG0LO", [P, SHC0, GTOK], F32R, at=q); q = m.end
        assert q <= lo_late + late_size
        q = phase_base + EARLY0 * COLS0 * 4
        CTX = m.put("CTX", [P, KC, TOKENS], F32, at=q)
        L0.XSHI = m.put("XS0HI", [P, 2, KC, GTOK], F32R, at=q); q = m.end
        L0.XSLO = m.put("XS0LO", [P, 2, KC, GTOK], F32R, at=q); q = m.end
        L0.SSIL = m.put("SSIL0", [P, 2, GTOK], F32, at=q); q = m.end
        L0.SU = m.put("SU0", [P, 2, GTOK], F32, at=q); q = m.end
        ZERO = m.put("ZERO", [P, D], F32, at=q); q = m.end
        assert q <= hi_late
        q = w0lo_at + 6 * COLS0 * 4
        CTXW = m.put("CTXW", [P, TOKENS], F32, at=q); q = m.end
        WIN = m.put("WIN", [P, KC, D], F32, at=q); q = m.end
        WOUT = m.put("WOUT", [P, KC, D], F32, at=q); q = m.end
        BOUT = m.put("BOUT", [P, D], F32, at=q); q = m.end
        GAMMA = m.put("GAMMA", [P, D], F32, at=q); q = m.end
        BETA = m.put("BETA", [P, D], F32, at=q); q = m.end
        assert q <= lo_late
        SELB = m.put("SELB", [BATCH, TOKENS], F32, at=phase_base)
        q = m.end
        EMA = m.put("EMA", [P, SEQ], F32, at=q); q = m.end
        EMAC = m.put("EMAC", [P, SEQ], F32, at=q); q = m.end
        CSUM = m.put("CSUM", [P, KC, BATCH], F32, at=q); q = m.end
        M1T = m.put("M1T", [P, KC, BATCH], F32, at=q); q = m.end
        SUMM = m.put("SUMM", [BATCH, D], F32, at=q); q = m.end
        BIN = m.put("BIN", [P, KC], F32, at=q); q = m.end
        L0.R = [m.put(f"R0_{i}", [P, 16, 16], F32, at=q + 1024 * i) for i in range(8)]
        assert m.end <= phase_base + 4 * COLS0 * 4

        q = phase_base
        WKVC = m.put("WKVC", [P, KC, P], F32, at=q); q = m.end
        WKR = m.put("WKR", [KVC, 2, P], F32, at=q); q = m.end
        WDQ = m.put("WDQ", [P, KC, QC], F32, at=q); q = m.end
        KB = m.put("KB", [P, TILES, 4, P], F32, at=q); q = m.end
        AHI = m.put("AHI", [QC, PAIRS, 3, P], F32R, at=q); q = m.end
        ARAW = m.put("ARAW", [QC, PAIRS, 3, P], F32, at=q)
        ALO = m.put("ALO", [QC, PAIRS, 3, P], F32R, at=q); q = m.end
        MASK = m.put("MASK", [P, TILES, SEQ], F32, at=q); q = m.end
        XNG = m.put("XNG", [P, 2, 2, D], F32, at=q); q = m.end
        QCHI = m.put("QCHI", [QC, 2 * P], F32R, at=q); q = m.end
        SMX = m.put("SMX", [P, 2, 2, HEADS], F32, at=q); q = m.end
        RC = m.put("RC", [P, RINGQ, 2 * P], F32, at=q); q = m.end
        assert q <= w0lo_at, (q, w0lo_at)
        prep_at = w0lo_at
        q = prep_at
        Q = m.put("Q", [P, 2, HEADS, 2 * P], F32, at=q); q = m.end
        SM = m.put("SM", [P, 2, HEADS, SEQ], F32, at=q); q = m.end
        PT = m.put("PT", [P, PAIRS, P], F32, at=q); q = m.end
        work_end = q
        q = prep_at
        CTX1 = m.put("CTX1", [P, KC, TOKENS], F32, at=q); q = m.end
        assert q <= w0lo_at + DEAD0 * COLS0 * 4
        UQT = m.put("UQT", [P, HEADS, QC], F32, at=q); q = m.end
        UKT = m.put("UKT", [P, HEADS, KVC], F32, at=q); q = m.end
        UVT = m.put("UVT", [P, HEADS, KVC], F32, at=q); q = m.end
        WO = m.put("WO", [P, HEADS, D], F32, at=q); q = m.end
        q = max(work_end, q)
        BHI = m.put("BHI", [P, PAIRS, D], F32R, at=q); q = m.end
        BLO = m.put("BLO", [P, PAIRS, D], F32R, at=q); q = m.end
        XTG = m.put("XTG", [P, KC, 2 * P], F32, at=q); q = m.end
        QCLO = m.put("QCLO", [QC, 2 * P], F32R, at=q); q = m.end
        RS = m.put("RS", [P, RINGQ, 2 * P], F32, at=q); q = m.end
        CTHI = m.put("CTHI", [P, PAIRS, P], F32R, at=q); q = m.end
        CTLO = m.put("CTLO", [P, PAIRS, P], F32R, at=q); q = m.end
        OX = m.put("OX", [P, 2, D], F32, at=q); q = m.end
        attn_end = q
        assert attn_end + TILES * D * 4 <= GB_AT, (attn_end, GB_AT)

        L1 = moe("l1_", L0, E1, HID1, TOP1, SLOTS1, SH1)
        L1.norm_base = 3 * TILES
        L1.logits = E1 + 1
        L1.XN = m.put("XN1", [P, TILES, D], F32, at=attn_end)
        q = phase_base
        L1.WHI = m.put("W1HI", [P, E1, COLS1], F32R, at=q); q = m.end
        w1lo_at = q
        L1.WLO = m.put("W1LO", [P, E1, COLS1], F32R, at=q); q = m.end
        L1.WRAW = [m.put(f"W1RAW{e}", [P, COLS1], F32, at=w1lo_at + e * COLS1 * 4) for e in range(E1)]
        L1.SHRAW = m.put("SH1RAW", [P, SHCOLS1], F32, at=q)
        L1.SHLO = m.put("SH1LO", [P, SHCOLS1], F32R, at=q); q = m.end
        L1.SHHI = m.put("SH1HI", [P, SHCOLS1], F32R, at=q); q = m.end
        L1.XSHI = m.put("XS1HI", [P, 2, KC, GTOK], F32R, at=q); q = m.end
        L1.XSLO = m.put("XS1LO", [P, 2, KC, GTOK], F32R, at=q); q = m.end
        L1.WG = m.put("WG1", [P, KC, E1 + 1], F32, at=q); q = m.end
        L1.XT = m.put("XT1", [P, KC, TOKENS], F32, at=q); q = m.end
        L1.SGHI = m.put("SG1HI", [P, SHC1, GTOK], F32R, at=q); q = m.end
        L1.SGLO = m.put("SG1LO", [P, SHC1, GTOK], F32R, at=q); q = m.end
        L1.SSIL = m.put("SSIL1", [P, 2, GTOK], F32, at=q); q = m.end
        L1.SU = m.put("SU1", [P, 2, GTOK], F32, at=q); q = m.end
        L1.R = [m.put(f"R1_{i}", [P, 16, 16], F32, at=q + 1024 * i) for i in range(8)]; q = m.end
        L1.XCMP = m.put("XCMP1", [1, SLOTS1 * (E1 + 1)], F32, at=q); q = m.end
        q = slot_buffers(L1, q)
        assert q <= attn_end

        PS = ctx.enter_context(nc.psum_tensor("PS", [P, 8, 512], F32))
        B = [PS[:, i, :] for i in range(8)]

        def const(name, rows=P):
            lo, hi = CONST[name]
            return C[0:rows, lo:hi]

        ident = const("ident")

        def absorbed_bank(p):
            return B[5 if p % 2 else 6]

        def rope_bank(p):
            return B[4 if p % 2 else 7]

        DECAY, KEEP, GX, TX, GF, TF, BC, CTOT = 0, 1, 2, 4, 6, 8, 10, 12
        L0.gate, L1.gate = TF, TF + 1

        s_const = sem("const_loaded")
        s_par = sem("params_loaded")
        s_x = [sem(f"x_loaded{g}") for g in range(GROUPS)]
        s_ctx = [sem(f"ctx_loaded{k}") for k in range(KC)]
        s_wio = sem("ema_weights_loaded")
        s_zero = sem("zero_tile")
        s_act = sem("act_chain")
        s_dve = sem("dve_chain")
        s_pool = sem("pool_chain")
        s_var = sem("variance_ready")
        s_sd = sem("sqrt_ready")
        s_rstd = sem("rstd_ready")
        s_norm = sem("tiles_normalised")
        s_beta = sem("beta_scaled")
        s_xb = sem("beta_added")
        s_csum = sem("ctx_sums_ready")
        s_ema = sem("ema_steps")
        s_spread = sem("summary_spread")
        s_spused = sem("spread_used")
        k_ctx, k_wkv, k_up, k_raw = sem("k_ctx_loaded"), sem("k_wkv_loaded"), sem("k_up_loaded"), sem("k_raw_loaded")
        k_mask, k_zero = sem("mask_ready"), sem("kv_blocks_zeroed")
        k_kvc, k_kvcc, k_tokc = sem("kvc_done"), sem("kvc_copied"), sem("kvc_token_copied")
        k_rope, k_ropem, k_roped = sem("key_rope_done"), sem("key_rope_terms"), sem("key_rope_added")
        k_a, k_b, k_hi, k_lo = sem("absorbed_done"), sem("out_weights_done"), sem("weights_hi"), sem("weights_lo")
        t_norm, t_xt, t_xtc = sem("pair_normalised"), sem("pair_transposed"), sem("pair_transpose_copied")
        t_qc, t_qchi, t_qclo = sem("qc_done"), sem("qc_hi"), sem("qc_lo")
        t_abs, t_absc, t_rv, t_rvm, t_q = (sem("q_absorbed"), sem("q_absorbed_copied"), sem("q_rope_done"),
                                           sem("q_rope_terms"), sem("q_rope_added"))
        t_s, t_masked, t_max, t_sub, t_exp, t_sum, t_rec, t_prob = (sem("scores"), sem("scores_masked"), sem("row_max"),
                                                            sem("max_subtracted"), sem("exp_done"), sem("row_sum"), sem("row_sum_inverse"),
                                                            sem("probs_ready"))
        t_pt, t_ptc, t_ct, t_cthi, t_ctlo = (sem("probsT"), sem("probsT_copied"), sem("ctxT"), sem("ctxT_hi"),
                                             sem("ctxT_lo"))
        t_o, t_oc, t_x = sem("attn_out"), sem("attn_out_scaled"), sem("attn_added")
        e_var, e_sd, e_rstd = sem("done_variance"), sem("done_sqrt"), sem("done_rstd")
        s_out = sem("out_stored")

        class Count:

            def __init__(self, eng, semaphore):
                self.eng, self.sem, self.n = eng, semaphore, 0

            def mark(self, ins):
                ins.then_inc(self.sem, 1)
                self.n += 1
                return ins

            def wait(self, back=0):
                self.eng.wait_ge(self.sem, self.n - back)

        def at_least(i, n):
            return not isinstance(i, int) or i >= n

        x_rows = a["x"].rearrange("(t p) d -> p t d", p=P)
        out_rows = a["out"].rearrange("(t p) d -> p t d", p=P)

        def run_stages(i, j, slots, stages):
            for d, stage in stages:
                if not isinstance(i, int) or 0 <= i + d < slots:
                    stage(i + d, (j + d) % UNROLL)

        def slot_loop(eng, slots, step, lead, trail):
            for i in range(-lead, UNROLL):
                step(i, i % UNROLL)
            for it in range(1, slots // UNROLL - 1):
                for j in range(UNROLL):
                    step(it * UNROLL + j, j)
            for i in range(slots - UNROLL, slots + trail):
                step(i, i % UNROLL)

        def tile_loop(step, first=-AHEAD, end=TILES + BEHIND):
            for t in range(first, end):
                step(t, t % 4, t // 4 * 2)

        def tile(i, j, h, d, stage):
            if not isinstance(i, int) or 0 <= i + d < TILES:
                stage(i + d, (j + d) % 4, h + (j + d) // 2, (j + d) % 2)

        def pair(i, j, h, d, stage):
            if not isinstance(i, int) or 0 <= i + d < TILES:
                stage(h + (j + d) // 2, (j + d) // 2 % 2)

        def shared_remainder(eng, M):
            eng.wait_ge(M.shsplit, 2 * M.n + 1)
            eng.tensor_tensor(M.SHLO[:, :], M.SHRAW[:, :], M.SHHI[:, :].bitcast(F32), ALU.subtract).then_inc(M.shsplit, 1)

        def expert_remainder(eng, M, e):
            eng.wait_ge(M.split, M.expert0 + e + 1)
            eng.tensor_tensor(M.WLO[:, e, :], M.WRAW[e][:, :], M.WHI[:, e, :].bitcast(F32), ALU.subtract)\
                .then_inc(M.wready, 1)

        block = ctx.enter_context(nc.Block())

        def load_gate_and_shared(sp, M, n):
            sp.dma_start(M.WG[:, :, :], a[f"Wg{n}T"].rearrange("(k p) n -> p k n", p=P)).then_inc(M.wg, 16)
            sp.dma_start(M.SHRAW[:, :], a[f"sh{n}"]).then_inc(M.shw, 16)

        def stream_slots(sp, M, from_slot=None, other_load=None):
            def load(i):
                if i >= XRING:
                    sp.wait_ge(M.p_xt, M.slot0 + i - XRING + 1)
                sp.dma_start(M.XS[:, i % XRING, :], M.x_by_expert[i * P:(i + 1) * P, :]).then_inc(M.xl[i % XRING], 16)

            def store(i):
                sp.wait_ge(M.a_y, M.slot0 + i + 1)
                sp.dma_start(M.y_by_expert[i * P:(i + 1) * P, :], M.YS[:, i % 4, :]).then_inc(M.st[i % 4], 16)

            for i in range(M.slots + XLEAD):
                if i < M.slots:
                    load(i)
                if i >= XLEAD:
                    store(i - XLEAD)
                if other_load and i - XLEAD >= from_slot:
                    other_load(i - XLEAD - from_slot)

        @block.sync
        def _(sp):
            sp.dma_start(C[:, :], a["const"]).then_inc(s_const, 16)
            sp.dma_start(PAR[:, DECAY:DECAY + 1], a["decay"].to_broadcast([P, 1])).then_inc(s_par, 16)
            sp.dma_start(PAR[:, GX:GX + 2], a["g_xattn"].to_broadcast([P, 2])).then_inc(s_par, 16)
            sp.dma_start(PAR[:, GF:GF + 2], a["g_ffn"].to_broadcast([P, 2])).then_inc(s_par, 16)
            sp.dma_start(BIN[:, :], a["b_in"]).then_inc(s_par, 16)
            for g in range(GROUPS):
                sp.dma_start(X[:, g * GT:(g + 1) * GT, :], x_rows[:, g * GT:(g + 1) * GT, :]).then_inc(s_x[g], 16)
            for k in range(KC):
                sp.dma_start(CTX[:, k, :], a["ctxT"][k * P:(k + 1) * P, :]).then_inc(s_ctx[k], 16)
            sp.dma_start(WIN[:, :, :], a["W_inT"].rearrange("(k p) n -> p k n", p=P)).then_inc(s_wio, 16)
            sp.dma_start(WOUT[:, :, :], a["W_outT"].rearrange("(k p) n -> p k n", p=P)).then_inc(s_wio, 16)
            sp.dma_start(BOUT[:, :], a["b_out"].to_broadcast([P, D])).then_inc(s_wio, 16)
            sp.dma_start(GAMMA[:, :], a["gamma"].to_broadcast([P, D])).then_inc(s_wio, 16)
            sp.dma_start(BETA[:, :], a["beta"].to_broadcast([P, D])).then_inc(s_wio, 16)
            sp.dma_start(SELB[:, :], a["select"]).then_inc(s_wio, 16)
            load_gate_and_shared(sp, L0, 0)
            sp.wait_ge(s_zero, 2)
            for M in (L0, L1):
                sp.dma_start(M.x_by_expert.rearrange("(n p) d -> p n d", p=P),
                             ZERO[:, :].unsqueeze(1).to_broadcast([P, M.slots, D])).then_inc(M.fill, 16)
            for e in range(EARLY0):
                sp.dma_start(L0.WRAW[e][:, :], a["w0"][e]).then_inc(L0.raw[e], 16)
            sp.wait_ge(L0.lgt, TILES)
            for e in range(EARLY0, LATE0):
                sp.dma_start(L0.WRAW[e][:, :], a["w0"][e]).then_inc(L0.raw[e], 16)
            sp.wait_ge(L0.shx, GROUPS)
            for e in range(LATE0, LATER0):
                sp.dma_start(L0.WRAW[e][:, :], a["w0"][e]).then_inc(L0.raw[e], 16)
            sp.wait_ge(L0.shadd, TILES)
            for e in range(LATER0, E0):
                sp.dma_start(L0.WRAW[e][:, :], a["w0"][e]).then_inc(L0.raw[e], 16)
            sp.wait_ge(L0.scat, 16 * TILES * TOP0)

            def load_context(n):
                if n == 0:
                    sp.wait_ge(L0.p_y, DEAD0_SLOTS)
                    sp.wait_ge(L0.wready, E0)
                    sp.dma_start(ITOK[:, :], a["seg"]).then_inc(k_wkv, 16)
                    sp.dma_start(WKVC[:, :, :], a["W_kvc2"].rearrange("p (k n) -> p k n", k=KC)).then_inc(k_wkv, 16)
                    sp.dma_start(WKR[:, :, :], a["W_kr2"].rearrange("p (k n) -> p k n", k=2)).then_inc(k_wkv, 16)
                    sp.dma_start(WDQ[:, :, :], a["W_dq"].rearrange("p (k n) -> p k n", k=KC)).then_inc(k_wkv, 16)
                if n < CTX_PIECES:
                    c = slice(n * TOKENS // CTX_PIECES, (n + 1) * TOKENS // CTX_PIECES)
                    sp.dma_start(CTX1[:, :, c], a["ctxT"].rearrange("(k p) t -> p k t", p=P)[:, :, c]).then_inc(k_ctx, 16)

            stream_slots(sp, L0, DEAD0_SLOTS, load_context)
            sp.dma_start(ARAW[:, :, 1:3, :], a["W_qrv"].rearrange("q (p v n) -> q p v n", p=PAIRS, v=2)).then_inc(k_raw, 16)
            sp.dma_start(UQT[:, :, :], a["W_uqT"].rearrange("p (h n) -> p h n", h=HEADS)).then_inc(k_up, 16)
            sp.dma_start(UKT[:, :, :], a["W_ukT"].rearrange("p (h n) -> p h n", h=HEADS)).then_inc(k_up, 16)
            sp.dma_start(UVT[:, :, :], a["W_uvT"].rearrange("p (h n) -> p h n", h=HEADS)).then_inc(k_up, 16)
            sp.dma_start(WO[:, :, :], a["W_oh"].rearrange("p (h n) -> p h n", h=HEADS)).then_inc(k_up, 16)
            sp.wait_ge(t_x, TILES)
            load_gate_and_shared(sp, L1, 1)
            for e in range(E1):
                sp.dma_start(L1.WRAW[e][:, :], a["w1"][e]).then_inc(L1.raw[e], 16)
            sp.wait_ge(L1.scat, 16 * TILES * TOP1)
            stream_slots(sp, L1)
            for g in range(GROUPS):
                sp.wait_ge(L1.comb, L1.copy0 + (g + 1) * GT * TOP1)
                sp.dma_start(out_rows[:, g * GT:(g + 1) * GT, :], X[:, g * GT:(g + 1) * GT, :]).then_inc(s_out, 16)
            sp.wait_ge(s_out, 16 * GROUPS)

        def scatter(pool, M):
            pool.wait_ge(M.fill, 16)
            pool.wait_ge(M.pos, 1)
            for t in range(TILES):
                for k in range(M.top):
                    pool.indirect_dma_start(M.x_by_expert, bass.IndirectOffsetOnAxis(POSI[:, k, t:t + 1], 0),
                                            M.XN[:, t, :], None, bounds_check=M.slots * P - 1,
                                            oob_is_err=False).then_inc(M.scat, 16)

        def gather(pool, M, t):
            for k in range(M.top):
                n = M.copy0 + t * M.top + k
                if n >= 8:
                    pool.wait_ge(M.comb, n - 7)
                pool.indirect_dma_start(M.GB[:, n % 8, :], None, M.y_by_expert,
                                        bass.IndirectOffsetOnAxis(POSI[:, k, t:t + 1], 0),
                                        bounds_check=M.slots * P - 1, oob_is_err=False).then_inc(M.gath[n % 8], 16)

        def wait_for_slots(pool, M):
            for r in range(4):
                pool.wait_ge(M.st[r], 16 * ((M.slot0 + M.slots) // 4))

        @block.gpsimd
        def _(pool):
            ch = Count(pool, s_pool)
            pool.memset(ZERO[:, :], 0.0).then_inc(s_zero, 1)
            pool.memset(ONE64[:, :], 1.0).then_inc(s_zero, 1)
            pool.wait_ge(s_wio, 16 * 6)
            pool.wait_ge(s_beta, 1)
            for t in range(TILES):
                pool.wait_ge(s_norm, t + 1)
                pool.tensor_tensor(X[:, t, :], X[:, t, :], BETA[:, :], ALU.add).then_inc(s_xb, 1)
            shared_remainder(pool, L0)
            scatter(pool, L0)
            for e in POOLS0:
                expert_remainder(pool, L0, e)
            wait_for_slots(pool, L0)
            gather(pool, L0, 0)
            gather(pool, L0, 1)
            pool.wait_ge(k_wkv, 16 * 4)
            pool.wait_ge(L0.p_y, SLOTS0)
            ch.mark(pool.tensor_copy(SEG[:, :], ITOK[:, :]))
            ch.wait()
            seen = XNG[:, :, :, :].rearrange("p a b d -> p (a b d)").rearrange("p (t s) -> p t s", s=SEQ)
            ch.mark(pool.tensor_tensor(MASK[:, :, :], const("key_id").unsqueeze(1).to_broadcast([P, TILES, SEQ]),
                                       SEG[:, :].unsqueeze(2).to_broadcast([P, TILES, SEQ]), ALU.subtract))
            ch.wait()
            ch.mark(pool.tensor_scalar(seen, MASK[:, :, :], float(-LOOKBACK), None, ALU.is_ge))
            ch.wait()
            ch.mark(pool.tensor_scalar(MASK[:, :, :], MASK[:, :, :], 0.0, None, ALU.is_le))
            ch.wait()
            ch.mark(pool.tensor_tensor(MASK[:, :, :], MASK[:, :, :], seen, ALU.mult))
            ch.wait()
            pool.tensor_scalar(MASK[:, :, :], MASK[:, :, :], -1.0, NEG, ALU.add, ALU.mult).then_inc(k_mask, 1)
            cos = const("cos").unsqueeze(1)

            last, gathers = [], []

            def after_last():
                if last:
                    pool.wait_ge(*last[-1])

            def gather_tile(t, r, u, o):
                if t < 2:
                    return
                after_last()
                gather(pool, L0, t)
                gathers.append(t)

            def sub(i, r, u, o):
                pool.wait_ge(t_max, i + 1)
                after_last()
                pool.tensor_tensor(SM[:, r % 2, :, :], SM[:, r % 2, :, :],
                                   SMX[:, r % 2, 0, :].unsqueeze(2).to_broadcast([P, HEADS, SEQ]), ALU.subtract)\
                    .then_inc(t_sub, 1)
                last.append((t_sub, i + 1))

            def rope(p):
                def stage(v, par):
                    n = v * PAIRS + p
                    pool.wait_ge(t_rvm, 2 * n + 2)
                    if v >= 2:
                        pool.wait_ge(t_s, v * 4 - 4)
                    if gathers:
                        for k in range(TOP0):
                            n_g = gathers[-1] * TOP0 + k
                            pool.wait_ge(L0.gath[n_g % 8], 16 * (n_g // 8 + 1))
                        gathers.clear()
                    for half, head in ((0, 2 * p + 1), (64, 2 * p)):
                        after_last()
                        s = slice(half, half + 64)
                        pool.tensor_tensor(Q[s, par, head, :], RC[s, n % RINGQ, :], RS[s, n % RINGQ, :], ALU.add)\
                            .then_inc(t_q, 1)
                        last.append((t_q, 2 * n + (2 if half else 1)))
                return stage

            def add_x(i, r, u, o):
                pool.wait_ge(t_oc, i + 1)
                after_last()
                pool.tensor_tensor(X[:, i, :], X[:, i, :], OX[:, r % 2, :], ALU.add).then_inc(t_x, 1)
                last.append((t_x, i + 1))

            def step(i, j, h):
                if j % 2:
                    tile(i, j, h, 1, sub)
                    pair(i, j, h, 3, rope(0))
                    pair(i, j, h, 3, rope(1))
                    pair(i, j, h, 3, rope(2))
                    pair(i, j, h, 3, rope(3))
                    tile(i, j, h, -1, add_x)
                    tile(i, j, h, 8, gather_tile)
                else:
                    tile(i, j, h, 1, sub)
                    pair(i, j, h, 2, rope(4))
                    pair(i, j, h, 2, rope(5))
                    pair(i, j, h, 2, rope(6))
                    pair(i, j, h, 2, rope(7))
                    tile(i, j, h, -1, add_x)
                    tile(i, j, h, 8, gather_tile)

            tile_loop(step)
            for e in range(DVE_SPLITS1, E1):
                expert_remainder(pool, L1, e)
            scatter(pool, L1)
            wait_for_slots(pool, L1)
            for t in range(TILES):
                gather(pool, L1, t)

        @block.scalar
        def _(act):
            act.wait_ge(s_par, 16 * 4)
            act.activation(PAR[:, KEEP:KEEP + 1], PAR[:, DECAY:DECAY + 1], ACT.Sigmoid).then_inc(s_act, 1)
            act.activation(PAR[:, TX:TX + 2], PAR[:, GX:GX + 2], ACT.Tanh).then_inc(s_act, 1)
            act.activation(PAR[:, TF:TF + 2], PAR[:, GF:GF + 2], ACT.Tanh).then_inc(s_act, 1)

            def deviations(n, t0, t1):
                act.wait_ge(s_var, n + 1)
                act.activation(SD[:, t0:t1], SD[:, t0:t1], ACT.Sqrt).then_inc(s_sd, 1)

            def norm_pass(n, src, ahead):
                for g in range(-ahead, GROUPS):
                    if g + ahead < GROUPS:
                        deviations(n * GROUPS + g + ahead, (g + ahead) * GT, (g + ahead + 1) * GT)
                    if g < 0:
                        continue
                    act.wait_ge(s_rstd, n * GROUPS + g + 1)
                    for t in range(g * GT, (g + 1) * GT):
                        act.activation(XN[:, t, :], src[:, t, :], ACT.Identity, bias=SHIFT[:, t:t + 1],
                                       scale=RSTD[:, t:t + 1]).then_inc(s_norm, 1)

            norm_pass(0, X, GROUPS)
            norm_pass(1, XN, 1)

            def norm_group(g):
                deviations(L0.var0 + g, g * GT, (g + 1) * GT)
                act.wait_ge(s_rstd, L0.var0 + g + 1)
                for t in range(g * GT, (g + 1) * GT):
                    act.activation(XN[:, t, :], X[:, t, :], ACT.Identity, bias=SHIFT[:, t:t + 1],
                                   scale=RSTD[:, t:t + 1]).then_inc(s_norm, 1)

            def copy_transposes(M, g):
                for k in range(KC):
                    act.wait_ge(M.xt, (M.n * GROUPS + g) * KC + k + 1)
                    act.copy(M.XT[:, k, g * GTOK:(g + 1) * GTOK], B[4 * (g % 2) + k][:, :]).then_inc(M.xtc, 1)

            def shared_weights(M):
                act.wait_ge(M.shw, 16 * (M.n + 1))
                act.copy(M.SHHI[:, :], M.SHRAW[:, :]).then_inc(M.shsplit, 1)

            def expert_weights(M, e):
                act.wait_ge(M.raw[e], 16 * (M.n + 1))
                act.copy(M.WHI[:, e, :], M.WRAW[e][:, :]).then_inc(M.split, 1)

            def shared(M, splits):
                def tokens(g):
                    if g >= 2:
                        act.wait_ge(M.shh, M.chunk0 + (g - 1) * M.shc)
                    act.wait_ge(M.xtc, KC * GROUPS * (M.n + 1))
                    act.copy(M.XSHI[:, g % 2, :, :], M.XT[:, :, g * GTOK:(g + 1) * GTOK]).then_inc(M.shxh, 1)

                tokens(0)
                tokens(1)
                for g in range(GROUPS):
                    for c in range(M.shc):
                        n = g * M.shc + c
                        act.wait_ge(M.shh, M.chunk0 + n + 1)
                        if n >= 2:
                            act.wait_ge(M.shu, M.chunk0 + n - 1)
                        act.activation(M.SSIL[:, n % 2, :], B[2 * (n % 2)][:, :], ACT.Silu).then_inc(M.shs, 1)
                        act.wait_ge(M.shu, M.chunk0 + n + 1)
                        if g:
                            act.wait_ge(M.shy, M.n * TILES + g * GT)
                        act.copy(M.SGHI[:, c, :], M.SU[:, n % 2, :]).then_inc(M.shg, 1)
                    if g + 2 < GROUPS:
                        tokens(g + 2)
                    each = splits // GROUPS
                    for e in range(g * each, (g + 1) * each):
                        act.wait_ge(M.eid, 2)
                        expert_weights(M, e)

            def other_experts():
                act.wait_ge(L0.shadd, TILES)
                act.wait_ge(L1.fill, 16)
                for e in range(EARLY0, E0):
                    expert_weights(L0, e)

            def slots(M):
                def hi(i, j):
                    act.wait_ge(M.p_xt, i + (M.slot0 + 1))
                    if at_least(i, 2):
                        act.wait_ge(M.p_h, i + (M.slot0 - 1))
                    act.copy(M.XHI[:, j % 2, :], B[j % 2][:, 0:D]).then_inc(M.a_xhi, 1)

                def sil(i, j):
                    act.wait_ge(M.p_h, i + (M.slot0 + 1))
                    if at_least(i, 2):
                        act.wait_ge(M.d_g, i + (M.slot0 - 1))
                    act.activation(M.SIL[:, j % 2, :], B[2 + j % 2][:, 0:M.hid], ACT.Silu).then_inc(M.a_sil, 1)

                def ghi(i, j):
                    act.wait_ge(M.p_gt, i + (M.slot0 + 1))
                    if at_least(i, 2):
                        act.wait_ge(M.p_y, i + (M.slot0 - 1))
                    act.copy(M.GHI[:, j % 2, :], B[4 + j % 2][:, 0:M.hchunks * P]).then_inc(M.a_ghi, 1)

                def y(i, j):
                    act.wait_ge(M.p_y, i + (M.slot0 + 1))
                    if at_least(i, 4):
                        if isinstance(i, int):
                            act.wait_ge(M.st[j % 4], 16 * ((i + M.slot0) // 4))
                        else:
                            act.wait_ge(M.st[j % 4], (i - j) * 4 + 4 * M.slot0)
                    act.copy(M.YS[:, j % 4, :], B[6 + j % 2][:, 0:D]).then_inc(M.a_y, 1)

                def step(i, j):
                    run_stages(i, j, M.slots, ((2, hi), (1, sil), (0, ghi), (-1, y)))

                slot_loop(act, M.slots, step, 2, 1)

            for g in range(GROUPS + 1):
                if g < GROUPS:
                    norm_group(g)
                if g:
                    copy_transposes(L0, g - 1)
            shared_weights(L0)
            act.wait_ge(L0.shifted, 1)
            act.activation(L0.R[0][:, :, :], L0.R[0][:, :, :], ACT.Exp).then_inc(L0.exped, 1)
            shared(L0, EARLY0)
            other_experts()
            act.wait_ge(L0.scat, 16 * TILES * TOP0)
            slots(L0)
            for n in range(GROUPS):
                act.wait_ge(k_kvc, n + 1)
                for half, which in ((0, 0), (64, 1)):
                    s = slice(half, half + 64)
                    act.copy(KB[s, n * GT:(n + 1) * GT, which, :],
                             B[n][s, :].rearrange("p (t n) -> p t n", n=P)).then_inc(k_kvcc, 1)
            act.wait_ge(k_zero, 1)
            for n in range(GROUPS):
                act.wait_ge(k_kvc, GROUPS + n + 1)
                for b in range(2):
                    for h in range(2):
                        src = B[4 + n][b * 64:(b + 1) * 64, :].rearrange("p (t n) -> p t n", n=P)[:, :, 0:KVC]
                        act.copy(KB[h * 64:(h + 1) * 64, n * GT:(n + 1) * GT, 2 + b, h * 64:(h + 1) * 64], src)\
                            .then_inc(k_tokc, 1)
            act.wait_ge(k_raw, 16)
            act.copy(AHI[:, :, 1:3, :], ARAW[:, :, 1:3, :]).then_inc(k_hi, 1)
            for n in range(2):
                act.wait_ge(k_a, n + 1)
                act.copy(AHI[:, 4 * n:4 * n + 4, 0, :], B[n][0:QC, :].rearrange("p (h n) -> p h n", n=P))\
                    .then_inc(k_hi, 1)

            def sqrt_pair(v, par):
                deviations(3 * GROUPS + v, 2 * v, 2 * v + 2)

            def norm_pair(v, par):
                act.wait_ge(s_rstd, 3 * GROUPS + v + 1)
                if v == 0:
                    act.wait_ge(k_mask, 1)
                if at_least(v, 2):
                    act.wait_ge(t_xt, v - 1)
                for o in range(2):
                    at = v * 2 + o
                    act.activation(XNG[:, par, o, :], X[:, bass.ds(at, 1), :].rearrange("p o d -> p (o d)"), ACT.Identity,
                                   bias=SHIFT[:, bass.ds(at, 1)], scale=RSTD[:, bass.ds(at, 1)]).then_inc(t_norm, 1)

            def copy_xt(v, par):
                act.wait_ge(t_xt, v + 1)
                if at_least(v, 1):
                    act.wait_ge(t_qc, v)
                act.copy(XTG[:, :, :], B[7][:, :].rearrange("p (k n) -> p k n", k=KC)).then_inc(t_xtc, 1)

            def qc_hi(v, par):
                act.wait_ge(t_qc, v + 1)
                if at_least(v, 1):
                    act.wait_ge(t_rv, v * PAIRS)
                act.copy(QCHI[:, :], B[5][0:QC, 0:2 * P]).then_inc(t_qchi, 1)

            def absorbed(p):
                def stage(v, par):
                    act.wait_ge(t_abs, v * PAIRS + (p + 1))
                    if at_least(v, 2):
                        act.wait_ge(t_s, v * 4 - 4)
                    for half, head in ((0, 2 * p), (64, 2 * p + 1)):
                        s = slice(half, half + 64)
                        act.copy(Q[s, par, head, :], absorbed_bank(p)[s, 0:2 * P]).then_inc(t_absc, 1)
                return stage

            def copy_pt(i, r, u, o):
                for n in range(2):
                    act.wait_ge(t_pt, i * 2 + (n + 1))
                    if at_least(i, 1):
                        act.wait_ge(t_ct, i * 2)
                    act.copy(PT[:, 4 * n:4 * n + 4, :], B[2 + n][:, :].rearrange("p (h n) -> p h n", n=P))\
                        .then_inc(t_ptc, 1)

            def scale_out(i, r, u, o):
                act.wait_ge(t_o, i + 1)
                if at_least(i, 2):
                    act.wait_ge(t_x, i - 1)
                act.activation(OX[:, r % 2, :], B[6][:, 2 * P:], ACT.Copy, scale=PAR[:, TX + 1:TX + 2]).then_inc(t_oc, 1)

            def exp(i, r, u, o):
                act.wait_ge(t_sub, i + 1)
                act.activation(SM[:, r % 2, :, :], SM[:, r % 2, :, :], ACT.Exp, scale=SM_SCALE).then_inc(t_exp, 1)

            def ct_hi(i, r, u, o):
                for b in range(2):
                    act.wait_ge(t_ct, i * 2 + (b + 1))
                    if at_least(i, 1):
                        act.wait_ge(t_o, i)
                    act.copy(CTHI[:, :, b * 64:(b + 1) * 64], B[2 + b][:, :].rearrange("p (h n) -> p h n", n=64))\
                        .then_inc(t_cthi, 1)

            def sqrt_done(v, par):
                act.wait_ge(e_var, v + 1)
                act.activation(SD[:, 2 * v:2 * v + 2], SD[:, 2 * v:2 * v + 2], ACT.Sqrt).then_inc(e_sd, 1)

            def norm_done(v, par):
                act.wait_ge(e_rstd, v + 1)
                for t in (2 * v, 2 * v + 1):
                    act.activation(L1.XN[:, t, :], X[:, t, :], ACT.Identity, bias=SHIFT[:, t:t + 1],
                                   scale=RSTD[:, t:t + 1]).then_inc(s_norm, 1)

            def step(i, j, h):
                if j % 2:
                    pair(i, j, h, 3, qc_hi)
                    pair(i, j, h, 5, sqrt_pair)
                    tile(i, j, h, 0, copy_pt)
                    pair(i, j, h, 3, absorbed(0))
                    tile(i, j, h, -1, scale_out)
                    pair(i, j, h, 3, absorbed(1))
                    tile(i, j, h, 1, exp)
                    tile(i, j, h, 0, ct_hi)
                    pair(i, j, h, 3, absorbed(2))
                    pair(i, j, h, 3, absorbed(3))
                    pair(i, j, h, 5, norm_pair)
                    pair(i, j, h, -5, norm_done)
                else:
                    pair(i, j, h, 2, absorbed(4))
                    pair(i, j, h, 2, absorbed(5))
                    tile(i, j, h, 0, copy_pt)
                    pair(i, j, h, 2, absorbed(6))
                    tile(i, j, h, 1, exp)
                    tile(i, j, h, -1, scale_out)
                    pair(i, j, h, 2, absorbed(7))
                    pair(i, j, h, 4, copy_xt)
                    tile(i, j, h, 0, ct_hi)
                    pair(i, j, h, -4, sqrt_done)

            tile_loop(step, end=SECOND)
            for n in range(4):
                act.wait_ge(k_b, n + 1)
                act.copy(BHI[:, 2 * n:2 * n + 2, :], B[n][:, :].rearrange("p (h n) -> p h n", n=D)).then_inc(k_hi, 1)
            tile_loop(step, first=SECOND)
            for g in range(GROUPS):
                copy_transposes(L1, g)
            shared_weights(L1)
            for e in range(DVE_SPLITS1):
                expert_weights(L1, e)
            act.wait_ge(L1.shifted, 1)
            act.activation(SGATE[:, :], L1.R[0][:, :, E1], ACT.Sigmoid).then_inc(L1.exped, 1)
            act.wait_ge(L1.shifted, 2)
            act.activation(SMALL[:, 6, :], SMALL[:, 5, :], ACT.Exp).then_inc(L1.exped, 1)
            for e in range(DVE_SPLITS1, E1):
                expert_weights(L1, e)
            shared(L1, 0)
            slots(L1)

        @block.tensor
        def _(pe):
            def three_passes(out, operands, first=True, last=True):
                passes = [(x, w) for xh, xl, wh, wl in operands for x, w in ((xh, wh), (xh, wl), (xl, wh))]
                for n, (x, w) in enumerate(passes):
                    mm = pe.matmul(out, x, w, start=(n == 0), stop=(n == len(passes) - 1))
                return mm

            def gate(M):
                pe.wait_ge(M.wg, 16 * (M.n + 1))
                for g in range(GROUPS + 1):
                    if g < GROUPS:
                        for k in range(KC):
                            if g >= 2:
                                pe.wait_ge(M.xtc, (M.n * GROUPS + g - 2) * KC + k + 1)
                            for t in range(GT):
                                pe.wait_ge(s_norm, M.norm_base + g * GT + t + 1)
                                tr = pe.transpose(B[4 * (g % 2) + k][:, t * P:(t + 1) * P],
                                                  M.XN[:, g * GT + t, k * P:(k + 1) * P], ident)
                            tr.then_inc(M.xt, 1)
                    if g:
                        pe.wait_ge(M.xtc, (M.n * GROUPS + g) * KC)
                        for t in range((g - 1) * GT, g * GT):
                            for k in range(KC):
                                mm = pe.matmul(B[3][:, t * 16:t * 16 + M.logits], M.XT[:, k, t * P:(t + 1) * P],
                                               M.WG[:, k, :], start=(k == 0), stop=(k == KC - 1))
                            mm.then_inc(M.lgt, 1)

            def counts(M):
                pe.wait_ge(M.sel, 1)
                pe.matmul(B[4][:, 0:256], TRI[:, :], SEL[:, :, :].rearrange("p t e -> p (t e)"), start=True, stop=True)
                pe.matmul(B[5][:, 0:256], ONES[:, :], SEL[:, :, :].rearrange("p t e -> p (t e)"),
                          start=True, stop=True).then_inc(M.counts, 1)

            at_expert = {}

            def load_expert(M, i):
                if i < M.slots:
                    at_expert[i] = pe.value_load(EID[0:1, i:i + 1], min_val=0, max_val=(M.E - 1) * M.cols)

            def shared(M):
                pe.wait_ge(M.shsplit, 2 * (M.n + 1))
                pe.wait_ge(M.routed, 1)
                SH, n13 = M.sh, KC * M.sh
                w1 = [s[:, 0:n13].rearrange("p (k n) -> p k n", k=KC) for s in (M.SHHI, M.SHLO)]
                w3 = [s[:, n13:2 * n13].rearrange("p (k n) -> p k n", k=KC) for s in (M.SHHI, M.SHLO)]
                w2 = [s[:, 2 * n13:].rearrange("p (c n) -> p c n", c=M.shc) for s in (M.SHHI, M.SHLO)]

                def hidden(g, c):
                    n = g * M.shc + c
                    if c == 0:
                        pe.wait_ge(M.shx, M.n * GROUPS + g + 1)
                    if n >= 2:
                        pe.wait_ge(M.shu, M.chunk0 + n - 1)
                    for w, bank in ((w1, B[2 * (n % 2)]), (w3, B[2 * (n % 2) + 1])):
                        mm = three_passes(bank[:, :], [(w[0][:, k, c * P:(c + 1) * P], w[1][:, k, c * P:(c + 1) * P],
                                                        M.XSHI[:, g % 2, k, :], M.XSLO[:, g % 2, k, :]) for k in range(KC)])
                    mm.then_inc(M.shh, 1)

                def outputs(g):
                    pe.wait_ge(M.shl, M.chunk0 + (g + 1) * M.shc)
                    for t in range(GT):
                        n = g * GT + t
                        if n >= 2:
                            pe.wait_ge(M.shadd, M.n * TILES + n - 1)
                        s = slice(t * P, (t + 1) * P)
                        three_passes(B[4 + n % 2][:, 0:D], [(M.SGHI[:, c, s], M.SGLO[:, c, s], w2[0][:, c, :], w2[1][:, c, :])
                                                            for c in range(M.shc)]).then_inc(M.shy, 1)

                for g in range(GROUPS):
                    for c in range(M.shc):
                        hidden(g, c)
                        if c == 0 and g:
                            outputs(g - 1)
                pe.wait_ge(M.eid, 2)
                for i in range(3):
                    load_expert(M, i)
                outputs(GROUPS - 1)

            def slots(M):
                whi = M.WHI[:, :, :].rearrange("p e c -> p (e c)")
                wlo = M.WLO[:, :, :].rearrange("p e c -> p (e c)")

                def xt(i, j):
                    pe.wait_ge(M.xl[i % XRING], 16 * ((i + M.slot0) // XRING + 1))
                    for k in range(KC):
                        tr = pe.transpose(B[j % 2][:, k * P:(k + 1) * P], M.XS[:, i % XRING, k * P:(k + 1) * P], ident)
                    tr.then_inc(M.p_xt, 1)

                def hidden(i, j):
                    if i == 0:
                        pe.wait_ge(M.wready, M.expert0 + M.E)
                    pe.wait_ge(M.d_xlo, i + (M.slot0 + 1))
                    out = B[2 + j % 2][:, 0:M.w13]
                    for k in range(KC):
                        at = bass.ds(at_expert[i] + k * M.w13, M.w13)
                        s = slice(k * P, (k + 1) * P)
                        pe.matmul(out, M.XHI[:, j % 2, s], whi[:, at], start=(k == 0), stop=False)
                        pe.matmul(out, M.XLO[:, j % 2, s], whi[:, at], start=False, stop=False)
                        mm = pe.matmul(out, M.XHI[:, j % 2, s], wlo[:, at], start=False, stop=(k == KC - 1))
                    mm.then_inc(M.p_h, 1)

                def gt(i, j):
                    if i == 0:
                        pe.wait_ge(M.shadd, (M.n + 1) * TILES)
                    pe.wait_ge(M.d_g, i + (M.slot0 + 1))
                    for c in range(M.hchunks):
                        tr = pe.transpose(B[4 + j % 2][:, c * P:(c + 1) * P], M.G[:, j % 2, c * P:(c + 1) * P], ident)
                    tr.then_inc(M.p_gt, 1)

                def y(i, j):
                    pe.wait_ge(M.d_glo, i + (M.slot0 + 1))
                    if at_least(i, 2):
                        pe.wait_ge(M.a_y, i + (M.slot0 - 1))
                    out = B[6 + j % 2][:, 0:D]
                    for c in range(M.hchunks):
                        at = bass.ds(at_expert[i] + KC * M.w13 + c * D, D)
                        s = slice(c * P, (c + 1) * P)
                        pe.matmul(out, M.GHI[:, j % 2, s], whi[:, at], start=(c == 0), stop=False)
                        pe.matmul(out, M.GLO[:, j % 2, s], whi[:, at], start=False, stop=False)
                        if c == 0:
                            load_expert(M, i + 3)
                        mm = pe.matmul(out, M.GHI[:, j % 2, s], wlo[:, at], start=False, stop=(c == M.hchunks - 1))
                    mm.then_inc(M.p_y, 1)

                def step(i, j):
                    run_stages(i, j, M.slots, ((2, xt), (1, hidden), (0, gt), (-1, y)))

                slot_loop(pe, M.slots, step, 2, 1)

            pe.wait_ge(s_const, 16)
            pe.wait_ge(s_wio, 16 * 6)
            pe.wait_ge(s_csum, KC)
            for j in range(KC):
                for k in range(KC):
                    mm = pe.matmul(B[0][:, j * BATCH:(j + 1) * BATCH], WIN[:, k, j * P:(j + 1) * P], CSUM[:, k, :],
                                   start=(k == 0), stop=(k == KC - 1))
            mm.then_inc(s_ema, 1)
            pe.wait_ge(s_ema, 1 + KC)
            for j in range(KC):
                mm = pe.matmul(B[1][0:BATCH, 0:D], M1T[:, j, :], WOUT[:, j, :], start=(j == 0), stop=(j == KC - 1))
            mm.then_inc(s_ema, 1)
            pe.wait_ge(s_ema, 3 + KC)
            for t in range(TILES):
                if t >= 6:
                    pe.wait_ge(s_spused, t - 5)
                pe.matmul(B[2 + t % 6][:, 0:D], SELB[:, t * P:(t + 1) * P],
                          SUMM[:, :], start=True, stop=True).then_inc(s_spread, 1)
            pe.wait_ge(s_spused, TILES)
            gate(L0)
            counts(L0)
            shared(L0)
            slots(L0)
            pe.wait_ge(k_wkv, 16 * 4)
            pe.wait_ge(k_ctx, 16 * CTX_PIECES)
            pe.wait_ge(L0.a_y, SLOTS0)
            for n in range(GROUPS):
                for k in range(KC):
                    mm = pe.matmul(B[n][:, :], WKVC[:, k, :], CTX1[:, k, n * GTOK:(n + 1) * GTOK],
                                   start=(k == 0), stop=(k == KC - 1))
                mm.then_inc(k_kvc, 1)
            for n in range(GROUPS):
                for t in range(GT):
                    for k in range(KC):
                        at = (n * GT + t) * P
                        mm = pe.matmul(B[4 + n][:, t * P:(t + 1) * P], CTX1[:, k, at:at + P], WKVC[:, k, :],
                                       start=(k == 0), stop=(k == KC - 1))
                mm.then_inc(k_kvc, 1)
            for n in range(GROUPS):
                pe.wait_ge(k_kvcc, 2 * (n + 1))
                kv = KB[0:KVC, n * GT:(n + 1) * GT, 0, :]
                pe.matmul(B[n][:, :], WKR[:, 0, :], kv, start=True, stop=True)
                pe.wait_ge(k_tokc, 4 * (n + 1))
                pe.matmul(B[4 + n][:, :], WKR[:, 1, :], kv, start=True, stop=True).then_inc(k_rope, 1)
            pe.wait_ge(k_up, 16 * 4)
            for n in range(2):
                pe.wait_ge(k_ropem, 2 * (n + 1))
                for h in range(8):
                    mm = pe.matmul(B[n][0:QC, h * KVC:(h + 1) * KVC], UQT[:, 8 * n + h, :], UKT[:, 8 * n + h, :],
                                   start=True, stop=True)
                mm.then_inc(k_a, 1)
            pe.wait_ge(k_ropem, 2 * GROUPS)

            def transpose_pair(v, par):
                pe.wait_ge(t_norm, v * 2 + 2)
                if at_least(v, 1):
                    pe.wait_ge(t_rvm, v * 2 * PAIRS - 2)
                for k in range(KC):
                    for o in range(2):
                        tr = pe.transpose(B[7][:, (2 * k + o) * P:(2 * k + o + 1) * P],
                                          XNG[:, par, o, k * P:(k + 1) * P], ident)
                tr.then_inc(t_xt, 1)

            def down(v, par):
                pe.wait_ge(t_xtc, v + 1)
                if at_least(v, 1):
                    pe.wait_ge(t_absc, v * 2 * PAIRS)
                for k in range(KC):
                    mm = pe.matmul(B[5][0:QC, 0:2 * P], WDQ[:, k, :], XTG[:, k, :], start=(k == 0), stop=(k == KC - 1))
                mm.then_inc(t_qc, 1)

            def up(p):
                def stage(v, par):
                    pe.wait_ge(t_qclo, v + 1)
                    n = v * PAIRS + p
                    if n >= 2:
                        pe.wait_ge(t_absc, 2 * (n - 1))
                        pe.wait_ge(t_rvm, 2 * (n - 1))
                    outs = v * 2 - (4 if p == 0 else 3)
                    if p % 2 == 0 and outs > 0:
                        pe.wait_ge(t_oc, outs)
                    three_passes(absorbed_bank(p)[:, 0:2 * P], [(AHI[:, p, 0, :], ALO[:, p, 0, :], QCHI[:, :], QCLO[:, :])])\
                        .then_inc(t_abs, 1)
                    for w in (1, 2):
                        mm = three_passes(rope_bank(p)[:, (w - 1) * 2 * P:w * 2 * P],
                                          [(AHI[:, p, w, :], ALO[:, p, w, :], QCHI[:, :], QCLO[:, :])])
                    mm.then_inc(t_rv, 1)
                return stage

            def score(i, r, u, o):
                pe.wait_ge(t_absc, u * 2 * PAIRS + 2 * PAIRS)
                pe.wait_ge(t_q, u * 2 * PAIRS + 2 * PAIRS)
                if i == 0:
                    pe.wait_ge(k_roped, 2 * GROUPS)
                else:
                    pe.wait_ge(t_masked, i * 2)
                for head in range(HEADS):
                    for b in range(2):
                        mm = pe.matmul(B[head // 8][b * 64:(b + 1) * 64, head % 8 * SEQ:(head % 8 + 1) * SEQ],
                                       Q[:, r // 2, head, o * P + b * 64:o * P + (b + 1) * 64],
                                       KB[:, i, head % 2, b * SEQ:(b + 1) * SEQ], start=True, stop=True)
                    if head % 8 == 7:
                        mm.then_inc(t_s, 1)

            def probs_t(i, r, u, o):
                pe.wait_ge(t_prob, i + 1)
                if at_least(i, 1):
                    pe.wait_ge(t_ctlo, i * 2)
                for n in range(2):
                    for h in range(4):
                        tr = pe.transpose(B[2 + n][:, h * P:(h + 1) * P],
                                          SM[:, r % 2, 8 * n + 2 * h:8 * n + 2 * h + 2, :].rearrange("p h n -> p (h n)"),
                                          ident)
                    tr.then_inc(t_pt, 1)

            def context(i, r, u, o):
                pe.wait_ge(t_ptc, i * 2 + 2)
                for b in range(2):
                    pe.matmul(B[2 + b][:, :], KB[:, i, 2 + b, :], PT[:, :, b * 64:(b + 1) * 64], start=True, stop=True)\
                        .then_inc(t_ct, 1)

            def out(i, r, u, o):
                pe.wait_ge(t_ctlo, i * 2 + 2)
                if at_least(i, 1):
                    pe.wait_ge(t_oc, i)
                copied = u * 2 * PAIRS + (34 if o == 0 else 46)
                pe.wait_ge(t_absc, min(copied, TILES * PAIRS) if isinstance(i, int) else copied)
                three_passes(B[6][:, 2 * P:], [(CTHI[:, p, :], CTLO[:, p, :], BHI[:, p, :], BLO[:, p, :])
                                               for p in range(PAIRS)]).then_inc(t_o, 1)

            def step(i, j, h):
                if j % 2:
                    pair(i, j, h, 3, down)
                    tile(i, j, h, 1, score)
                    tile(i, j, h, 0, probs_t)
                    pair(i, j, h, 3, up(0))
                    tile(i, j, h, -1, out)
                    pair(i, j, h, 3, up(1))
                    tile(i, j, h, 0, context)
                    pair(i, j, h, 3, up(2))
                    pair(i, j, h, 3, up(3))
                else:
                    tile(i, j, h, 1, score)
                    pair(i, j, h, 2, up(4))
                    pair(i, j, h, 2, up(5))
                    tile(i, j, h, 0, probs_t)
                    pair(i, j, h, 2, up(6))
                    tile(i, j, h, -1, out)
                    pair(i, j, h, 4, transpose_pair)
                    pair(i, j, h, 2, up(7))
                    tile(i, j, h, 0, context)

            tile_loop(step, end=SECOND)
            pe.wait_ge(k_lo, 3)
            for n in range(4):
                for h in range(4):
                    half = h % 2 * 64
                    mm = pe.matmul(B[n][half:half + 64, h // 2 * D:(h // 2 + 1) * D], UVT[:, 4 * n + h, :],
                                   WO[:, 4 * n + h, :], start=True, stop=True)
                mm.then_inc(k_b, 1)
            pe.wait_ge(k_lo, 7)
            tile_loop(step, first=SECOND)
            gate(L1)
            counts(L1)
            shared(L1)
            slots(L1)

        @block.vector
        def _(dve):
            ch = Count(dve, s_dve)
            mk = ch.mark

            def moments(src, t0, t1):
                for t in range(t0, t1):
                    mk(dve.bn_stats(STAT[:, t, :], src[:, t, :]))
                ch.wait()
                for t in range(t0, t1):
                    mk(dve.bn_aggr(MV[:, t, :], STAT[:, t, :]))

            def variances(t0, t1):
                ch.wait()
                dve.tensor_scalar(SD[:, t0:t1], MV[:, t0:t1, 1], LN_EPS, None, ALU.add).then_inc(s_var, 1)

            def stats(src, g):
                moments(src, g * GT, (g + 1) * GT)
                variances(g * GT, (g + 1) * GT)

            def inverse(n, t0, t1):
                s = slice(t0, t1)
                dve.wait_ge(s_sd, n + 1)
                mk(dve.reciprocal(RSTD[:, s], SD[:, s]))
                ch.wait()
                dve.scalar_tensor_tensor(out=SHIFT[:, s], in0=MV[:, s, 0], scalar=-1.0, in1=RSTD[:, s],
                                         op0=ALU.mult, op1=ALU.mult).then_inc(s_rstd, 1)

            def rstd(n, g):
                inverse(n * GROUPS + g, g * GT, (g + 1) * GT)

            def route(M, SC, weights):
                E, TOP, R = M.E, M.top, M.R
                for t in range(TILES):
                    mk(dve.max(TOPW[:, t, :], SC[:, t, :]))
                ch.wait()
                for t in range(TILES):
                    mk(dve.max_index(TOPI[:, t, :], TOPW[:, t, :], SC[:, t, :]))
                ch.wait()
                IDX = R[5][:, 0:8, :].rearrange("p a b -> p (a b)").rearrange("p (t k) -> p t k", k=8)
                mk(dve.tensor_copy(IDX, TOPI[:, :, :]))
                weights()
                ch.wait()
                eid = const("expert_id")[:, 0:E].unsqueeze(1).to_broadcast([P, TILES, E])
                OH = [R[i][:, :, 0:E] for i in range(TOP)]
                for k in range(TOP):
                    mk(dve.tensor_tensor(OH[k], IDX[:, :, k:k + 1].to_broadcast([P, TILES, E]), eid, ALU.is_equal))
                ch.wait()
                acc = R[4][:, :, 0:E]
                mk(dve.tensor_tensor(acc, OH[0], OH[1], ALU.add))
                for k in range(2, TOP):
                    ch.wait()
                    mk(dve.tensor_tensor(acc, acc, OH[k], ALU.add))
                ch.wait()
                dve.tensor_copy(SEL[:, :, 0:E], acc).then_inc(M.sel, 1)
                dve.wait_ge(M.counts, 1)
                CNT = R[5][:, :, :].rearrange("p a b -> p (a b)")[:, 0:E * TILES].rearrange("p (e t) -> p e t", t=TILES)
                INC = R[6][:, :, :].rearrange("p a b -> p (a b)")[:, 0:E * TILES].rearrange("p (e t) -> p e t", t=TILES)
                mk(dve.tensor_copy(CNT, B[5][:, 0:256].rearrange("p (t e) -> p e t", e=16)[:, 0:E, :]))
                ch.wait()
                mk(dve.tensor_tensor_scan(INC.rearrange("p e t -> p (e t)"), const("keep")[:, 0:E * TILES],
                                          CNT.rearrange("p e t -> p (e t)"), 0.0, ALU.mult, ALU.add))
                ch.wait()
                n, cum, base = SMALL[:, 0, 0:E], SMALL[:, 1, 0:E], SMALL[:, 2, 0:E]
                mk(dve.tensor_scalar(SMALLI[:, 0:E], INC[:, :, TILES - 1], float(P - 1), None, ALU.add))
                ch.wait()
                mk(dve.tensor_scalar(SMALLI[:, 0:E], SMALLI[:, 0:E], 7, None, ALU.arith_shift_right))
                ch.wait()
                mk(dve.tensor_copy(n, SMALLI[:, 0:E]))
                ch.wait()
                mk(dve.tensor_tensor_scan(cum, ONE64[:, 0:E], n, 0.0, ALU.mult, ALU.add))
                ch.wait()
                mk(dve.tensor_tensor(base, cum, n, ALU.subtract))
                ch.wait()
                mk(dve.tensor_scalar(base, base, float(P), None, ALU.mult))
                mk(dve.tensor_tensor(INC, INC, CNT, ALU.subtract))
                ch.wait()
                POS = R[7][:, :, 0:E]
                mk(dve.tensor_tensor(POS, INC.rearrange("p e t -> p t e"), base.unsqueeze(1).to_broadcast([P, TILES, E]),
                                     ALU.add))
                ch.wait()
                dve.tensor_tensor(POS, POS, B[4][:, 0:256].rearrange("p (t e) -> p t e", e=16)[:, :, 0:E], ALU.add)\
                    .then_inc(M.routed, 1)
                dve.wait_ge(M.routed, 1)
                for k in range(TOP):
                    mk(dve.tensor_tensor(OH[k], OH[k], POS, ALU.mult))
                ch.wait()
                PK = R[4][:, 0:4, :]
                for k in range(TOP):
                    mk(dve.tensor_reduce(PK[:, k, :], OH[k], AX.X, ALU.add))
                ch.wait()
                dve.tensor_copy(POSI[:, 0:TOP, :], PK[:, 0:TOP, :]).then_inc(M.pos, 1)
                slots = M.slots
                CMP = M.XCMP[0:1, 0:slots * E].rearrange("p (s e) -> p s e", e=E)
                mk(dve.tensor_tensor(CMP, cum[0:1, :].unsqueeze(1).to_broadcast([1, slots, E]),
                                     const("slot_id")[0:1, 0:slots].unsqueeze(2).to_broadcast([1, slots, E]), ALU.is_le))
                ch.wait()
                row = M.XCMP[0:1, slots * E:slots * E + slots]
                mk(dve.tensor_reduce(row, CMP, AX.X, ALU.add))
                ch.wait()
                dve.tensor_scalar(row, row, float(E - 1), float(M.cols), ALU.min, ALU.mult).then_inc(M.eid, 1)
                dve.wait_ge(M.eid, 1)
                ch.wait()
                dve.tensor_copy(EID[0:1, 0:slots], row).then_inc(M.eid, 1)

            def shared(M, scale, splits):
                def tokens(g):
                    dve.wait_ge(M.shxh, M.n * GROUPS + g + 1)
                    dve.tensor_tensor(M.XSLO[:, g % 2, :, :], M.XT[:, :, g * GTOK:(g + 1) * GTOK],
                                      M.XSHI[:, g % 2, :, :].bitcast(F32), ALU.subtract).then_inc(M.shx, 1)

                def add(g):
                    for t in range(g * GT, (g + 1) * GT):
                        dve.wait_ge(M.shy, M.n * TILES + t + 1)
                        dve.scalar_tensor_tensor(out=X[:, t, :], in0=B[4 + t % 2][:, 0:D], scalar=scale(t),
                                                 in1=X[:, t, :], op0=ALU.mult, op1=ALU.add).then_inc(M.shadd, 1)

                tokens(0)
                tokens(1)
                for g in range(GROUPS):
                    for c in range(M.shc):
                        n = g * M.shc + c
                        dve.wait_ge(M.shs, M.chunk0 + n + 1)
                        if n >= 2:
                            dve.wait_ge(M.shl, M.chunk0 + n - 1)
                            dve.wait_ge(M.shg, M.chunk0 + n - 1)
                        dve.tensor_tensor(M.SU[:, n % 2, :], M.SSIL[:, n % 2, :], B[2 * (n % 2) + 1][:, :], ALU.mult)\
                            .then_inc(M.shu, 1)
                        if c == 0 and g:
                            add(g - 1)
                        dve.wait_ge(M.shg, M.chunk0 + n + 1)
                        dve.wait_ge(M.shu, M.chunk0 + n + 1)
                        dve.tensor_tensor(M.SGLO[:, c, :], M.SU[:, n % 2, :], M.SGHI[:, c, :].bitcast(F32), ALU.subtract)\
                            .then_inc(M.shl, 1)
                    if g + 2 < GROUPS:
                        tokens(g + 2)
                    each = splits // GROUPS
                    for e in range(g * each, (g + 1) * each):
                        expert_remainder(dve, M, e)
                add(GROUPS - 1)

            def slots(M):
                def lo(i, j):
                    dve.wait_ge(M.a_xhi, i + (M.slot0 + 1))
                    dve.tensor_tensor(M.XLO[:, j % 2, :], B[j % 2][:, 0:D], M.XHI[:, j % 2, :].bitcast(F32), ALU.subtract)\
                        .then_inc(M.d_xlo, 1)

                def g_(i, j):
                    dve.wait_ge(M.a_sil, i + (M.slot0 + 1))
                    if at_least(i, 2):
                        dve.wait_ge(M.p_gt, i + (M.slot0 - 1))
                    dve.tensor_tensor(M.G[:, j % 2, 0:M.hid], M.SIL[:, j % 2, :], B[2 + j % 2][:, M.hid:M.w13], ALU.mult)\
                        .then_inc(M.d_g, 1)

                def glo(i, j):
                    dve.wait_ge(M.a_ghi, i + (M.slot0 + 1))
                    dve.tensor_tensor(M.GLO[:, j % 2, :], B[4 + j % 2][:, 0:M.hchunks * P], M.GHI[:, j % 2, :].bitcast(F32),
                                      ALU.subtract).then_inc(M.d_glo, 1)

                def step(i, j):
                    run_stages(i, j, M.slots, ((2, lo), (1, g_), (0, glo)))

                slot_loop(dve, M.slots, step, 2, 1)

            def combine_copy(M, t, k):
                n = M.copy0 + t * M.top + k
                dve.wait_ge(M.gath[n % 8], 16 * (n // 8 + 1))
                if n:
                    dve.wait_ge(M.comb, n)
                dve.scalar_tensor_tensor(out=X[:, t, :], in0=M.GB[:, n % 8, :], scalar=WK[:, k, t:t + 1],
                                         in1=X[:, t, :], op0=ALU.mult, op1=ALU.add).then_inc(M.comb, 1)

            mk(dve.memset(ONES[:, :], 1.0))
            mk(dve.memset(SEL[:, :, :], 0.0))
            dve.wait_ge(s_const, 16)
            mk(dve.tensor_copy(TRI[:, :], const("before")))
            for g in range(GROUPS):
                dve.wait_ge(s_x[g], 16)
                stats(X, g)
            for g in range(GROUPS):
                rstd(0, g)
            dve.wait_ge(s_act, 3)
            dve.wait_ge(s_zero, 2)
            mk(dve.tensor_tensor_scan(EMA[:, :], PAR[:, KEEP:KEEP + 1].to_broadcast([P, SEQ]), ONE64[:, :], 0.0,
                                      ALU.mult, ALU.add))
            ch.wait()
            mk(dve.tensor_scalar(EMAC[:, :], EMA[:, SEQ - 1::-1], 1.0 / SEQ, None, ALU.mult))
            ch.wait()
            mk(dve.tensor_reduce(PAR[:, CTOT:CTOT + 1], EMAC[:, :], AX.X, ALU.add))
            ch.wait()
            mk(dve.tensor_scalar(PAR[:, BC:BC + KC], BIN[:, :], PAR[:, CTOT:CTOT + 1], None, ALU.mult))
            for k in range(KC):
                dve.wait_ge(s_ctx[k], 16)
                ch.wait()
                if k:
                    dve.wait_ge(s_csum, k)
                mk(dve.tensor_tensor(CTXW[:, :].rearrange("p (b s) -> p b s", s=SEQ),
                                     CTX[:, k, :].rearrange("p (b s) -> p b s", s=SEQ),
                                     EMAC[:, :].unsqueeze(1).to_broadcast([P, BATCH, SEQ]), ALU.mult))
                ch.wait()
                dve.tensor_reduce(CSUM[:, k, :], CTXW[:, :].rearrange("p (b s) -> p b s", s=SEQ), AX.X, ALU.add)\
                    .then_inc(s_csum, 1)
            dve.wait_ge(s_wio, 16 * 6)
            mk(dve.tensor_scalar(GAMMA[:, :], GAMMA[:, :], PAR[:, TX:TX + 1], None, ALU.mult))
            dve.tensor_scalar(BETA[:, :], BETA[:, :], PAR[:, TX:TX + 1], None, ALU.mult).then_inc(s_beta, 1)
            dve.wait_ge(s_ema, 1)
            ch.wait()
            for j in range(KC):
                dve.tensor_scalar(M1T[:, j, :], B[0][:, j * BATCH:(j + 1) * BATCH], PAR[:, BC + j:BC + j + 1], None,
                                  ALU.add).then_inc(s_ema, 1)
            dve.wait_ge(s_ema, 2 + KC)
            dve.tensor_tensor(SUMM[:, :], B[1][0:BATCH, 0:D], BOUT[0:BATCH, :], ALU.add).then_inc(s_ema, 1)
            for g in range(GROUPS):
                for t in range(g * GT, (g + 1) * GT):
                    dve.wait_ge(s_norm, t + 1)
                    dve.wait_ge(s_spread, t + 1)
                    dve.tensor_tensor(XN[:, t, :], XN[:, t, :], B[2 + t % 6][:, 0:D], ALU.add).then_inc(s_spused, 1)
                dve.wait_ge(s_spused, (g + 1) * GT)
                stats(XN, g)
                if g:
                    rstd(1, g - 1)
            rstd(1, GROUPS - 1)
            for g in range(GROUPS):
                for t in range(g * GT, (g + 1) * GT):
                    dve.wait_ge(s_norm, TILES + t + 1)
                    mk(dve.tensor_tensor(XN[:, t, :], XN[:, t, :], GAMMA[:, :], ALU.mult))
                ch.wait()
                for t in range(g * GT, (g + 1) * GT):
                    dve.wait_ge(s_xb, t + 1)
                    mk(dve.tensor_tensor(X[:, t, :], X[:, t, :], XN[:, t, :], ALU.add))
                ch.wait()
                stats(X, g)
                if g:
                    rstd(2, g - 1)
            rstd(2, GROUPS - 1)
            R256 = L0.R
            dve.wait_ge(L0.lgt, TILES)
            LG = B[3][:, 0:256].rearrange("p (t e) -> p t e", e=E0)
            mx, inv = SMALL[:, 0, :], SMALL[:, 1, :]
            mk(dve.tensor_reduce(mx, LG, AX.X, ALU.max))
            ch.wait()
            dve.tensor_tensor(R256[0][:, :, :], LG, mx.unsqueeze(2).to_broadcast([P, TILES, E0]), ALU.subtract)\
                .then_inc(L0.shifted, 1)
            dve.wait_ge(L0.exped, 1)
            mk(dve.tensor_reduce(mx, R256[0][:, :, :], AX.X, ALU.add))
            ch.wait()
            mk(dve.reciprocal(inv, mx))
            ch.wait()
            mk(dve.tensor_tensor(R256[1][:, :, :], R256[0][:, :, :], inv.unsqueeze(2).to_broadcast([P, TILES, E0]), ALU.mult))
            ch.wait()
            gm = SMALL[:, 2:6, :].rearrange("p a b -> p (a b)").rearrange("p (t g) -> p t g", g=EGROUPS)
            mk(dve.tensor_reduce(gm, R256[1][:, :, :].rearrange("p t (g i) -> p (t g) i", i=EPG), AX.X, ALU.max))
            ch.wait()
            R4 = R256[2][:, :, :].rearrange("p t (j i) -> p t j i", i=EGROUPS)
            mk(dve.tensor_tensor(R4, gm.unsqueeze(2).to_broadcast([P, TILES, EGROUPS, EGROUPS]),
                                 gm.unsqueeze(3).to_broadcast([P, TILES, EGROUPS, EGROUPS]), ALU.is_ge))
            ch.wait()
            mk(dve.tensor_tensor(R256[3][:, :, :], R256[2][:, :, :],
                                 const("earlier_group").unsqueeze(1).to_broadcast([P, TILES, 16]), ALU.mult))
            ch.wait()
            ra = R256[4][:, 0:4, :].rearrange("p a b -> p (a b)").rearrange("p (t g) -> p t g", g=EGROUPS)
            rb = R256[4][:, 4:8, :].rearrange("p a b -> p (a b)").rearrange("p (t g) -> p t g", g=EGROUPS)
            R4b = R256[3][:, :, :].rearrange("p t (j i) -> p t j i", i=EGROUPS)
            mk(dve.tensor_reduce(ra, R4b, AX.X, ALU.add))
            mk(dve.tensor_reduce(rb, R4b.rearrange("p t j i -> p t i j"), AX.X, ALU.add))
            ch.wait()
            mk(dve.tensor_tensor(ra, ra, rb, ALU.subtract))
            ch.wait()
            mk(dve.tensor_tensor(ra, ra, const("later_groups").unsqueeze(1).to_broadcast([P, TILES, EGROUPS]), ALU.add))
            ch.wait()
            mk(dve.tensor_scalar(ra, ra, TOPG - 0.5, None, ALU.is_lt))
            ch.wait()
            mk(dve.tensor_scalar(rb, ra, 1.0, None, ALU.subtract))
            by_group = "p t (g i) -> p (t g) i"
            mk(dve.tensor_tensor(R256[2][:, :, :].rearrange(by_group, i=EPG), R256[1][:, :, :].rearrange(by_group, i=EPG),
                                 ra.rearrange("p t g -> p (t g)").unsqueeze(2).to_broadcast([P, TILES * EGROUPS, EPG]),
                                 ALU.mult))
            ch.wait()
            mk(dve.tensor_tensor(R256[0][:, :, :].rearrange(by_group, i=EPG), R256[2][:, :, :].rearrange(by_group, i=EPG),
                                 rb.rearrange("p t g -> p (t g)").unsqueeze(2).to_broadcast([P, TILES * EGROUPS, EPG]),
                                 ALU.add))
            ch.wait()

            def weights0():
                mk(dve.tensor_scalar(WK[:, :, :], TOPW[:, :, 0:4].rearrange("p t k -> p k t"), PAR[:, TF:TF + 1], None,
                                     ALU.mult))

            route(L0, R256[0][:, :, 0:E0], weights0)
            shared(L0, lambda t: PAR[:, TF:TF + 1], EARLY0)
            for e in range(EARLY0, E0):
                if e in POOLS0:
                    continue
                expert_remainder(dve, L0, e)
            dve.wait_ge(L0.scat, 16 * TILES * TOP0)
            mk(dve.memset(L0.G[:, :, :], 0.0))
            ch.wait()
            slots(L0)
            dve.wait_ge(L0.p_y, SLOTS0)
            dve.wait_ge(L0.wready, E0)
            dve.memset(KB[:, :, 2:4, :], 0.0).then_inc(k_zero, 1)

            def combine(k):
                return lambda t, r, u, o: combine_copy(L0, t, k)

            def combined(t, r, u, o):
                dve.wait_ge(L0.comb, (t + 1) * TOP0)
                moments(X, t, t + 1)
                if o:
                    variances(t - 1, t + 1)

            def inverse_pair(v, par):
                inverse(3 * GROUPS + v, 2 * v, 2 * v + 2)

            def moments_done(t, r, u, o):
                dve.wait_ge(t_x, t + 1)
                moments(X, t, t + 1)
                if o:
                    ch.wait()
                    dve.tensor_scalar(SD[:, t - 1:t + 1], MV[:, t - 1:t + 1, 1], LN_EPS, None, ALU.add).then_inc(e_var, 1)

            def inverse_done(v, par):
                s = slice(2 * v, 2 * v + 2)
                dve.wait_ge(e_sd, v + 1)
                mk(dve.reciprocal(RSTD[:, s], SD[:, s]))
                ch.wait()
                dve.scalar_tensor_tensor(out=SHIFT[:, s], in0=MV[:, s, 0], scalar=-1.0, in1=RSTD[:, s],
                                         op0=ALU.mult, op1=ALU.mult).then_inc(e_rstd, 1)

            def mask(i, r, u, o):
                if i == 0:
                    dve.wait_ge(k_mask, 1)
                if at_least(i, 2):
                    dve.wait_ge(t_pt, i * 2 - 2)
                for n in range(2):
                    dve.wait_ge(t_s, i * 2 + (n + 1))
                    dve.tensor_tensor(SM[:, r % 2, 8 * n:8 * n + 8, :], B[n][:, :].rearrange("p (h n) -> p h n", n=SEQ),
                                      MASK[:, bass.ds(i, 1), :].to_broadcast([P, 8, SEQ]), ALU.add).then_inc(t_masked, 1)
                dve.wait_ge(t_masked, i * 2 + 2)
                dve.tensor_reduce(SMX[:, r % 2, 0, :], SM[:, r % 2, :, :], AX.X, ALU.max).then_inc(t_max, 1)

            def row_sum(i, r, u, o):
                dve.wait_ge(t_exp, i + 1)
                dve.tensor_reduce(SMX[:, r % 2, 1, :], SM[:, r % 2, :, :], AX.X, ALU.add).then_inc(t_sum, 1)
                dve.wait_ge(t_sum, i + 1)
                dve.reciprocal(SMX[:, r % 2, 1, :], SMX[:, r % 2, 1, :]).then_inc(t_rec, 1)
                dve.wait_ge(t_rec, i + 1)
                dve.tensor_tensor(SM[:, r % 2, :, :], SM[:, r % 2, :, :],
                                  SMX[:, r % 2, 1, :].unsqueeze(2).to_broadcast([P, HEADS, SEQ]), ALU.mult)\
                    .then_inc(t_prob, 1)

            def qc_lo(v, par):
                dve.wait_ge(t_qchi, v + 1)
                dve.tensor_tensor(QCLO[:, :], B[5][0:QC, 0:2 * P], QCHI[:, :].bitcast(F32), ALU.subtract).then_inc(t_qclo, 1)

            def terms(p):
                def stage(v, par):
                    dve.wait_ge(t_rv, v * PAIRS + (p + 1))
                    n = v * PAIRS + p
                    if n >= RINGQ:
                        dve.wait_ge(t_q, 2 * (n - RINGQ + 1))
                    for w, dst, table in ((0, RC, "cos"), (1, RS, "sin")):
                        dve.tensor_tensor(dst[:, n % RINGQ, :].rearrange("p (b s) -> p b s", s=SEQ),
                                          rope_bank(p)[:, w * 2 * P:(w + 1) * 2 * P].rearrange("p (b s) -> p b s", s=SEQ),
                                          const(table).unsqueeze(1).to_broadcast([P, 4, SEQ]), ALU.mult).then_inc(t_rvm, 1)
                return stage

            def ct_lo(i, r, u, o):
                for b in range(2):
                    dve.wait_ge(t_cthi, i * 2 + (b + 1))
                    dve.tensor_tensor(CTLO[:, :, b * 64:(b + 1) * 64], B[2 + b][:, :].rearrange("p (h n) -> p h n", n=64),
                                      CTHI[:, :, b * 64:(b + 1) * 64].bitcast(F32), ALU.subtract).then_inc(t_ctlo, 1)

            def step(i, j, h):
                if j % 2:
                    pair(i, j, h, 3, qc_lo)
                    tile(i, j, h, 1, mask)
                    pair(i, j, h, 3, terms(0))
                    pair(i, j, h, 5, inverse_pair)
                    tile(i, j, h, 7, combine(0))
                    pair(i, j, h, 3, terms(1))
                    tile(i, j, h, 1, row_sum)
                    tile(i, j, h, 0, ct_lo)
                    pair(i, j, h, 3, terms(2))
                    tile(i, j, h, 7, combine(1))
                    pair(i, j, h, 3, terms(3))
                    tile(i, j, h, 7, combine(2))
                    tile(i, j, h, -2, moments_done)
                    tile(i, j, h, 7, combine(3))
                    tile(i, j, h, 7, combined)
                else:
                    tile(i, j, h, 1, mask)
                    pair(i, j, h, 2, terms(4))
                    pair(i, j, h, 2, terms(5))
                    tile(i, j, h, 7, combine(0))
                    pair(i, j, h, 2, terms(6))
                    tile(i, j, h, 1, row_sum)
                    pair(i, j, h, 2, terms(7))
                    tile(i, j, h, 7, combine(1))
                    tile(i, j, h, 0, ct_lo)
                    tile(i, j, h, 7, combine(2))
                    tile(i, j, h, -2, moments_done)
                    tile(i, j, h, 7, combine(3))
                    tile(i, j, h, 7, combined)
                    pair(i, j, h, -4, inverse_done)

            tile_loop(step, end=FIRST)
            RC5 = RC[:, 0:2, :].rearrange("p a n -> p (a n)")
            RS5 = RS[:, 0:2, :].rearrange("p a n -> p (a n)")
            for n in range(GROUPS):
                dve.wait_ge(k_rope, n + 1)
                if n:
                    dve.wait_ge(k_roped, 2 * n)
                for dst, src, table in ((RC5, B[n], "cos"), (RS5, B[4 + n], "sin")):
                    dve.tensor_tensor(dst.rearrange("p (b s) -> p b s", s=SEQ), src[:, :].rearrange("p (b s) -> p b s", s=SEQ),
                                      const(table).unsqueeze(1).to_broadcast([P, 8, SEQ]), ALU.mult).then_inc(k_ropem, 1)
                dve.wait_ge(k_ropem, 2 * n + 2)
                for half, which in ((64, 0), (0, 1)):
                    s = slice(half, half + 64)
                    dve.tensor_tensor(KB[s, n * GT:(n + 1) * GT, which, :], RC5[s, :].rearrange("p (t n) -> p t n", n=P),
                                      RS5[s, :].rearrange("p (t n) -> p t n", n=P), ALU.add).then_inc(k_roped, 1)
            dve.wait_ge(k_hi, 1)
            dve.tensor_tensor(ALO[:, :, 1:3, :], ARAW[:, :, 1:3, :], AHI[:, :, 1:3, :].bitcast(F32), ALU.subtract)\
                .then_inc(k_lo, 1)
            for n in range(2):
                dve.wait_ge(k_hi, n + 2)
                dve.tensor_tensor(ALO[:, 4 * n:4 * n + 4, 0, :], B[n][0:QC, :].rearrange("p (h n) -> p h n", n=P),
                                  AHI[:, 4 * n:4 * n + 4, 0, :].bitcast(F32), ALU.subtract).then_inc(k_lo, 1)
            tile_loop(step, first=FIRST, end=SECOND)
            for n in range(4):
                dve.wait_ge(k_hi, n + 4)
                dve.tensor_tensor(BLO[:, 2 * n:2 * n + 2, :], B[n][:, :].rearrange("p (h n) -> p h n", n=D),
                                  BHI[:, 2 * n:2 * n + 2, :].bitcast(F32), ALU.subtract).then_inc(k_lo, 1)
            tile_loop(step, first=SECOND)
            shared_remainder(dve, L1)
            for e in range(DVE_SPLITS1):
                expert_remainder(dve, L1, e)
            dve.wait_ge(L1.lgt, 2 * TILES)
            dve.tensor_copy(L1.R[0][:, :, 0:E1 + 1], B[3][:, 0:256].rearrange("p (t e) -> p t e", e=16)[:, :, 0:E1 + 1])\
                .then_inc(L1.shifted, 1)
            dve.wait_ge(L1.exped, 1)
            mk(dve.tensor_scalar(SGATE[:, :], SGATE[:, :], PAR[:, TF + 1:TF + 2], None, ALU.mult))
            ch.wait()

            def weights1():
                dve.tensor_tensor(SMALL[:, 5, :], TOPW[:, :, 1], TOPW[:, :, 0], ALU.subtract).then_inc(L1.shifted, 1)
                dve.wait_ge(L1.exped, 2)
                mk(dve.tensor_scalar(SMALL[:, 5, :], SMALL[:, 6, :], 1.0, None, ALU.add))
                ch.wait()
                mk(dve.reciprocal(SMALL[:, 5, :], SMALL[:, 5, :]))
                ch.wait()
                mk(dve.tensor_scalar(WK[:, 0, :], SMALL[:, 5, :], PAR[:, TF + 1:TF + 2], None, ALU.mult))
                ch.wait()
                mk(dve.tensor_tensor(WK[:, 1, :], WK[:, 0, :], SMALL[:, 6, :], ALU.mult))

            route(L1, L1.R[0][:, :, 0:E1], weights1)
            shared(L1, lambda t: SGATE[:, t:t + 1], 0)
            slots(L1)
            for t in range(TILES):
                for k in range(TOP1):
                    combine_copy(L1, t, k)


def host_layout(v):
    f = {k: np.asarray(x) for k, x in v.items()}
    c, select = constants()
    o = {"const": c, "select": select}
    o["x"] = f["x"].reshape(TOKENS, D)
    o["ctxT"] = f["ctx_2048"].reshape(TOKENS, D).T
    o["decay"] = f["L0_xattn_decay"].reshape(1, 1)
    o["g_xattn"] = f["g_xattn"].reshape(1, 2)
    o["g_ffn"] = f["g_ffn"].reshape(1, 2)
    o["W_inT"] = f["L0_xattn_W_in"].T
    o["W_outT"] = f["L0_xattn_W_out"].T
    o["b_in"] = f["L0_xattn_b_in"].reshape(KC, P).T
    o["b_out"] = f["L0_xattn_b_out"].reshape(1, D)
    o["gamma"] = f["L0_xattn_gamma"].reshape(1, D)
    o["beta"] = f["L0_xattn_beta"].reshape(1, D)
    o["Wg0T"] = f["L0_ffn_Wg"].T

    def chunks(w):
        r, n = w.shape
        k = -(-r // P)
        z = np.zeros((k * P, n), w.dtype)
        z[:r] = w
        return z.reshape(k, P, n).transpose(1, 0, 2).reshape(P, k * n)

    def wide(w, n):
        z = np.zeros((w.shape[0], n), w.dtype)
        z[:, :w.shape[1]] = w
        return z

    o["w0"] = np.stack([np.concatenate([
        chunks(np.concatenate([f["L0_ffn_W1"][e].T, f["L0_ffn_W3"][e].T], 1)), chunks(f["L0_ffn_W2"][e].T)], 1)
        for e in range(E0)])
    o["sh0"] = np.concatenate([chunks(wide(f["L0_ffn_Ws1"].T, SH0)), chunks(wide(f["L0_ffn_Ws3"].T, SH0)),
                               chunks(f["L0_ffn_Ws2"].T)], 1)
    o["seg"] = f["itok_BxS_0_1023"].reshape(TILES, P).T
    o["W_kvc2"] = chunks(np.concatenate([f["L1_xattn_W_kvc"]] * 2, 1))
    swap = np.arange(ROPE).reshape(2, ROPE // 2)[::-1].reshape(-1)
    kr = f["L1_xattn_W_kr"]
    o["W_kr2"] = np.concatenate([kr, kr, kr[:, swap], kr[:, swap]], 1)
    o["W_dq"] = chunks(f["L1_xattn_W_dq"])
    qr = f["L1_xattn_W_qr"].reshape(QC, PAIRS, 2, ROPE)[:, :, ::-1]
    o["W_qrv"] = np.stack([qr, qr[..., swap]], 2).reshape(QC, PAIRS * 2 * P)
    for n in ("uq", "uk", "uv"):
        w = f["L1_xattn_W_" + n]
        o[f"W_{n}T"] = w.reshape(w.shape[0], HEADS, HD).transpose(2, 1, 0).reshape(HD, -1)
    o["W_oh"] = f["L1_xattn_W_o"].reshape(HEADS, HD, D).transpose(1, 0, 2).reshape(HD, HEADS * D)
    o["Wg1T"] = np.concatenate([f["L1_ffn_gate_w"], f["L1_ffn_se_gate_w"]], 0).T
    o["w1"] = np.stack([np.concatenate([
        chunks(np.concatenate([f["L1_ffn_w_gate"][e].T, f["L1_ffn_w_up"][e].T], 1)), chunks(f["L1_ffn_w_down"][e].T)], 1)
        for e in range(E1)])
    o["sh1"] = np.concatenate([chunks(f["L1_ffn_sh_gate"].T), chunks(f["L1_ffn_sh_up"].T),
                               chunks(f["L1_ffn_sh_down"].T)], 1)
    return {k: np.ascontiguousarray(x) for k, x in o.items()}


def kernel(**inputs):
    import concourse.bacc as bacc
    from concourse.bass_utils import run_bass_kernel_spmd

    arrays = host_layout(inputs)
    nc = bacc.Bacc("TRN2", target_bir_lowering=False, num_devices=1)
    aps = {n: nc.dram_tensor(n, x.shape, mybir.dt.from_np(x.dtype), kind="ExternalInput").ap() for n, x in arrays.items()}
    aps["out"] = nc.dram_tensor("out", (TOKENS, D), F32, kind="ExternalOutput").ap()
    build_program(nc, aps)
    r = run_bass_kernel_spmd(nc, [arrays], core_ids=[0])
    return np.asarray(r.results[0]["out"]).reshape(BATCH, SEQ, D)
```
